# Optimizing a Trainium2 kernel written in Bass

```python
import numpy as np
import jax
import jax.numpy as jnp

def _softmax(x, axis=-1):
    return jax.nn.softmax(x, axis=axis)

def _gelu(x):
    return jax.nn.gelu(x, approximate=True)

def _silu(x):
    return jax.nn.silu(x)

def _sigmoid(x):
    return jax.nn.sigmoid(x)

def _layernorm(x, axis=-1, eps=1e-05):
    m = jnp.mean(x, axis=axis, keepdims=True)
    v = jnp.var(x, axis=axis, keepdims=True)
    return (x - m) / jnp.sqrt(v + eps)

def _scatter_add(tgt, idx, src, axis=0):
    return tgt.at[idx].add(src)

def _segment_sum(src, seg, n):
    return jax.ops.segment_sum(src, seg, n)
kernel_name = 'mk_adaln_d2_jaxref_r8_f66651'

def setup_inputs(seed: int=0):
    np.random.seed(seed)
    _w = jnp.asarray

    def _L0_attn_setup():
        import jax, jax.numpy as jnp
        import numpy as np
        N_HEADS = 16
        HEAD_DIM = 128
        ROPE_BASE = 10000.0

        def _apply_rope(x, start_pos):
            B, T, H, Dh = x.shape
            half = Dh // 2
            inv_freq = 1.0 / ROPE_BASE ** (jnp.arange(0, Dh, 2, dtype=jnp.float32) / Dh)
            pos = jnp.arange(T, dtype=jnp.float32) + start_pos
            ang = pos[:, None] * inv_freq[None, :]
            cos = jnp.cos(ang)[None, :, None, :].astype(x.dtype)
            sin = jnp.sin(ang)[None, :, None, :].astype(x.dtype)
            x1 = x[..., 0::2]
            x2 = x[..., 1::2]
            r1 = x1 * cos - x2 * sin
            r2 = x1 * sin + x2 * cos
            return jnp.stack([r1, r2], axis=-1).reshape(B, T, H, Dh)
        key = jax.random.key(seed)
        k0, k1, k2, k3, k4 = jax.random.split(key, 5)
        B, T, D = (2, 256, 256)
        d_lat = 128
        x = jax.random.normal(k0, (B, T, D), dtype=jnp.float32)
        wq = jax.random.normal(k1, (D, N_HEADS * HEAD_DIM), dtype=jnp.float32) / np.sqrt(D)
        w_down = jax.random.normal(k2, (D, d_lat), dtype=jnp.float32) / np.sqrt(D)
        w_up = jax.random.normal(k3, (d_lat, 2 * N_HEADS * HEAD_DIM), dtype=jnp.float32) / np.sqrt(d_lat)
        wo = jax.random.normal(k4, (N_HEADS * HEAD_DIM, D), dtype=jnp.float32) / np.sqrt(N_HEADS * HEAD_DIM)
        return {'x': x, 'wq': wq, 'w_down': w_down, 'w_up': w_up, 'wo': wo}
    _L0_attn_in = _L0_attn_setup()

    def _L0_ffn_setup():
        import jax, jax.numpy as jnp
        import numpy as np
        B, S, D = (1, 128, 256)
        E, K, F = (64, 8, 96)
        C = 32

        def _moe(x, router_w, w1, v1, w2):
            T = x.shape[0]
            logits = x @ router_w.T
            probs = jax.nn.softmax(logits, axis=-1)
            wts, idx = jax.lax.top_k(probs, K)
            wts = wts / jnp.sum(wts, axis=-1, keepdims=True)
            R = T * K
            e_flat = idx.reshape(-1)
            tok = jnp.arange(R) // K
            order = jnp.argsort(e_flat)
            e_s, tok_s = (e_flat[order], tok[order])
            w_s = wts.reshape(-1)[order]
            counts = jnp.bincount(e_flat, length=E)
            starts = jnp.cumsum(counts) - counts
            pos = jnp.arange(R) - starts[e_s]
            valid = pos < C
            pos_c = jnp.minimum(pos, C - 1)
            xg = jnp.zeros((E, C, D), x.dtype).at[e_s, pos_c].add(jnp.where(valid[:, None], x[tok_s], 0.0))
            h = jax.nn.silu(jnp.einsum('ecd,efd->ecf', xg, w1)) * jnp.einsum('ecd,efd->ecf', xg, v1)
            y = jnp.einsum('ecf,efd->ecd', h, w2)
            yr = y[e_s, pos_c] * jnp.where(valid, w_s, 0.0)[:, None]
            return jnp.zeros((T, D), x.dtype).at[tok_s].add(yr)
        key = jax.random.key(seed)
        k0, k1, k2, k3, k4 = jax.random.split(key, 5)
        return {'hidden_states': jax.random.normal(k0, (B, S, D), jnp.float32), 'router_w': jax.random.normal(k1, (E, D), jnp.float32) * 0.02, 'w1': jax.random.normal(k2, (E, F, D), jnp.float32) * 0.02, 'v1': jax.random.normal(k3, (E, F, D), jnp.float32) * 0.02, 'w2': jax.random.normal(k4, (E, F, D), jnp.float32) * 0.02}
    _L0_ffn_in = _L0_ffn_setup()
    _L0_c = _w((lambda *s: np.random.randn(*s).astype(np.float32) * 0.05)(1, 256))
    _L0_wmod = _w((lambda *s: np.random.randn(*s).astype(np.float32) * 0.05)(256, 6 * 256) * 256 ** (-0.5))

    def _L1_attn_setup():
        import jax, jax.numpy as jnp
        import numpy as np
        import math
        B, S, D = (4, 256, 256)
        QK = D // 8
        EXP = D * 2
        RESIDUAL_DEPTH = 144
        NUM_BLOCKS = 24
        key = jax.random.key(seed)
        k_x, k_e, k_p = jax.random.split(key, 3)
        x = jax.random.normal(k_x, (B, S, D), jnp.float32)
        expand_scale = 0.5 / math.sqrt(RESIDUAL_DEPTH) / 2.0
        project_scale = 1.0 / math.sqrt(RESIDUAL_DEPTH) / 2.0 / NUM_BLOCKS
        expand = expand_scale * jax.random.normal(k_e, (2 * QK + 2 * EXP, D), jnp.float32)
        project = project_scale * jax.random.normal(k_p, (D, EXP), jnp.float32)
        return {'x': x, 'ln_gamma': jnp.ones((D,), jnp.float32), 'ln_beta': jnp.zeros((D,), jnp.float32), 'expand': expand, 'project': project, 'pos_mult': jnp.float32(1.0)}
    _L1_attn_in = _L1_attn_setup()

    def _L1_ffn_setup():
        import jax, jax.numpy as jnp
        import numpy as np
        B, S, H = (4, 256, 256)
        E, K = (8, 2)
        I = 176
        SI = I * 2

        def swiglu_mlp(x, wg, wd):
            y = x @ wg.T
            gate, proj = jnp.split(y, 2, axis=-1)
            return jax.nn.silu(gate) * proj @ wd.T
        key = jax.random.key(seed)
        k0, k1, k2, k3, k4, k5 = jax.random.split(key, 6)
        x = jax.random.normal(k0, (B, S, H), dtype=jnp.float32)
        gate_w = jax.random.normal(k1, (E, H), dtype=jnp.float32) * 0.02
        expert_wg = jax.random.normal(k2, (E, 2 * I, H), dtype=jnp.float32) * 0.02
        expert_wd = jax.random.normal(k3, (E, H, I), dtype=jnp.float32) * 0.02
        shared_wg = jax.random.normal(k4, (2 * SI, H), dtype=jnp.float32) * 0.02
        shared_wd = jax.random.normal(k5, (H, SI), dtype=jnp.float32) * 0.02
        return {'x': x, 'gate_w': gate_w, 'expert_wg': expert_wg, 'expert_wd': expert_wd, 'shared_wg': shared_wg, 'shared_wd': shared_wd}
    _L1_ffn_in = _L1_ffn_setup()
    _L1_c = _w((lambda *s: np.random.randn(*s).astype(np.float32) * 0.05)(1, 256))
    _L1_wmod = _w((lambda *s: np.random.randn(*s).astype(np.float32) * 0.05)(256, 6 * 256) * 256 ** (-0.5))
    _d = {'L0_attn_x': _L0_attn_in['x'], 'L0_attn_wq': _L0_attn_in['wq'], 'L0_attn_w_down': _L0_attn_in['w_down'], 'L0_attn_w_up': _L0_attn_in['w_up'], 'L0_attn_wo': _L0_attn_in['wo'], 'L0_ffn_router_w': _L0_ffn_in['router_w'], 'L0_ffn_w1': _L0_ffn_in['w1'], 'L0_ffn_v1': _L0_ffn_in['v1'], 'L0_ffn_w2': _L0_ffn_in['w2'], 'L0_c': _L0_c, 'L0_wmod': _L0_wmod, 'L1_attn_ln_gamma': _L1_attn_in['ln_gamma'], 'L1_attn_ln_beta': _L1_attn_in['ln_beta'], 'L1_attn_expand': _L1_attn_in['expand'], 'L1_attn_project': _L1_attn_in['project'], 'L1_attn_pos_mult': _L1_attn_in['pos_mult'], 'L1_ffn_gate_w': _L1_ffn_in['gate_w'], 'L1_ffn_expert_wg': _L1_ffn_in['expert_wg'], 'L1_ffn_expert_wd': _L1_ffn_in['expert_wd'], 'L1_ffn_shared_wg': _L1_ffn_in['shared_wg'], 'L1_ffn_shared_wd': _L1_ffn_in['shared_wd'], 'L1_c': _L1_c, 'L1_wmod': _L1_wmod}
    _x0 = _d['L0_attn_x']
    _d['L0_attn_x'] = jax.random.normal(jax.random.fold_in(jax.random.key(seed), 1), (1, 1024, 256), dtype=_x0.dtype)
    del _x0
    return _d

def reference(L0_attn_x, L0_attn_wq, L0_attn_w_down, L0_attn_w_up, L0_attn_wo, L0_ffn_router_w, L0_ffn_w1, L0_ffn_v1, L0_ffn_w2, L0_c, L0_wmod, L1_attn_ln_gamma, L1_attn_ln_beta, L1_attn_expand, L1_attn_project, L1_attn_pos_mult, L1_ffn_gate_w, L1_ffn_expert_wg, L1_ffn_expert_wd, L1_ffn_shared_wg, L1_ffn_shared_wd, L1_c, L1_wmod):

    def _L0_attn_ref(x, wq, w_down, w_up, wo):
        import jax, jax.numpy as jnp
        import numpy as np
        N_HEADS = 16
        HEAD_DIM = 128
        ROPE_BASE = 10000.0

        def _apply_rope(x, start_pos):
            B, T, H, Dh = x.shape
            half = Dh // 2
            inv_freq = 1.0 / ROPE_BASE ** (jnp.arange(0, Dh, 2, dtype=jnp.float32) / Dh)
            pos = jnp.arange(T, dtype=jnp.float32) + start_pos
            ang = pos[:, None] * inv_freq[None, :]
            cos = jnp.cos(ang)[None, :, None, :].astype(x.dtype)
            sin = jnp.sin(ang)[None, :, None, :].astype(x.dtype)
            x1 = x[..., 0::2]
            x2 = x[..., 1::2]
            r1 = x1 * cos - x2 * sin
            r2 = x1 * sin + x2 * cos
            return jnp.stack([r1, r2], axis=-1).reshape(B, T, H, Dh)
        B, T, D = x.shape
        H, Dh = (N_HEADS, HEAD_DIM)
        scale = Dh ** (-0.5)
        q = (x @ wq).reshape(B, T, H, Dh)
        c_kv = x @ w_down
        kv_up = (c_kv @ w_up).reshape(B, T, H, 2 * Dh)
        k, v = (kv_up[..., :Dh], kv_up[..., Dh:])
        q = _apply_rope(q, 0)
        k = _apply_rope(k, 0)
        scores = jnp.einsum('bqhd,bkhd->bhqk', q, k) * scale
        causal = jnp.tril(jnp.ones((T, T), dtype=bool))
        scores = jnp.where(causal[None, None, :, :], scores, jnp.float32(-jnp.inf))
        attn = jax.nn.softmax(scores, axis=-1)
        out = jnp.einsum('bhqk,bkhd->bqhd', attn, v).reshape(B, T, H * Dh)
        return out @ wo

    def _L0_ffn_ref(hidden_states, router_w, w1, v1, w2):
        import jax, jax.numpy as jnp
        import numpy as np
        B, S, D = (1, 128, 256)
        E, K, F = (64, 8, 96)
        C = 32

        def _moe(x, router_w, w1, v1, w2):
            T = x.shape[0]
            logits = x @ router_w.T
            probs = jax.nn.softmax(logits, axis=-1)
            wts, idx = jax.lax.top_k(probs, K)
            wts = wts / jnp.sum(wts, axis=-1, keepdims=True)
            R = T * K
            e_flat = idx.reshape(-1)
            tok = jnp.arange(R) // K
            order = jnp.argsort(e_flat)
            e_s, tok_s = (e_flat[order], tok[order])
            w_s = wts.reshape(-1)[order]
            counts = jnp.bincount(e_flat, length=E)
            starts = jnp.cumsum(counts) - counts
            pos = jnp.arange(R) - starts[e_s]
            valid = pos < C
            pos_c = jnp.minimum(pos, C - 1)
            xg = jnp.zeros((E, C, D), x.dtype).at[e_s, pos_c].add(jnp.where(valid[:, None], x[tok_s], 0.0))
            h = jax.nn.silu(jnp.einsum('ecd,efd->ecf', xg, w1)) * jnp.einsum('ecd,efd->ecf', xg, v1)
            y = jnp.einsum('ecf,efd->ecd', h, w2)
            yr = y[e_s, pos_c] * jnp.where(valid, w_s, 0.0)[:, None]
            return jnp.zeros((T, D), x.dtype).at[tok_s].add(yr)
        b, s, d = hidden_states.shape
        x = hidden_states.transpose(1, 0, 2).reshape(s * b, d)
        out = _moe(x, router_w, w1, v1, w2)
        return out.reshape(s, b, d).transpose(1, 0, 2)

    def _L1_attn_ref(x, ln_gamma, ln_beta, expand, project, pos_mult):
        import jax, jax.numpy as jnp
        import numpy as np
        import math
        B, S, D = (4, 256, 256)
        QK = D // 8
        EXP = D * 2
        RESIDUAL_DEPTH = 144
        NUM_BLOCKS = 24
        Bx, Sx, Dx = x.shape
        qk_dim = Dx // 8
        expand_dim = Dx * 2
        v_dim = Dx
        idx = jnp.arange(Sx)
        rel = (idx[None, :] - idx[:, None]).astype(x.dtype)
        causal = idx[None, :] <= idx[:, None]
        attn_mask = jnp.where(causal, jax.nn.softplus(pos_mult) * rel, -jnp.inf)
        mu = x.mean(-1, keepdims=True)
        var = x.var(-1, keepdims=True)
        h = (x - mu) * jax.lax.rsqrt(var + 1e-05) * ln_gamma + ln_beta
        fused = jnp.einsum('bsd,ed->bse', h, expand)
        query = fused[..., :qk_dim]
        key_ = fused[..., qk_dim:2 * qk_dim]
        linear = fused[..., 2 * qk_dim:2 * qk_dim + expand_dim]
        pre_gelu = fused[..., 2 * qk_dim + expand_dim:]
        geglu = linear * jax.nn.gelu(pre_gelu, approximate=False)
        geglu_local = geglu[..., :expand_dim - v_dim]
        value = geglu[..., expand_dim - v_dim:]
        scale = 1.0 / math.sqrt(qk_dim)
        scores = jnp.einsum('bqd,bkd->bqk', query, key_) * scale + attn_mask
        attn = jnp.einsum('bqk,bkd->bqd', jax.nn.softmax(scores, axis=-1), value)
        out = jnp.einsum('bse,de->bsd', jnp.concatenate([geglu_local, attn], axis=-1), project)
        return x + out

    def _L1_ffn_ref(x, gate_w, expert_wg, expert_wd, shared_wg, shared_wd):
        import jax, jax.numpy as jnp
        import numpy as np
        B, S, H = (4, 256, 256)
        E, K = (8, 2)
        I = 176
        SI = I * 2

        def swiglu_mlp(x, wg, wd):
            y = x @ wg.T
            gate, proj = jnp.split(y, 2, axis=-1)
            return jax.nn.silu(gate) * proj @ wd.T
        b, s, h = x.shape
        flat = x.reshape(-1, h)
        T = flat.shape[0]
        scores = jax.nn.softmax(flat @ gate_w.T, axis=-1)
        topk_w, topk_idx = jax.lax.top_k(scores, K)
        topk_w = topk_w / (topk_w.sum(axis=-1, keepdims=True) + 1e-20)
        combine = jnp.zeros((T, E), dtype=flat.dtype).at[jnp.arange(T)[:, None], topk_idx].set(topk_w)
        y = jnp.zeros_like(flat)
        for e in range(E):
            y = y + combine[:, e:e + 1] * swiglu_mlp(flat, expert_wg[e], expert_wd[e])
        y = y.reshape(x.shape)
        y = y + swiglu_mlp(x, shared_wg, shared_wd)
        return y
    x = L0_attn_x
    mod = (_silu(L0_c) @ L0_wmod).reshape(L0_c.shape[0], 6, 1, -1)
    sa, ca, ga, sb, cb, gb = (mod[:, 0], mod[:, 1], mod[:, 2], mod[:, 3], mod[:, 4], mod[:, 5])
    ga = (2 * (ga >= 0) - 1) * jnp.maximum(jnp.abs(ga), 0.25)
    gb = (2 * (gb >= 0) - 1) * jnp.maximum(jnp.abs(gb), 0.25)
    h = _layernorm(x, axis=-1) * (1 + ca) + sa
    x = x + ga * _L0_attn_ref(h, L0_attn_wq, L0_attn_w_down, L0_attn_w_up, L0_attn_wo)
    h = _layernorm(x, axis=-1) * (1 + cb) + sb
    x = x + gb * _L0_ffn_ref(h, L0_ffn_router_w, L0_ffn_w1, L0_ffn_v1, L0_ffn_w2)
    mod = (_silu(L1_c) @ L1_wmod).reshape(L1_c.shape[0], 6, 1, -1)
    sa, ca, ga, sb, cb, gb = (mod[:, 0], mod[:, 1], mod[:, 2], mod[:, 3], mod[:, 4], mod[:, 5])
    ga = (2 * (ga >= 0) - 1) * jnp.maximum(jnp.abs(ga), 0.25)
    gb = (2 * (gb >= 0) - 1) * jnp.maximum(jnp.abs(gb), 0.25)
    h = _layernorm(x, axis=-1) * (1 + ca) + sa
    x = x + ga * _L1_attn_ref(h, L1_attn_ln_gamma, L1_attn_ln_beta, L1_attn_expand, L1_attn_project, L1_attn_pos_mult)
    h = _layernorm(x, axis=-1) * (1 + cb) + sb
    x = x + gb * _L1_ffn_ref(h, L1_ffn_gate_w, L1_ffn_expert_wg, L1_ffn_expert_wd, L1_ffn_shared_wg, L1_ffn_shared_wd)
    return x

_drawn_inputs = setup_inputs


def setup_inputs(seed=0):
    import zlib

    import numpy as np

    out = dict(_drawn_inputs(seed))
    spreads = {'L1_attn_ln_gamma': (1.0, 0.6), 'L1_attn_ln_beta': (0.0, 0.8)}
    factors = {'L0_ffn_router_w': 8.0,
     'L0_ffn_w1': 8.0,
     'L0_ffn_v1': 8.0,
     'L0_ffn_w2': 8.0,
     'L1_attn_expand': 8.0,
     'L1_attn_project': 8.0,
     'L1_ffn_gate_w': 8.0,
     'L1_ffn_expert_wg': 8.0,
     'L1_ffn_expert_wd': 8.0,
     'L1_ffn_shared_wg': 8.0,
     'L1_ffn_shared_wd': 8.0}
    for name, (base, spread) in spreads.items():
        noise = np.random.default_rng([zlib.crc32(name.encode()), seed]).standard_normal(out[name].shape)
        drawn = base * np.exp(spread * noise) if base else spread * noise
        out[name] = jnp.asarray(drawn.astype(out[name].dtype))
    for name, factor in factors.items():
        out[name] = (out[name] * factor).astype(out[name].dtype)
    return out
```

```python
from contextlib import ExitStack

import concourse.bass as bass
from concourse import mybir

F32 = mybir.dt.float32
F32R = mybir.dt.float32r
BF16 = mybir.dt.bfloat16
ALU = mybir.AluOpType
ACT = mybir.ActivationFunctionType
AX = mybir.AxisListType.X

P = 128
T = 1024
NT = T // P
D = 256
KD = D // P
H = 16
DH = 128
LAG = 6
EPS = 1e-5

E0, K0, F0, C0 = 64, 8, 96, 32
SLOTS = E0 * C0
NSB = SLOTS // P
EPB = P // C0

QK1, EXP1 = D // 8, 2 * D
E1, K1, I1 = 8, 2, 176
SI1 = 2 * I1


def wait_pos(eng, sem, count):
    if not isinstance(count, int) or count > 0:
        eng.wait_ge(sem, count)


def modulation(nc, sb, src, cst, modv, x_res, load_sem):
    with ExitStack() as ctx:
        c_col = ctx.enter_context(nc.sbuf_tensor("c_col", [P, 2, KD], F32))
        s_col = ctx.enter_context(nc.sbuf_tensor("s_col", [P, 2, KD], F32))
        s_wide = ctx.enter_context(nc.sbuf_tensor("s_wide", [P, 2, KD, P], F32))
        wmod = ctx.enter_context(nc.sbuf_tensor("wmod", [P, 2, KD, 6 * D], F32))
        gneg = ctx.enter_context(nc.sbuf_tensor("gneg", [P, 2, 2, D], F32))
        gsign = ctx.enter_context(nc.sbuf_tensor("gsign", [P, 2, 2, D], F32))
        ps = [ctx.enter_context(nc.psum_tensor(f"mod_ps{i}", [P, 512], F32)) for i in range(6)]
        c_loaded, wmod_loaded, const_loaded = (nc.alloc_semaphore(n) for n in ("c_loaded", "wmod_loaded", "const_loaded"))
        silu_done, wide_done, mod_ready, mod_copied, gate_step = (
            nc.alloc_semaphore(n) for n in ("silu_done", "wide_done", "mod_ready", "mod_copied", "gate_step"))
        with nc.Block() as block:

            @block.sync
            def _(sp):
                for l in range(2):
                    sp.dma_start(c_col[:, l, :], src[f"L{l}_c"].rearrange("o (k p) -> p (o k)", p=P),
                                 allow_slow_non_contiguous=True).then_inc(c_loaded, 16)
                for l in range(2):
                    sp.dma_start(wmod[:, l], src[f"L{l}_wmod"].rearrange("(k p) n -> p k n", p=P)).then_inc(wmod_loaded, 16)
                sp.dma_start(x_res[:], src["L0_attn_x"].rearrange("o (n p) d -> p (o n) d", p=P)).then_inc(load_sem, 16)
                for dst, name in cst:
                    sp.dma_start(dst, src[name]).then_inc(const_loaded, 16)
                sp.wait_ge(load_sem, 16)
                sp.wait_ge(const_loaded, 16 * len(cst))

            @block.scalar
            def _(act):
                act.wait_ge(c_loaded, 32)
                act.activation(s_col[:], c_col[:], ACT.Silu).then_inc(silu_done, 1)

            @block.tensor
            def _(pe):
                pe.wait_ge(wmod_loaded, 32)
                pe.wait_ge(wide_done, 4)
                for l in range(2):
                    for n in range(3):
                        for k in range(KD):
                            mm = pe.matmul(ps[3 * l + n][:], s_wide[:, l, k, :], wmod[:, l, k, n * 512:(n + 1) * 512],
                                           start=(k == 0), stop=(k == KD - 1))
                        mm.then_inc(mod_ready, 1)

            @block.vector
            def _(dve):
                dve.wait_ge(silu_done, 1)
                for l in range(2):
                    for k in range(KD):
                        dve.tensor_copy(s_wide[:, l, k, :], s_col[:, l, k:k + 1].to_broadcast([P, P])).then_inc(wide_done, 1)
                for l in range(2):
                    for n in range(3):
                        dve.wait_ge(mod_ready, 3 * l + n + 1)
                        dve.tensor_copy(modv[:, l, n * 512:(n + 1) * 512], ps[3 * l + n][:]).then_inc(mod_copied, 1)
                dve.wait_ge(mod_copied, 6)
                m = modv[:].rearrange("p l (a b d) -> p l a b d", a=2, b=3)
                dve.tensor_scalar(m[:, :, :, 1, :], m[:, :, :, 1, :], 1.0, None, ALU.add).then_inc(gate_step, 1)
                dve.tensor_scalar(gneg[:], m[:, :, :, 2, :], -1.0, 0.25, ALU.mult, ALU.max).then_inc(gate_step, 1)
                dve.tensor_scalar(gsign[:], m[:, :, :, 2, :], 0.0, 2.0, ALU.is_ge, ALU.mult).then_inc(gate_step, 1)
                dve.wait_ge(gate_step, 3)
                for l in range(2):
                    dve.tensor_tensor(gneg[:, l], gneg[:, l], m[:, l, :, 2, :], ALU.max).then_inc(gate_step, 1)
                dve.wait_ge(gate_step, 5)
                for l in range(2):
                    dve.scalar_tensor_tensor(m[:, l, :, 2, :], gsign[:, l], -1.0, gneg[:, l], ALU.add, ALU.mult).then_inc(gate_step, 1)
                dve.wait_ge(gate_step, 7)


def norm_tiles(nc, tag, x, scale, shift, h, hT, ident, eps_col):
    with ExitStack() as ctx:
        stats = ctx.enter_context(nc.sbuf_tensor(f"{tag}_stats", [P, NT, 6], F32))
        mv = ctx.enter_context(nc.sbuf_tensor(f"{tag}_mv", [P, NT, 2], F32))
        std = ctx.enter_context(nc.sbuf_tensor(f"{tag}_std", [P, NT], F32))
        rstd = ctx.enter_context(nc.sbuf_tensor(f"{tag}_rstd", [P, NT], F32))
        z = ctx.enter_context(nc.sbuf_tensor(f"{tag}_z", [P, NT, D], F32))
        ps = [ctx.enter_context(nc.psum_tensor(f"{tag}_ps{i}", [P, 512], F32)) for i in range(4)]
        stats_done, mv_done, std_done, rstd_done, z_done, h_done, turned, copied = (
            nc.alloc_semaphore(f"{tag}_{n}") for n in
            ("stats_done", "mv_done", "std_done", "rstd_done", "z_done", "h_done", "turned", "copied"))
        with nc.Block() as block:

            @block.vector
            def _(dve):
                for t in range(NT):
                    dve.bn_stats(stats[:, t, :], x[:, t, :]).then_inc(stats_done, 1)
                for t in range(NT):
                    dve.wait_ge(stats_done, t + 1)
                    dve.bn_aggr(mv[:, t, :], stats[:, t, :]).then_inc(mv_done, 1)
                dve.wait_ge(mv_done, NT)
                for t in range(NT):
                    dve.scalar_tensor_tensor(z[:, t, :], x[:, t, :], mv[:, t, 0:1], scale, ALU.subtract, ALU.mult).then_inc(z_done, 1)
                    if t == 1:
                        dve.wait_ge(std_done, 1)
                        dve.reciprocal(rstd[:], std[:]).then_inc(rstd_done, 1)
                dve.wait_ge(rstd_done, 1)
                for t in range(NT):
                    dve.wait_ge(z_done, t + 1)
                    dve.scalar_tensor_tensor(h[:, t, :], z[:, t, :], rstd[:, t:t + 1], shift, ALU.mult, ALU.add).then_inc(h_done, 1)

            @block.scalar
            def _(act):
                act.wait_ge(mv_done, NT)
                act.activation(std[:], mv[:, :, 1], ACT.Sqrt, bias=eps_col[:]).then_inc(std_done, 1)
                if hT is not None:
                    for t in range(NT):
                        act.wait_ge(turned, t + 1)
                        act.activation(hT[:, :, t * P:(t + 1) * P], ps[t % 4][:, 0:KD * P].rearrange("p (k c) -> p k c", k=KD),
                                       ACT.Copy).then_inc(copied, 1)

            @block.tensor
            def _(pe):
                if hT is not None:
                    for t in range(NT):
                        pe.wait_ge(h_done, t + 1)
                        if t >= 4:
                            pe.wait_ge(copied, t - 3)
                        for k in range(KD):
                            mm = pe.transpose(ps[t % 4][:, k * P:(k + 1) * P], h[:, t, k * P:(k + 1) * P], ident[:])
                        mm.then_inc(turned, 1)


def latent(nc, src, hT, ckvT, w_down):
    with ExitStack() as ctx:
        ps = [ctx.enter_context(nc.psum_tensor(f"lat_ps{i}", [P, 512], F32)) for i in range(2)]
        lat_ready, lat_copied = nc.alloc_semaphore("lat_ready"), nc.alloc_semaphore("lat_copied")
        with nc.Block() as block:

            @block.tensor
            def _(pe):
                for c in range(2):
                    for k in range(KD):
                        mm = pe.matmul(ps[c][:], w_down[:, k, :], hT[:, k, c * 512:(c + 1) * 512], start=(k == 0), stop=(k == KD - 1))
                    mm.then_inc(lat_ready, 1)

            @block.vector
            def _(dve):
                for c in range(2):
                    dve.wait_ge(lat_ready, c + 1)
                    dve.tensor_copy(ckvT[:, c * 512:(c + 1) * 512], ps[c][:]).then_inc(lat_copied, 1)


def attention0(nc, src, hT, ckvT, outT, rope, ident, ident_b, mask_b):
    with ExitStack() as ctx:
        def sb(name, shape, dt=F32):
            return ctx.enter_context(nc.sbuf_tensor(name, shape, dt))

        def ps(name):
            return ctx.enter_context(nc.psum_tensor(name, [P, 512], F32))

        w_q = [sb(f"w_q{b}", [P, KD, DH]) for b in range(2)]
        w_kv = [sb(f"w_kv{b}", [P, 2 * DH]) for b in range(2)]
        qkT = [sb(f"qkT{b}", [P, 2, T]) for b in range(2)]
        v_sb = [sb(f"v_sb{b}", [P, NT, DH]) for b in range(2)]
        rope_a = [sb(f"rope_a{b}", [P, 2, DH]) for b in range(2)]
        rope_b = [sb(f"rope_b{b}", [P, 2, DH]) for b in range(2)]
        rope_r = [sb(f"rope_r{b}", [P, 2, DH]) for b in range(2)]
        probs = [sb(f"probs{b}", [P, T]) for b in range(4)]
        probsT = [sb(f"probsT{b}", [P, NT, P]) for b in range(2)]
        nmax, rowsum, rinv = sb("nmax", [P, 4]), sb("rowsum", [P, 4]), sb("rinv", [P, 4])
        s_ps = [ctx.enter_context(nc.psum_tensor(f"s_ps{b}", [P, 2, 512], F32)) for b in range(2)]
        t_ps, o_ps, pj_ps = [ps("t_ps0"), ps("t_ps1")], ps("o_ps"), ps("pj_ps")

        def sem(n):
            return nc.alloc_semaphore("a0_" + n)

        w_ready = [sem("w_ready0"), sem("w_ready1")]
        proj_done, ab_done, v_done, rope_done, qk_turned, qk_copied = (
            sem(n) for n in ("proj_done", "ab_done", "v_done", "rope_done", "qk_turned", "qk_copied"))
        s_ready, max_done, exp_done, recip_done, norm_done = (
            sem(n) for n in ("s_ready", "max_done", "exp_done", "recip_done", "norm_done"))
        t_ready = [sem("t_ready0"), sem("t_ready1")]
        t_copied = [sem("t_copied0"), sem("t_copied1")]
        pv_done, o_copied, pool_steps = sem("pv_done"), sem("o_copied"), sem("pool_steps")

        wq_d = src["wq_split"].rearrange("(k p) n -> p k n", p=P)
        wkv_d = src["L0_attn_w_up"]

        def scores_view(slot, i):
            w = (i + 1) * P
            if w <= 512:
                return s_ps[slot][:, 0:1, 0:w], [(0, 0, w)]
            return s_ps[slot][:, 0:2, 0:w // 2], [(0, 0, w // 2), (1, w // 2, w)]

        def steps(eng, step):
            for i in range(NT):
                step(0, i, 0)
            with eng.Fori(0, (H - 2) // 2) as pair:
                for u in (1, 2):
                    for i in range(NT):
                        step(2 * pair + u, i, u % 2)
            for i in range(NT):
                step(H - 1, i, (H - 1) % 2)
            for i in range(2):
                step(H, i, H % 2)

        def at(h, i, u):
            if i < 0:
                h, i, u = h - 1, i + NT, 1 - u
            if i >= NT:
                h, i, u = h + 1, i - NT, 1 - u
            return h, i, u, h * NT + i

        def real(h):
            return not isinstance(h, int) or 0 <= h < H

        with nc.Block() as block:

            @block.sync
            def _(sp):
                def load(h, b):
                    wait_pos(sp, proj_done, NT * (h - 1))
                    sp.dma_start(w_q[b][:], wq_d[:, :, bass.ds(h * DH, DH)]).then_inc(w_ready[b], 16)
                    sp.dma_start(w_kv[b][:], wkv_d[:, bass.ds(h * 2 * DH, 2 * DH)]).then_inc(w_ready[b], 16)

                load(0, 0)
                load(1, 1)
                with sp.Fori(1, H // 2) as pair:
                    for b in range(2):
                        load(2 * pair + b, b)

            @block.tensor
            def _(pe):
                def project(h, i, u, n):
                    wait_pos(pe, qk_copied, n)
                    pe.wait_ge(w_ready[u], 16 * h + 32 - 16 * u)
                    for k in range(KD):
                        pe.matmul(pj_ps[:, 0:DH], hT[:, k, i * P:(i + 1) * P], w_q[u][:, k, :],
                                  start=(k == 0), stop=(k == KD - 1))
                    pe.matmul(pj_ps[:, DH:3 * DH], ckvT[:, i * P:(i + 1) * P], w_kv[u][:],
                              start=False, stop=True, skip_group_check=True).then_inc(proj_done, 1)

                def turn_qk(n, b):
                    pe.wait_ge(rope_done, n + 1)
                    pe.wait_ge(v_done, n + 1)
                    for j in range(2):
                        mm = pe.transpose(pj_ps[:, j * P:(j + 1) * P], rope_r[b][:, j, :], ident[:])
                    mm.then_inc(qk_turned, 1)

                def step(h, i, u):
                    g = h * NT + i
                    hn, tn, un, n = at(h, i + LAG, u)
                    hp, tp, up, _ = at(h, i - 2, u)
                    hl = at(h, i + LAG - 1, u)[0]
                    if real(hl):
                        turn_qk(n - 1, (i + 1) % 2)
                    if real(h):
                        pe.wait_ge(qk_copied, g + 1)
                        wait_pos(pe, exp_done, g - 1)
                        _, parts = scores_view(i % 2, i)
                        d0 = i * P
                        for bank, lo, hi in parts:
                            last = hi == (i + 1) * P
                            if last:
                                pe.matmul(s_ps[i % 2][:, bank, d0 - lo:d0 - lo + P], ident_b[:], mask_b[:],
                                          start=True, stop=False, skip_group_check=True)
                            mm = pe.matmul(s_ps[i % 2][:, bank, 0:hi - lo], qkT[u][:, 0, i * P:(i + 1) * P],
                                           qkT[u][:, 1, lo:hi], start=not last, stop=True, skip_group_check=True)
                        mm.then_inc(s_ready, 1)
                    if real(hp):
                        pe.wait_ge(norm_done, g - 1)
                        for j in range(tp // 4 + 1):
                            before = g - 2 if j == 0 else hp * 4 + tp - 4
                            wait_pos(pe, t_copied[j], before)
                            blocks = range(4 * j, min(4 * j + 4, tp + 1))
                            for kb in blocks:
                                mm = pe.transpose(t_ps[j][:, (kb % 4) * P:(kb % 4 + 1) * P],
                                                  probs[tp % 4][:, kb * P:(kb + 1) * P], ident[:])
                            mm.then_inc(t_ready[j], 1)
                    if real(hn):
                        project(hn, tn, un, n)
                    if real(hp):
                        pe.wait_ge(t_copied[0], g - 1)
                        if tp >= 4:
                            pe.wait_ge(t_copied[1], hp * 4 + tp - 3)
                        wait_pos(pe, o_copied, g - 2)
                        for kb in range(tp + 1):
                            mm = pe.matmul(o_ps[:, 0:P], v_sb[up][:, kb, :], probsT[tp % 2][:, kb, :],
                                           start=(kb == 0), stop=(kb == tp))
                        mm.then_inc(pv_done, 1)

                for n in range(LAG):
                    if n:
                        turn_qk(n - 1, (n - 1) % 2)
                    project(0, n, 0, n)
                steps(pe, step)

            @block.vector
            def _(dve):
                def rope_products(i, n, b):
                    dve.wait_ge(proj_done, n + 1)
                    wait_pos(dve, rope_done, n - 1)
                    x = pj_ps[:, 0:2 * DH].rearrange("p (a d) -> p a d", a=2)
                    half = DH // 2
                    dve.tensor_tensor(rope_a[b][:], x, rope[:, 0, i], ALU.mult)
                    dve.tensor_tensor(rope_b[b][:, :, 0:half], x[:, :, half:DH], rope[:, 1, i, :, 0:half], ALU.mult)
                    dve.tensor_tensor(rope_b[b][:, :, half:DH], x[:, :, 0:half], rope[:, 1, i, :, half:DH],
                                      ALU.mult).then_inc(ab_done, 1)

                def step(h, i, u):
                    g = h * NT + i
                    hn, tn, un, n = at(h, i + LAG, u)
                    hp, tp, up, _ = at(h, i - 2, u)
                    if real(h):
                        dve.wait_ge(s_ready, g + 1)
                        dve.tensor_reduce(nmax[:, i % 4:i % 4 + 1], scores_view(i % 2, i)[0], mybir.AxisListType.XY, ALU.max,
                                          negate=True).then_inc(max_done, 1)
                    if real(hp):
                        dve.wait_ge(t_ready[0], g - 1)
                        wait_pos(dve, pv_done, g - 3)
                        w = min(tp + 1, 4)
                        dve.tensor_copy(probsT[tp % 2][:, 0:w, :], t_ps[0][:, 0:w * P].rearrange("p (a c) -> p a c", a=w))\
                           .then_inc(t_copied[0], 1)
                    if real(hn):
                        rope_products(tn, n, i % 2)
                    if real(h):
                        dve.wait_ge(exp_done, g + 1)
                        dve.reciprocal(rinv[:, i % 4:i % 4 + 1], rowsum[:, i % 4:i % 4 + 1]).then_inc(recip_done, 1)
                    if real(hp):
                        dve.wait_ge(pv_done, g - 1)
                        dve.tensor_copy(outT[:, hp, tp * P:(tp + 1) * P], o_ps[:, 0:P]).then_inc(o_copied, 1)

                for n in range(LAG):
                    rope_products(n, n, n % 2)
                steps(dve, step)

            @block.scalar
            def _(act):
                def copy_qk(i, u, n):
                    act.wait_ge(qk_turned, n + 1)
                    act.activation(qkT[u][:, :, i * P:(i + 1) * P], pj_ps[:, 0:2 * P].rearrange("p (a c) -> p a c", a=2),
                                   ACT.Copy).then_inc(qk_copied, 1)

                def copy_v(i, u, n):
                    act.wait_ge(ab_done, n + 1)
                    act.activation(v_sb[u][:, i, :], pj_ps[:, 2 * DH:3 * DH], ACT.Copy).then_inc(v_done, 1)

                def step(h, i, u):
                    g = h * NT + i
                    hn, tn, un, n = at(h, i + LAG, u)
                    hl, tl, ul, nl = at(h, i + LAG - 1, u)
                    hp, tp, up, _ = at(h, i - 2, u)
                    if real(hl):
                        copy_qk(tl, ul, nl)
                    if real(h):
                        act.wait_ge(max_done, g + 1)
                        view, parts = scores_view(i % 2, i)
                        out = probs[i % 4][:, 0:(i + 1) * P].rearrange("p (a c) -> p a c", a=len(parts))
                        act.activation(out, view, ACT.Exp, bias=nmax[:, i % 4:i % 4 + 1],
                                       accum_out=rowsum[:, i % 4:i % 4 + 1]).then_inc(exp_done, 1)
                    if real(hp) and tp >= 4:
                        act.wait_ge(t_ready[1], hp * 4 + tp - 3)
                        wait_pos(act, pv_done, g - 3)
                        w = tp - 3
                        act.activation(probsT[tp % 2][:, 4:4 + w, :], t_ps[1][:, 0:w * P].rearrange("p (a c) -> p a c", a=w),
                                       ACT.Copy).then_inc(t_copied[1], 1)
                    if real(hn):
                        copy_v(tn, un, n)

                for n in range(LAG):
                    if n:
                        copy_qk(n - 1, 0, n - 1)
                    copy_v(n, 0, n)
                steps(act, step)

            @block.gpsimd
            def _(pool):
                def rope_sum(n, b):
                    pool.wait_ge(ab_done, n + 1)
                    wait_pos(pool, qk_turned, n - 1)
                    pool.tensor_tensor(rope_r[b][:], rope_a[b][:], rope_b[b][:], ALU.add).then_inc(rope_done, 1)

                def step(h, i, u):
                    g = h * NT + i
                    hn, _, _, n = at(h, i + LAG, u)
                    if real(hn):
                        rope_sum(n, i % 2)
                    if real(h):
                        pool.wait_ge(recip_done, g + 1)
                        pool.sem_inc(pool_steps, 1)
                        p = probs[i % 4][:, 0:(i + 1) * P]
                        pool.tensor_scalar(p, p, rinv[:, i % 4:i % 4 + 1], 1.0, ALU.mult, ALU.mult).then_inc(norm_done, 1)

                for n in range(LAG):
                    rope_sum(n, n % 2)
                steps(pool, step)


def output0(nc, src, outT, gate, x_res):
    with ExitStack() as ctx:
        wo = ctx.enter_context(nc.sbuf_tensor("wo", [P, H, D], F32))
        part = [ctx.enter_context(nc.sbuf_tensor(f"wo_part{i}", [P, D], F32)) for i in range(2)]
        ps = [ctx.enter_context(nc.psum_tensor(f"wo_ps{i}", [P, 512], F32)) for i in range(2)]
        wo_loaded, y_ready, gated, added = (nc.alloc_semaphore(n) for n in ("wo_loaded", "wo_ready", "wo_gated", "wo_added"))
        with nc.Block() as block:

            @block.sync
            def _(sp):
                sp.dma_start(wo[:], src["L0_attn_wo"].rearrange("(h p) d -> p h d", p=P)).then_inc(wo_loaded, 16)

            @block.tensor
            def _(pe):
                pe.wait_ge(wo_loaded, 16)
                for t in range(NT):
                    if t >= 2:
                        pe.wait_ge(gated, t - 1)
                    for h in range(H):
                        mm = pe.matmul(ps[t % 2][:, 0:D], outT[:, h, t * P:(t + 1) * P], wo[:, h, :], start=(h == 0), stop=(h == H - 1))
                    mm.then_inc(y_ready, 1)

            @block.vector
            def _(dve):
                for t in range(NT):
                    dve.wait_ge(y_ready, t + 1)
                    dve.tensor_tensor(part[t % 2][:], ps[t % 2][:, 0:D], gate, ALU.mult).then_inc(gated, 1)
                    dve.wait_ge(gated, t + 1)
                    dve.tensor_tensor(x_res[:, t, :], x_res[:, t, :], part[t % 2][:], ALU.add).then_inc(added, 1)


def route0(nc, src, h, hT, hw_hi, hw_lo, onehot, posT, ident):
    with ExitStack() as ctx:
        def sb(name, shape, dt=F32):
            return ctx.enter_context(nc.sbuf_tensor(name, shape, dt))

        def sem(n):
            return nc.alloc_semaphore("r0_" + n)

        rw = sb("rw", [P, KD, E0])
        ones_b, before_b = sb("ones_b", [P, P], BF16), sb("before_b", [P, P], BF16)
        slot_c = sb("slot_c", [P, C0])
        nmax, total, inv = sb("r_nmax", [P, NT]), sb("r_total", [P, NT]), sb("r_inv", [P, NT])
        shifted, ex, marked = sb("r_shifted", [P, NT, E0]), sb("r_ex", [P, NT, E0]), sb("r_marked", [P, NT, E0])
        top = sb("r_top", [P, NT, K0])
        chosen, chosen_b = sb("r_chosen", [P, NT, E0]), sb("r_chosen_b", [P, NT, E0], BF16)
        off, place = sb("r_off", [P, NT, E0]), sb("r_place", [P, NT, E0])
        wts = sb("r_wts", [P, NT, E0])
        ps = [ctx.enter_context(nc.psum_tensor(f"r_ps{i}", [P, 512], F32)) for i in range(4)]
        loaded, logits_ready, shifted_done, exp_done, step_done, chosen_done, pos_ready, place_done, turned, split_hi = (
            sem(n) for n in ("loaded", "logits_ready", "shifted_done", "exp_done", "step_done", "chosen_done", "pos_ready",
                             "place_done", "turned", "split_hi"))
        logits = ps[0][:].rearrange("p (n e) -> p n e", n=NT)
        pos = ps[1][:].rearrange("p (n e) -> p n e", n=NT)
        with nc.Block() as block:

            @block.sync
            def _(sp):
                sp.dma_start(rw[:], src["router_t"]).then_inc(loaded, 16)
                sp.dma_start(ones_b[:], src["ones_b"]).then_inc(loaded, 16)
                sp.dma_start(before_b[:], src["before_b"]).then_inc(loaded, 16)
                sp.dma_start(slot_c[:], src["slot_c"]).then_inc(loaded, 16)

            @block.tensor
            def _(pe):
                pe.wait_ge(loaded, 64)
                for n in range(NT):
                    for k in range(KD):
                        mm = pe.matmul(logits[:, n, :], hT[:, k, n * P:(n + 1) * P], rw[:, k, :], start=(k == 0), stop=(k == KD - 1))
                mm.then_inc(logits_ready, 1)
                pe.wait_ge(chosen_done, 1)
                for n in range(NT):
                    for m in range(n + 1):
                        mm = pe.matmul(pos[:, n, :], (before_b if m == n else ones_b)[:], chosen_b[:, m, :],
                                       start=(m == 0), stop=(m == n))
                mm.then_inc(pos_ready, 1)
                pe.wait_ge(place_done, 1)
                for n in range(NT):
                    mm = pe.transpose(ps[2 + n // 4][0:E0, (n % 4) * P:(n % 4 + 1) * P], place[:, n, :], ident[:])
                    if n % 4 == 3:
                        mm.then_inc(turned, 1)

            @block.scalar
            def _(act):
                act.wait_ge(shifted_done, 1)
                act.activation(ex[:], shifted[:], ACT.Exp).then_inc(exp_done, 1)
                act.activation(hw_hi[:, :, 0:D], h[:], ACT.Copy).then_inc(split_hi, 1)

            @block.gpsimd
            def _(pool):
                pool.memset(hw_hi[:, :, D + E0:].bitcast(F32), 0.0).then_inc(split_hi, 1)
                pool.memset(hw_lo[:, :, D + E0:].bitcast(F32), 0.0).then_inc(split_hi, 1)
                pool.memset(posT[:], 0.0).then_inc(split_hi, 1)

            @block.vector
            def _(dve):
                done = [0]

                def after(ins):
                    done[0] += 1
                    ins.then_inc(step_done, 1)
                    dve.wait_ge(step_done, done[0])

                dve.wait_ge(logits_ready, 1)
                after(dve.tensor_reduce(nmax[:], logits, AX, ALU.max, negate=True))
                dve.tensor_tensor(shifted[:], logits, nmax[:].unsqueeze(2).to_broadcast([P, NT, E0]), ALU.add).then_inc(shifted_done, 1)
                dve.wait_ge(exp_done, 1)
                for n in range(NT):
                    ins = dve.max(top[:, n, :], ex[:, n, :])
                after(ins)
                for n in range(NT):
                    ins = dve.match_replace(marked[:, n, :], top[:, n, :], ex[:, n, :], -1.0)
                after(ins)
                after(dve.tensor_scalar(chosen[:], marked[:], 0.0, None, ALU.is_lt))
                dve.tensor_copy(chosen_b[:], chosen[:]).then_inc(chosen_done, 1)
                after(dve.tensor_tensor(wts[:], ex[:], chosen[:], ALU.mult))
                after(dve.tensor_reduce(total[:], wts[:], AX, ALU.add))
                after(dve.reciprocal(inv[:], total[:]))
                after(dve.tensor_tensor(wts[:], wts[:], inv[:].unsqueeze(2).to_broadcast([P, NT, E0]), ALU.mult))
                after(dve.tensor_scalar(off[:], chosen[:], -100.0, 100.0, ALU.mult, ALU.add))
                dve.wait_ge(pos_ready, 1)
                after(dve.tensor_tensor(off[:], off[:], pos, ALU.add))
                after(dve.tensor_scalar(place[:], off[:], 200.0, None, ALU.min))
                dve.sem_inc(place_done, 1)
                for n in range(NT):
                    dve.tensor_tensor(onehot[:, n].rearrange("p (e c) -> p e c", c=C0), place[:, n, :].unsqueeze(2).to_broadcast([P, E0, C0]),
                                      slot_c[:].unsqueeze(1).to_broadcast([P, E0, C0]), ALU.is_equal)
                after(dve.tensor_copy(hw_hi[:, :, D:D + E0], wts[:]))
                dve.tensor_tensor(hw_lo[:, :, D:D + E0], wts[:], hw_hi[:, :, D:D + E0], ALU.subtract)
                dve.wait_ge(split_hi, 4)
                dve.tensor_tensor(hw_lo[:, :, 0:D], h[:], hw_hi[:, :, 0:D], ALU.subtract)
                for j in range(2):
                    dve.wait_ge(turned, j + 1)
                    ins = dve.tensor_copy(posT[0:E0, j * 512:(j + 1) * 512], ps[2 + j][0:E0, :])
                after(ins)


def gather0(nc, src, hw_hi, hw_lo, onehot, xgT, wg):
    with ExitStack() as ctx:
        own = ctx.enter_context(nc.sbuf_tensor("own_b", [P, SLOTS], BF16))
        ps = [ctx.enter_context(nc.psum_tensor(f"g_ps{i}", [P, 512], F32)) for i in range(4)]
        own_loaded, g_ready, g_copied = (nc.alloc_semaphore(n) for n in ("own_loaded", "g_ready", "g_copied"))
        groups = [(s, k) for s in range(SLOTS // 512) for k in range(KD + 1)]
        with nc.Block() as block:

            @block.sync
            def _(sp):
                sp.dma_start(own[:], src["own_b"]).then_inc(own_loaded, 16)

            @block.tensor
            def _(pe):
                for q, (s, k) in enumerate(groups):
                    if q >= 4:
                        pe.wait_ge(g_copied, q - 3)
                    for n in range(NT):
                        for part in (hw_hi, hw_lo):
                            mm = pe.matmul(ps[q % 4][:], part[:, n, k * P:(k + 1) * P], onehot[:, n, s * 512:(s + 1) * 512],
                                           start=(n == 0 and part is hw_hi), stop=(n == NT - 1 and part is hw_lo))
                    mm.then_inc(g_ready, 1)

            @block.vector
            def _(dve):
                dve.wait_ge(own_loaded, 16)
                for q, (s, k) in enumerate(groups):
                    dve.wait_ge(g_ready, q + 1)
                    cols = slice(s * 512, (s + 1) * 512)
                    if k < KD:
                        dve.tensor_copy(xgT[:, k, cols], ps[q % 4][:]).then_inc(g_copied, 1)
                    else:
                        dve.tensor_tensor(wg[:, cols], ps[q % 4][:], own[:, cols], ALU.mult).then_inc(g_copied, 1)


def experts0(nc, src, xgT, wg, posT, gate, x_res):
    with ExitStack() as ctx:
        def sb(name, shape, dt=F32):
            return ctx.enter_context(nc.sbuf_tensor(name, shape, dt))

        def sem(n):
            return nc.alloc_semaphore("e0_" + n)

        RING = 4
        w_up = [sb(f"e_up{i}", [P, EPB, 2, KD, F0]) for i in range(RING)]
        w_dn = [sb(f"e_dn{i}", [F0, EPB, D]) for i in range(RING)]
        sel = sb("e_sel", [P, NSB, P], BF16)
        ones = sb("e_ones", [P, F0])
        c_col = sb("e_c", [P, 1])
        sil, act_v, act_w = ([sb(f"e_{n}{i}", [F0, P]) for i in range(2)] for n in ("sil", "av", "aw"))
        y_hi = [sb(f"e_yhi{i}", [P, D], F32R) for i in range(2)]
        y_lo = [sb(f"e_ylo{i}", [P, D], F32R) for i in range(2)]
        back = [sb(f"e_back{i}", [P, T], F32R) for i in range(4)]
        part = [sb(f"e_part{i}", [P, D]) for i in range(2)]
        up_ps = ctx.enter_context(nc.psum_tensor("e_up_ps", [P, 512], F32))
        y_ps = ctx.enter_context(nc.psum_tensor("e_y_ps", [P, 512], F32))
        sel_ps = [ctx.enter_context(nc.psum_tensor(f"e_sel_ps{i}", [P, 512], F32)) for i in range(2)]
        sum_ps = ctx.enter_context(nc.psum_tensor("e_sum_ps", [P, NT // 2, 2, D], F32))
        w_ready = [sem(f"w_ready{i}") for i in range(RING)]
        const_ready, up_ready, sil_done, act_v_done, act_done, y_ready, hi_done, lo_done, sel_ready, back_done, comb_done, gated, added = (
            sem(n) for n in ("const_ready", "up_ready", "sil_done", "act_v_done", "act_done", "y_ready", "hi_done", "lo_done",
                             "sel_ready", "back_done", "comb_done", "gated", "added"))

        def steps(eng, step):
            for u in range(4):
                step(u, u)
            with eng.Fori(1, NSB // 4) as four:
                for u in range(4):
                    step(4 * four + u, u)
            for u in range(2):
                step(NSB + u, u)

        def real(b):
            return not isinstance(b, int) or 0 <= b < NSB

        with nc.Block() as block:

            @block.sync
            def _(sp):
                def load(b, i):
                    wait_pos(sp, y_ready, b - RING + 1)
                    sp.dma_start(w_up[i][:], src["w_up0"][:, bass.ds(b * EPB, EPB)]).then_inc(w_ready[i], 16)
                    sp.dma_start(w_dn[i][:], src["w_dn0"][:, bass.ds(b * EPB, EPB)]).then_inc(w_ready[i], 16)

                sp.dma_start(sel[:], src["sel_b"]).then_inc(const_ready, 16)
                sp.dma_start(ones[:], src["ones_f"]).then_inc(const_ready, 16)
                sp.dma_start(c_col[:], src["c_col"]).then_inc(const_ready, 16)
                for i in range(RING):
                    load(i, i)
                with sp.Fori(1, NSB // 4) as four:
                    for i in range(RING):
                        load(4 * four + i, i)

            @block.tensor
            def _(pe):
                def select(b, half):
                    wait_pos(pe, back_done, 2 * b + half - 1)
                    pe.matmul(sel_ps[half][:], sel[:, b, :], posT[:, half * 512:(half + 1) * 512],
                              start=True, stop=True).then_inc(sel_ready, 1)

                def step(b, u):
                    if real(b):
                        pe.wait_ge(w_ready[u], 8 * b - 8 * u + 32)
                        wait_pos(pe, act_done, b)
                        for e in range(EPB):
                            for a in range(2):
                                for k in range(KD):
                                    pe.matmul(up_ps[0:F0, a * P + e * C0:a * P + (e + 1) * C0], w_up[u][:, e, a, k, :],
                                              xgT[:, k, bass.ds(b * P + e * C0, C0)],
                                              start=(e == 0 and a == 0 and k == 0), stop=(k == KD - 1), skip_group_check=True)
                        pe.matmul(up_ps[0:F0, 2 * P:3 * P], ones[:], wg[:, bass.ds(b * P, P)], start=False, stop=True,
                                  skip_group_check=True).then_inc(up_ready, 1)
                        select(b, 0)
                        select(b, 1)
                    if real(b - 1):
                        pe.wait_ge(act_done, b)
                        wait_pos(pe, lo_done, b - 1)
                        for e in range(EPB):
                            mm = pe.matmul(y_ps[e * C0:(e + 1) * C0, 0:D], act_w[(u - 1) % 2][:, e * C0:(e + 1) * C0],
                                           w_dn[(u - 1) % 4][:, e, :], start=True, stop=True)
                        mm.then_inc(y_ready, 1)
                    if real(b - 2):
                        pe.wait_ge(lo_done, b - 1)
                        pe.wait_ge(back_done, 2 * b - 2)
                        for t in range(NT):
                            for y in (y_hi, y_lo):
                                first = isinstance(b, int) and b == 2 and t % 2 == 0 and y is y_hi
                                mm = pe.matmul(sum_ps[:, t // 2, t % 2, :], back[(u - 2) % 4][:, t * P:(t + 1) * P], y[(u - 2) % 2][:],
                                               start=first, stop=(isinstance(b, int) and b == NSB + 1 and y is y_lo),
                                               skip_group_check=True)
                        mm.then_inc(comb_done, 1)

                pe.wait_ge(const_ready, 48)
                steps(pe, step)

            @block.scalar
            def _(act):
                def step(b, u):
                    if real(b):
                        act.wait_ge(up_ready, b + 1)
                        wait_pos(act, act_v_done, b - 1)
                        act.activation(sil[u % 2][:], up_ps[0:F0, 0:P], ACT.Silu).then_inc(sil_done, 1)
                    if real(b - 1):
                        act.wait_ge(y_ready, b)
                        wait_pos(act, comb_done, b - 2)
                        act.activation(y_hi[(u - 1) % 2][:], y_ps[:, 0:D], ACT.Copy).then_inc(hi_done, 1)

                steps(act, step)

            @block.vector
            def _(dve):
                def step(b, u):
                    if real(b):
                        dve.wait_ge(sil_done, b + 1)
                        dve.tensor_tensor(act_v[u % 2][:], sil[u % 2][:], up_ps[0:F0, P:2 * P], ALU.mult).then_inc(act_v_done, 1)
                        dve.wait_ge(act_v_done, b + 1)
                        wait_pos(dve, y_ready, b - 1)
                        dve.tensor_tensor(act_w[u % 2][:], act_v[u % 2][:], up_ps[0:F0, 2 * P:3 * P], ALU.mult).then_inc(act_done, 1)
                        for half in range(2):
                            dve.wait_ge(sel_ready, 2 * b + half + 1)
                            wait_pos(dve, comb_done, b - 3)
                            dve.tensor_scalar(back[u][:, half * 512:(half + 1) * 512], sel_ps[half][:], c_col[:], None,
                                              ALU.is_equal).then_inc(back_done, 1)
                    if real(b - 1):
                        dve.wait_ge(hi_done, b)
                        dve.tensor_tensor(y_lo[(u - 1) % 2][:], y_ps[:, 0:D], y_hi[(u - 1) % 2][:], ALU.subtract).then_inc(lo_done, 1)

                dve.wait_ge(const_ready, 48)
                steps(dve, step)
                dve.wait_ge(comb_done, NSB)
                for t in range(NT):
                    dve.tensor_tensor(part[t % 2][:], sum_ps[:, t // 2, t % 2, :], gate, ALU.mult).then_inc(gated, 1)
                    dve.wait_ge(gated, t + 1)
                    dve.tensor_tensor(x_res[:, t, :], x_res[:, t, :], part[t % 2][:], ALU.add).then_inc(added, 1)


def project1(nc, src, hT, qT, kT, value, catT, bias, mask_b):
    LOC, VAL, PRE = 2 * QK1, 2 * QK1 + EXP1 - D, EXP1
    with ExitStack() as ctx:
        def sb(name, shape, dt=F32):
            return ctx.enter_context(nc.sbuf_tensor(name, shape, dt))

        def sem(n):
            return nc.alloc_semaphore("p1_" + n)

        w = sb("expand", [P, KD, 2 * QK1 + 2 * EXP1])
        gate_v = [sb(f"gate_v{i}", [P, D]) for i in range(2)]
        gate_l = [sb(f"gate_l{i}", [P, 512]) for i in range(2)]
        pm, pos_e, pos_l, pos_s = sb("pm", [P, 1]), sb("pos_e", [P, 2]), sb("pos_l", [P, 1]), sb("pos_s", [P, 2])
        ps = [ctx.enter_context(nc.psum_tensor(f"p1_ps{i}", [P, 512], F32)) for i in range(8)]
        w_loaded, pos_loaded, pos_abs, pos_ln, pos_step = (sem(n) for n in ("w_loaded", "pos_loaded", "pos_abs", "pos_ln", "pos_step"))
        qk_ready, qk_copied, v_ready, v_gate, v_done, l_ready, l_gate, l_done = (
            sem(n) for n in ("qk_ready", "qk_copied", "v_ready", "v_gate", "v_done", "l_ready", "l_gate", "l_done"))
        with nc.Block() as block:

            @block.sync
            def _(sp):
                sp.dma_start(w[:], src["expand_t"]).then_inc(w_loaded, 16)
                sp.dma_start(pm[:], src["pos_mult"].to_broadcast([P, 1])).then_inc(pos_loaded, 16)
                sp.dma_start(bias[:], src["rel"]).then_inc(pos_loaded, 16)

            @block.tensor
            def _(pe):
                pe.wait_ge(w_loaded, 16)

                def product(out, lhs, rhs):
                    for k in range(KD):
                        mm = pe.matmul(out, lhs(k), rhs(k), start=(k == 0), stop=(k == KD - 1))
                    return mm

                for j in range(2):
                    for c in range(2):
                        product(ps[2 * j + c][0:QK1, :], lambda k: w[:, k, j * QK1:(j + 1) * QK1],
                                lambda k: hT[:, k, c * 512:(c + 1) * 512]).then_inc(qk_ready, 1)
                for t in range(NT):
                    if t >= 2:
                        pe.wait_ge(v_done, t - 1)
                    for g in range(2):
                        mm = product(ps[4 + t % 2][:, g * D:(g + 1) * D], lambda k: hT[:, k, t * P:(t + 1) * P],
                                     lambda k: w[:, k, VAL + g * PRE:VAL + g * PRE + D])
                    mm.then_inc(v_ready, 1)
                for q in range(4):
                    c, half = q // 2, q % 2
                    pe.wait_ge(qk_copied, 4)
                    if q >= 2:
                        pe.wait_ge(l_done, q - 1)
                    for g in range(2):
                        mm = product(ps[2 * (q % 2) + g][:], lambda k: w[:, k, LOC + g * PRE + c * P:LOC + g * PRE + (c + 1) * P],
                                     lambda k: hT[:, k, half * 512:(half + 1) * 512])
                    mm.then_inc(l_ready, 1)

            @block.scalar
            def _(act):
                act.wait_ge(pos_abs, 1)
                act.activation(pos_e[:, 1:2], pos_e[:, 0:1], ACT.Exp).then_inc(pos_ln, 1)
                act.wait_ge(pos_ln, 1)
                act.activation(pos_l[:], pos_e[:, 1:2], ACT.Ln, bias=1.0).then_inc(pos_ln, 1)
                for t in range(NT):
                    act.wait_ge(v_ready, t + 1)
                    if t >= 2:
                        act.wait_ge(v_done, t - 1)
                    act.activation(gate_v[t % 2][:], ps[4 + t % 2][:, D:2 * D], ACT.Gelu).then_inc(v_gate, 1)
                for q in range(4):
                    act.wait_ge(l_ready, q + 1)
                    if q >= 2:
                        act.wait_ge(l_done, q - 1)
                    act.activation(gate_l[q % 2][:], ps[2 * (q % 2) + 1][:], ACT.Gelu).then_inc(l_gate, 1)

            @block.vector
            def _(dve):
                dve.wait_ge(pos_loaded, 32)
                dve.scalar_tensor_tensor(pos_e[:, 0:1], pm[:], -1.0, pm[:], ALU.mult, ALU.min).then_inc(pos_abs, 1)
                dve.tensor_scalar(pos_s[:, 0:1], pm[:], 0.0, None, ALU.max).then_inc(pos_step, 1)
                dve.wait_ge(pos_step, 1)
                dve.wait_ge(pos_ln, 2)
                dve.tensor_tensor(pos_s[:, 1:2], pos_s[:, 0:1], pos_l[:], ALU.add).then_inc(pos_step, 1)
                for j in range(2):
                    for c in range(2):
                        dve.wait_ge(qk_ready, 2 * j + c + 1)
                        dve.tensor_scalar((kT if j else qT)[:, c * 512:(c + 1) * 512], ps[2 * j + c][0:QK1, :],
                                          1.0 if j else QK1 ** -0.5, None, ALU.mult).then_inc(qk_copied, 1)
                dve.wait_ge(pos_step, 2)
                dve.tensor_scalar(bias[:], bias[:], pos_s[:, 1:2], None, ALU.mult).then_inc(pos_step, 1)
                dve.wait_ge(pos_step, 3)
                dve.tensor_tensor(bias[:, T - P:T], bias[:, T - P:T], mask_b[:], ALU.add).then_inc(pos_step, 1)
                for t in range(NT):
                    dve.wait_ge(v_gate, t + 1)
                    dve.tensor_tensor(value[:, t, :], gate_v[t % 2][:], ps[4 + t % 2][:, 0:D], ALU.mult).then_inc(v_done, 1)
                for q in range(4):
                    c, half = q // 2, q % 2
                    dve.wait_ge(l_gate, q + 1)
                    dve.tensor_tensor(catT[:, c, half * 512:(half + 1) * 512], gate_l[q % 2][:], ps[2 * (q % 2)][:],
                                      ALU.mult).then_inc(l_done, 1)


def attend1(nc, src, qT, kT, value, catT, bias, hm, gate, x_res, ident):
    with ExitStack() as ctx:
        def sb(name, shape, dt=F32):
            return ctx.enter_context(nc.sbuf_tensor(name, shape, dt))

        def sem(n):
            return nc.alloc_semaphore("a1_" + n)

        proj = sb("proj1", [P, 4, D])
        s_sb = [sb(f"s1_{i}", [P, T]) for i in range(2)]
        probs = [sb(f"probs1_{i}", [P, T]) for i in range(3)]
        probsT = [sb(f"probs1T{i}", [P, NT, P]) for i in range(2)]
        nmax, rowsum, rinv = sb("nmax1", [P, NT]), sb("rowsum1", [P, NT]), sb("rinv1", [P, NT])
        part = [sb(f"part1_{i}", [P, 2, D]) for i in range(2)]
        s_ps = [ctx.enter_context(nc.psum_tensor(f"s1_ps{b}", [P, 2, 512], F32)) for b in range(2)]
        t_ps = [ctx.enter_context(nc.psum_tensor(f"t1_ps{b}", [P, 512], F32)) for b in range(2)]
        o_ps = ctx.enter_context(nc.psum_tensor("o1_ps", [P, 512], F32))
        y_ps = ctx.enter_context(nc.psum_tensor("y1_ps", [P, 512], F32))
        w_loaded, s_ready, biased, max_done, exp_done, recip_done, norm_done, pv_done, o_copied, y_ready, y_step, added = (
            sem(n) for n in ("w_loaded", "s_ready", "biased", "max_done", "exp_done", "recip_done", "norm_done", "pv_done",
                             "o_copied", "y_ready", "y_step", "added"))
        t_ready = [sem("t_ready0"), sem("t_ready1")]
        t_copied = [sem("t_copied0"), sem("t_copied1")]
        parts = [[(0, 0, (i + 1) * P)] if i < 4 else [(0, 0, (i + 1) * P // 2), (1, (i + 1) * P // 2, (i + 1) * P)] for i in range(NT)]

        def view(slot, i):
            return s_ps[slot][:, 0:len(parts[i]), 0:parts[i][0][2]]

        def halves(ap, i):
            return ap.rearrange("p (a c) -> p a c", a=len(parts[i]))

        with nc.Block() as block:

            @block.sync
            def _(sp):
                sp.dma_start(proj[:], src["project_t"]).then_inc(w_loaded, 16)

            @block.tensor
            def _(pe):
                for i in range(NT + 3):
                    if i < NT:
                        if i >= 2:
                            pe.wait_ge(biased, i - 1)
                        for bank, lo, hi in parts[i]:
                            mm = pe.matmul(s_ps[i % 2][:, bank, 0:hi - lo], qT[:, i * P:(i + 1) * P], kT[:, lo:hi], start=True, stop=True)
                        mm.then_inc(s_ready, 1)
                    p = i - 2
                    if 0 <= p < NT:
                        pe.wait_ge(norm_done, p + 1)
                        for j in range(p // 4 + 1):
                            wait_pos(pe, t_copied[j], p if j == 0 else p - 4)
                            for kb in range(4 * j, min(4 * j + 4, p + 1)):
                                mm = pe.transpose(t_ps[j][:, (kb % 4) * P:(kb % 4 + 1) * P], probs[p % 3][:, kb * P:(kb + 1) * P], ident[:])
                            mm.then_inc(t_ready[j], 1)
                    y = i - 3
                    if 0 <= y < NT:
                        pe.wait_ge(w_loaded, 16)
                        pe.wait_ge(o_copied, y + 1)
                        wait_pos(pe, y_step, 2 * y - 1)
                        for c in range(4):
                            mm = pe.matmul(y_ps[:, 0:D], catT[:, c, y * P:(y + 1) * P], proj[:, c, :], start=(c == 0), stop=(c == 3))
                        mm.then_inc(y_ready, 1)
                    if 0 <= p < NT:
                        pe.wait_ge(t_copied[0], p + 1)
                        if p >= 4:
                            pe.wait_ge(t_copied[1], p - 3)
                        wait_pos(pe, o_copied, p)
                        for v in range(2):
                            for kb in range(p + 1):
                                mm = pe.matmul(o_ps[:, v * P:(v + 1) * P], value[:, kb, v * P:(v + 1) * P], probsT[p % 2][:, kb, :],
                                               start=(kb == 0), stop=(kb == p))
                        mm.then_inc(pv_done, 1)

            @block.vector
            def _(dve):
                for i in range(NT + 3):
                    if i < NT:
                        dve.wait_ge(s_ready, i + 1)
                        wait_pos(dve, exp_done, i - 1)
                        off = (NT - 1 - i) * P
                        dve.tensor_tensor(halves(s_sb[i % 2][:, 0:(i + 1) * P], i), view(i % 2, i),
                                          halves(bias[:, off:off + (i + 1) * P], i), ALU.add).then_inc(biased, 1)
                        dve.wait_ge(biased, i + 1)
                        dve.tensor_reduce(nmax[:, i:i + 1], s_sb[i % 2][:, 0:(i + 1) * P], AX, ALU.max, negate=True).then_inc(max_done, 1)
                    p = i - 2
                    if 0 <= p < NT:
                        dve.wait_ge(t_ready[0], p + 1)
                        wait_pos(dve, pv_done, p - 1)
                        n = min(p + 1, 4)
                        dve.tensor_copy(probsT[p % 2][:, 0:n, :], t_ps[0][:, 0:n * P].rearrange("p (a c) -> p a c", a=n))\
                           .then_inc(t_copied[0], 1)
                    if i < NT:
                        dve.wait_ge(exp_done, i + 1)
                        dve.reciprocal(rinv[:, i:i + 1], rowsum[:, i:i + 1]).then_inc(recip_done, 1)
                    y = i - 3
                    if 0 <= y < NT:
                        dve.wait_ge(y_ready, y + 1)
                        dve.tensor_tensor(part[y % 2][:, 0, :], y_ps[:, 0:D], hm[:, y, :], ALU.add).then_inc(y_step, 1)
                        dve.wait_ge(y_step, 2 * y + 1)
                        dve.tensor_tensor(part[y % 2][:, 1, :], part[y % 2][:, 0, :], gate, ALU.mult).then_inc(y_step, 1)
                        dve.wait_ge(y_step, 2 * y + 2)
                        dve.tensor_tensor(x_res[:, y, :], x_res[:, y, :], part[y % 2][:, 1, :], ALU.add).then_inc(added, 1)
                    if 0 <= p < NT:
                        dve.wait_ge(pv_done, p + 1)
                        dve.tensor_copy(catT[:, 2:4, p * P:(p + 1) * P], o_ps[:, 0:2 * P].rearrange("p (a c) -> p a c", a=2))\
                           .then_inc(o_copied, 1)

            @block.scalar
            def _(act):
                for i in range(NT + 2):
                    if i < NT:
                        act.wait_ge(max_done, i + 1)
                        act.activation(probs[i % 3][:, 0:(i + 1) * P], s_sb[i % 2][:, 0:(i + 1) * P], ACT.Exp, bias=nmax[:, i:i + 1],
                                       accum_out=rowsum[:, i:i + 1]).then_inc(exp_done, 1)
                    p = i - 2
                    if p >= 4:
                        act.wait_ge(t_ready[1], p - 3)
                        wait_pos(act, pv_done, p - 1)
                        n = p - 3
                        act.activation(probsT[p % 2][:, 4:4 + n, :], t_ps[1][:, 0:n * P].rearrange("p (a c) -> p a c", a=n),
                                       ACT.Copy).then_inc(t_copied[1], 1)

            @block.gpsimd
            def _(pool):
                for i in range(NT):
                    pool.wait_ge(recip_done, i + 1)
                    p = probs[i % 3][:, 0:(i + 1) * P]
                    pool.tensor_scalar(p, p, rinv[:, i:i + 1], 1.0, ALU.mult, ALU.mult).then_inc(norm_done, 1)


NE1 = E1 + 2
HI1 = I1 // 2


def route1(nc, src, hT, comb, h_hi, h_lo):
    with ExitStack() as ctx:
        def sb(name, shape, dt=F32):
            return ctx.enter_context(nc.sbuf_tensor(name, shape, dt))

        rw = sb("rw1", [P, KD, E1])
        one_t = sb("one_t", [P, E1])
        nmax, total, inv, best2, above_n, wsum = (sb(f"r1_{n}", [P, NT]) for n in ("nmax", "total", "inv", "second", "above_n", "wsum"))
        shifted, prob, above, equal, rank, ok, wts = (sb(f"r1_{n}", [P, NT, E1]) for n in
                                                      ("shifted", "prob", "above", "equal", "rank", "ok", "wts"))
        top = sb("r1_top", [P, NT, 8])
        ps = ctx.enter_context(nc.psum_tensor("r1_ps", [P, 512], F32))
        loaded, logits_ready, shifted_done, exp_done, step_done, split_done = (
            nc.alloc_semaphore("r1_" + n) for n in ("loaded", "logits_ready", "shifted_done", "exp_done", "step_done", "split_done"))
        logits = ps[:, 0:NT * E1].rearrange("p (n e) -> p n e", n=NT)

        def wide(col):
            return col.unsqueeze(2).to_broadcast([P, NT, E1])

        with nc.Block() as block:

            @block.sync
            def _(sp):
                sp.dma_start(rw[:], src["gate_t"]).then_inc(loaded, 16)

            @block.tensor
            def _(pe):
                pe.wait_ge(loaded, 16)
                for n in range(NT):
                    for k in range(KD):
                        mm = pe.matmul(logits[:, n, :], hT[:, k, n * P:(n + 1) * P], rw[:, k, :], start=(k == 0), stop=(k == KD - 1))
                mm.then_inc(logits_ready, 1)

            @block.scalar
            def _(act):
                act.activation(h_hi[:], hT[:], ACT.Copy).then_inc(split_done, 1)
                act.wait_ge(shifted_done, 1)
                act.activation(prob[:], shifted[:], ACT.Exp).then_inc(exp_done, 1)

            @block.vector
            def _(dve):
                done = [0]

                def after(ins):
                    done[0] += 1
                    ins.then_inc(step_done, 1)
                    dve.wait_ge(step_done, done[0])

                after(dve.memset(one_t[:], 1.0))
                after(dve.memset(comb[:], 1.0))
                dve.wait_ge(logits_ready, 1)
                after(dve.tensor_reduce(nmax[:], logits, AX, ALU.max, negate=True))
                dve.tensor_tensor(shifted[:], logits, wide(nmax[:]), ALU.add).then_inc(shifted_done, 1)
                dve.wait_ge(exp_done, 1)
                after(dve.tensor_reduce(total[:], prob[:], AX, ALU.add))
                after(dve.reciprocal(inv[:], total[:]))
                after(dve.tensor_tensor(prob[:], prob[:], wide(inv[:]), ALU.mult))
                for n in range(NT):
                    ins = dve.max(top[:, n, :], prob[:, n, :])
                after(ins)
                after(dve.tensor_copy(best2[:], top[:, :, K1 - 1]))
                dve.tensor_tensor(above[:], prob[:], wide(best2[:]), ALU.is_gt)
                after(dve.tensor_tensor(equal[:], prob[:], wide(best2[:]), ALU.is_equal))
                dve.tensor_reduce(above_n[:], above[:], AX, ALU.add)
                for n in range(NT):
                    ins = dve.tensor_tensor_scan(rank[:, n, :], one_t[:], equal[:, n, :], 0.0, ALU.mult, ALU.add)
                after(ins)
                after(dve.tensor_tensor(rank[:], rank[:], wide(above_n[:]), ALU.add))
                after(dve.scalar_tensor_tensor(ok[:], rank[:], float(K1), equal[:], ALU.is_le, ALU.mult))
                after(dve.tensor_tensor(ok[:], ok[:], above[:], ALU.add))
                after(dve.tensor_tensor(wts[:], prob[:], ok[:], ALU.mult))
                after(dve.tensor_reduce(wsum[:], wts[:], AX, ALU.add))
                after(dve.tensor_scalar(wsum[:], wsum[:], 1e-20, None, ALU.add))
                after(dve.reciprocal(inv[:], wsum[:]))
                after(dve.tensor_tensor(comb[:, :, 0:E1], wts[:], wide(inv[:]), ALU.mult))
                dve.wait_ge(split_done, 1)
                after(dve.tensor_tensor(h_lo[:], hT[:], h_hi[:], ALU.subtract))


def experts1(nc, src, h_hi, h_lo, comb, gate, x_res):
    with ExitStack() as ctx:
        def sb(name, shape, dt=F32):
            return ctx.enter_context(nc.sbuf_tensor(name, shape, dt))

        def sem(n):
            return nc.alloc_semaphore("e1_" + n)

        wu = [sb(f"wu{i}", [P, KD, 2 * I1]) for i in range(2)]
        wd = [sb(f"wd{i}", [HI1, 2, D]) for i in range(2)]
        wu_hi, wu_lo = ([sb(f"wu_{n}{i}", [P, KD, 2 * I1], F32R) for i in range(2)] for n in ("hi", "lo"))
        wd_hi, wd_lo = ([sb(f"wd_{n}{i}", [HI1, 2, D], F32R) for i in range(2)] for n in ("hi", "lo"))
        sil = [sb(f"sil{i}", [HI1, 512]) for i in range(2)]
        prod = [sb(f"prod{i}", [HI1, 512]) for i in range(2)]
        a_hi, a_lo = ([sb(f"a_{n}{i}", [HI1, 2, T], F32R) for i in range(2)] for n in ("hi", "lo"))
        acc = sb("acc", [P, NT, D])
        up_ps = [ctx.enter_context(nc.psum_tensor(f"up1_ps{i}", [P, 2, 512], F32)) for i in range(2)]
        dn_ps = [ctx.enter_context(nc.psum_tensor(f"dn1_ps{i}", [P, 512], F32)) for i in range(4)]
        w_ready = [sem("w_ready0"), sem("w_ready1")]
        w_hi, w_split, up_ready, sil_done, prod_done, hi_done, lo_done, dn_ready, summed, last_step = (
            sem(n) for n in ("w_hi", "w_split", "up_ready", "sil_done", "prod_done", "hi_done", "lo_done", "dn_ready", "summed", "last_step"))
        acc_zero, pool_steps = sem("acc_zero"), sem("pool_steps")
        UNITS = [(c, half) for c in range(2) for half in range(2)]

        def steps(eng, step):
            step(0, 0)
            step(1, 1)
            with eng.Fori(1, NE1 // 2) as pair:
                for b in range(2):
                    step(2 * pair + b, b)
            step(NE1, 0)

        def real(e):
            return not isinstance(e, int) or 0 <= e < NE1

        with nc.Block() as block:

            @block.sync
            def _(sp):
                def load(e, b):
                    wait_pos(sp, w_split, 2 * (e - 1))
                    sp.dma_start(wu[b][:], src["w_up1"][:, bass.ds(e, 1)].rearrange("p a k i -> p (a k) i")).then_inc(w_ready[b], 16)
                    sp.dma_start(wd[b][:], src["w_dn1"][:, bass.ds(e, 1)].rearrange("p a c d -> p (a c) d")).then_inc(w_ready[b], 16)

                load(0, 0)
                load(1, 1)
                with sp.Fori(1, NE1 // 2) as pair:
                    for b in range(2):
                        load(2 * pair + b, b)

            @block.gpsimd
            def _(pool):
                def step(e, b):
                    if not real(e):
                        return
                    pool.wait_ge(w_ready[b], 16 * e - 16 * b + 32)
                    wait_pos(pool, dn_ready, NT * (e - 1))
                    pool.sem_inc(pool_steps, 1)
                    pool.tensor_copy(wu_hi[b][:], wu[b][:]).then_inc(w_hi, 1)
                    pool.tensor_copy(wd_hi[b][:], wd[b][:]).then_inc(w_hi, 1)
                    pool.wait_ge(w_hi, 2 * e + 2)
                    pool.tensor_tensor(wu_lo[b][:], wu[b][:], wu_hi[b][:], ALU.subtract).then_inc(w_split, 1)
                    pool.tensor_tensor(wd_lo[b][:], wd[b][:], wd_hi[b][:], ALU.subtract).then_inc(w_split, 1)

                steps(pool, step)

            @block.tensor
            def _(pe):
                def step(e, b):
                    if real(e):
                        pe.wait_ge(w_split, 2 * e + 2)
                        for q, (c, half) in enumerate(UNITS):
                            wait_pos(pe, prod_done, 4 * e + q - 1)
                            for g in range(2):
                                cols = slice(g * I1 + c * HI1, g * I1 + (c + 1) * HI1)
                                for k in range(KD):
                                    for n, (w, h) in enumerate(((wu_hi, h_hi), (wu_lo, h_hi), (wu_hi, h_lo))):
                                        mm = pe.matmul(up_ps[q % 2][0:HI1, g, :], w[b][:, k, cols], h[:, k, half * 512:(half + 1) * 512],
                                                       start=(k == 0 and n == 0), stop=(k == KD - 1 and n == 2))
                            mm.then_inc(up_ready, 1)
                    if real(e - 1):
                        for t in range(NT):
                            if t % 4 == 0:
                                pe.wait_ge(lo_done, 4 * e - 1 + t // 4)
                            wait_pos(pe, summed, NT * (e - 1) + t - 3)
                            for c in range(2):
                                for n, (a, w) in enumerate(((a_hi, wd_hi), (a_hi, wd_lo), (a_lo, wd_hi))):
                                    mm = pe.matmul(dn_ps[t % 4][:, 0:D], a[1 - b][:, c, t * P:(t + 1) * P], w[1 - b][:, c, :],
                                                   start=(c == 0 and n == 0), stop=(c == 1 and n == 2))
                            mm.then_inc(dn_ready, 1)

                steps(pe, step)

            @block.scalar
            def _(act):
                def step(e, b):
                    if not real(e):
                        return
                    for q in range(5):
                        if q < 4:
                            act.wait_ge(up_ready, 4 * e + q + 1)
                            wait_pos(act, prod_done, 4 * e + q - 1)
                            act.activation(sil[q % 2][:], up_ps[q % 2][0:HI1, 0, :], ACT.Silu).then_inc(sil_done, 1)
                        if q >= 1:
                            c, half = UNITS[q - 1]
                            act.wait_ge(prod_done, 4 * e + q)
                            wait_pos(act, dn_ready, NT * (e - 1))
                            act.activation(a_hi[b][:, c, half * 512:(half + 1) * 512], prod[(q - 1) % 2][:], ACT.Copy).then_inc(hi_done, 1)

                steps(act, step)

            @block.vector
            def _(dve):
                def step(e, b):
                    if real(e):
                        for q in range(5):
                            if q < 4:
                                dve.wait_ge(sil_done, 4 * e + q + 1)
                                wait_pos(dve, lo_done, 4 * e + q - 1)
                                dve.tensor_tensor(prod[q % 2][:], sil[q % 2][:], up_ps[q % 2][0:HI1, 1, :], ALU.mult).then_inc(prod_done, 1)
                            if q >= 1:
                                c, half = UNITS[q - 1]
                                dve.wait_ge(hi_done, 4 * e + q)
                                cols = slice(half * 512, (half + 1) * 512)
                                dve.tensor_tensor(a_lo[b][:, c, cols], prod[(q - 1) % 2][:], a_hi[b][:, c, cols], ALU.subtract)\
                                   .then_inc(lo_done, 1)
                    if real(e - 1):
                        for t in range(NT):
                            dve.wait_ge(dn_ready, NT * (e - 1) + t + 1)
                            wait_pos(dve, summed, NT * (e - 2) + t + 1)
                            w = comb[:, t, e - 1:e] if isinstance(e, int) else comb[:, t, bass.ds(e - 1, 1)]
                            dve.scalar_tensor_tensor(acc[:, t, :], dn_ps[t % 4][:, 0:D], w, acc[:, t, :], ALU.mult, ALU.add).then_inc(summed, 1)

                dve.memset(acc[:], 0.0).then_inc(acc_zero, 1)
                dve.wait_ge(acc_zero, 1)
                steps(dve, step)
                for t in range(NT):
                    dve.wait_ge(summed, NT * (NE1 - 1) + t + 1)
                    dve.tensor_tensor(acc[:, t, :], acc[:, t, :], gate, ALU.mult).then_inc(last_step, 1)
                dve.wait_ge(last_step, NT)
                dve.tensor_tensor(x_res[:], x_res[:], acc[:], ALU.add).then_inc(last_step, 1)


def rest(nc, src, x_res, row, ident, ident_b, mask_b, eps_col, stop):
    with ExitStack() as ctx:
        def sb(name, shape, dt=F32):
            return ctx.enter_context(nc.sbuf_tensor(name, shape, dt))

        posT, xgT, wg = sb("posT", [P, T], BF16), sb("xgT", [P, KD, SLOTS]), sb("wg", [P, SLOTS])
        with ExitStack() as inner:
            onehot = inner.enter_context(nc.sbuf_tensor("onehot", [P, NT, SLOTS], F32R))
            hw_hi = inner.enter_context(nc.sbuf_tensor("hw_hi", [P, NT, D + P], F32R))
            hw_lo = inner.enter_context(nc.sbuf_tensor("hw_lo", [P, NT, D + P], F32R))
            with ExitStack() as routing:
                h = routing.enter_context(nc.sbuf_tensor("h1", [P, NT, D], F32))
                hT = routing.enter_context(nc.sbuf_tensor("h1T", [P, KD, T], F32))
                norm_tiles(nc, "ln1", x_res, row(0, 4), row(0, 3), h, hT, ident, eps_col)
                route0(nc, src, h, hT, hw_hi, hw_lo, onehot, posT, ident)
            gather0(nc, src, hw_hi, hw_lo, onehot, xgT, wg)
        experts0(nc, src, xgT, wg, posT, row(0, 5), x_res)
    if stop < 3:
        return
    with ExitStack() as ctx:
        def sb(name, shape, dt=F32):
            return ctx.enter_context(nc.sbuf_tensor(name, shape, dt))

        rows = sb("ln_rows", [P, 2, D])
        hm, h, hT = sb("hm", [P, NT, D]), sb("h2", [P, NT, D]), sb("h2T", [P, KD, T])
        qT, kT, value, catT = sb("q1T", [QK1, T]), sb("k1T", [QK1, T]), sb("value", [P, NT, D]), sb("catT", [P, 4, T])
        bias = sb("bias", [P, T])
        rows_loaded = nc.alloc_semaphore("rows_loaded")
        with nc.Block() as block:

            @block.sync
            def _(sp):
                sp.dma_start(rows[:, 0, :], src["ln_gamma"].to_broadcast([P, D])).then_inc(rows_loaded, 16)
                sp.dma_start(rows[:, 1, :], src["ln_beta"].to_broadcast([P, D])).then_inc(rows_loaded, 16)
                sp.wait_ge(rows_loaded, 32)

        norm_tiles(nc, "ln2", x_res, row(1, 1), row(1, 0), hm, None, ident, eps_col)
        norm_tiles(nc, "ln3", hm, rows[:, 0, :], rows[:, 1, :], h, hT, ident, eps_col)
        project1(nc, src, hT, qT, kT, value, catT, bias, mask_b)
        attend1(nc, src, qT, kT, value, catT, bias, hm, row(1, 2), x_res, ident)
    if stop < 4:
        return
    with ExitStack() as ctx:
        def sb(name, shape, dt=F32):
            return ctx.enter_context(nc.sbuf_tensor(name, shape, dt))

        h_hi, h_lo, comb = sb("h3_hi", [P, KD, T], F32R), sb("h3_lo", [P, KD, T], F32R), sb("comb", [P, NT, NE1])
        with nc.sbuf_tensor("h3", [P, NT, D], F32) as h, nc.sbuf_tensor("h3T", [P, KD, T], F32) as hT:
            norm_tiles(nc, "ln4", x_res, row(1, 4), row(1, 3), h, hT, ident, eps_col)
            route1(nc, src, hT, comb, h_hi, h_lo)
        experts1(nc, src, h_hi, h_lo, comb, row(1, 5), x_res)


def store(nc, x, out):
    stored = nc.alloc_semaphore("stored")
    with nc.Block() as block:

        @block.sync
        def _(sp):
            sp.dma_start(out.rearrange("o (n p) d -> p (o n) d", p=P), x[:]).then_inc(stored, 16)
            sp.wait_ge(stored, 16)


def build(nc, src, out, stop=99):
    with ExitStack() as ctx:
        def sb(name, shape, dt=F32):
            return ctx.enter_context(nc.sbuf_tensor(name, shape, dt))

        x_res = sb("x_res", [P, NT, D])
        modv = sb("modv", [P, 2, 6 * D])
        ident, ident_b = sb("ident", [P, P]), sb("ident_b", [P, P], BF16)
        mask_b = sb("mask_b", [P, P], BF16)
        eps_col = sb("eps_col", [P, 1])
        x_loaded = nc.alloc_semaphore("x_loaded")

        def row(l, j):
            return modv[:, l, j * D:(j + 1) * D]

        consts = [(ident[:], "ident"), (ident_b[:], "ident_b"), (mask_b[:], "mask_b"), (eps_col[:], "eps")]
        with ExitStack() as inner:
            outT = inner.enter_context(nc.sbuf_tensor("outT", [P, H, T], F32))
            with ExitStack() as first:
                rope = first.enter_context(nc.sbuf_tensor("rope", [P, 2, NT, 2, DH], F32))
                w_down = first.enter_context(nc.sbuf_tensor("w_down", [P, KD, P], F32))
                hT = first.enter_context(nc.sbuf_tensor("hT", [P, KD, T], F32))
                modulation(nc, sb, src, consts + [(rope[:], "rope"), (w_down[:], "w_down_p")], modv, x_res, x_loaded)
                with nc.sbuf_tensor("h0", [P, NT, D], F32) as h:
                    norm_tiles(nc, "ln0", x_res, row(0, 1), row(0, 0), h, hT, ident, eps_col)
                ckvT = first.enter_context(nc.sbuf_tensor("ckvT", [P, T], F32))
                latent(nc, src, hT, ckvT, w_down)
                attention0(nc, src, hT, ckvT, outT, rope, ident, ident_b, mask_b)
            output0(nc, src, outT, row(0, 2), x_res)
        if stop > 1:
            rest(nc, src, x_res, row, ident, ident_b, mask_b, eps_col, stop)
        store(nc, x_res, out)


def laid_out(inputs):
    import numpy as np

    a = {k: np.ascontiguousarray(v) for k, v in inputs.items()}
    f32 = np.float32
    wq = a["L0_attn_wq"].reshape(D, H, DH // 2, 2).transpose(0, 1, 3, 2).reshape(D, H * DH)
    wup = a["L0_attn_w_up"].reshape(P, H, 2, DH)
    wk = wup[:, :, 0].reshape(P, H, DH // 2, 2).transpose(0, 1, 3, 2).reshape(P, H, 1, DH)
    wup = np.concatenate([wk, wup[:, :, 1:]], axis=2).reshape(P, H * 2 * DH)
    inv_freq = (1.0 / 10000.0 ** (np.arange(0, DH, 2, dtype=f32) / f32(DH))).astype(f32)
    ang = np.arange(T, dtype=f32)[:, None] * inv_freq[None, :]
    cos, sin = np.cos(ang).astype(f32), np.sin(ang).astype(f32)
    table = np.stack([np.concatenate([cos, cos], 1), np.concatenate([-sin, sin], 1)])
    table = np.stack([table * f32(DH ** -0.5), table], axis=2)
    table = table.reshape(2, NT, P, 2, DH).transpose(2, 0, 1, 3, 4)
    upper = np.arange(P)[None, :] > np.arange(P)[:, None]
    bf = np.dtype("bfloat16")
    out = {
        "L0_attn_x": a["L0_attn_x"], "wq_split": wq, "L0_attn_w_up": wup, "L0_attn_wo": a["L0_attn_wo"],
        "w_down_p": a["L0_attn_w_down"].reshape(KD, P, P).transpose(1, 0, 2),
        "L0_c": a["L0_c"], "L1_c": a["L1_c"], "L0_wmod": a["L0_wmod"], "L1_wmod": a["L1_wmod"],
        "rope": table, "ident": np.eye(P, dtype=f32), "ident_b": np.eye(P).astype(bf),
        "mask_b": np.where(upper, -3e38, 0.0).astype(bf), "eps": np.full((P, 1), EPS, f32),
    }
    experts, slots = np.arange(P), np.arange(SLOTS)
    w1 = np.stack([a["L0_ffn_w1"], a["L0_ffn_v1"]]).reshape(2, E0, F0, KD, P)
    out |= {
        "router_t": a["L0_ffn_router_w"].reshape(E0, KD, P).transpose(2, 1, 0),
        "ones_b": np.ones((P, P)).astype(bf), "before_b": upper.astype(bf),
        "slot_c": np.tile(np.arange(C0, dtype=f32), (P, 1)),
        "own_b": (slots[None, :] // C0 == experts[:, None]).astype(bf),
        "sel_b": (slots[None, :] // C0 == experts[:, None]).astype(bf).reshape(P, NSB, P),
        "ones_f": np.ones((P, F0), f32), "c_col": (np.arange(P) % C0).astype(f32)[:, None],
        "w_up0": w1.transpose(4, 1, 0, 3, 2), "w_dn0": a["L0_ffn_w2"].transpose(1, 0, 2),
    }
    rel = np.arange(T, dtype=f32)[None, :] - np.arange(P, dtype=f32)[:, None] - f32(T - P)
    gate_s, up_s = a["L1_ffn_shared_wg"].reshape(2, 2, I1, D)
    wg = np.concatenate([a["L1_ffn_expert_wg"], np.stack([gate_s, up_s], 1).reshape(2, 2 * I1, D)])
    wd = np.concatenate([a["L1_ffn_expert_wd"], a["L1_ffn_shared_wd"].reshape(D, 2, I1).transpose(1, 0, 2)])
    out |= {
        "expand_t": a["L1_attn_expand"].reshape(-1, KD, P).transpose(2, 1, 0), "rel": rel,
        "project_t": a["L1_attn_project"].reshape(D, 4, P).transpose(2, 1, 0),
        "pos_mult": a["L1_attn_pos_mult"].reshape(1, 1),
        "ln_gamma": a["L1_attn_ln_gamma"].reshape(1, D), "ln_beta": a["L1_attn_ln_beta"].reshape(1, D),
        "gate_t": a["L1_ffn_gate_w"].reshape(E1, KD, P).transpose(2, 1, 0),
        "w_up1": wg.reshape(NE1, 2 * I1, KD, P).transpose(3, 0, 2, 1),
        "w_dn1": wd.reshape(NE1, D, 2, HI1).transpose(3, 0, 2, 1),
    }
    return {k: np.ascontiguousarray(v) for k, v in out.items()}


def kernel(**inputs):
    import concourse.bacc as _bacc
    from concourse import mybir as _mybir
    from concourse.bass_utils import run_bass_kernel_spmd as _run

    nc = _bacc.Bacc("TRN2", target_bir_lowering=False, num_devices=1)
    arrays = laid_out(inputs)
    src = {n: nc.dram_tensor(f"in_{n}", a.shape, _mybir.dt.from_np(a.dtype), kind="ExternalInput").ap() for n, a in arrays.items()}
    out = nc.dram_tensor("out", (1, T, D), F32, kind="ExternalOutput").ap()
    build(nc, src, out)
    r = _run(nc, [{f"in_{n}": a for n, a in arrays.items()}], core_ids=[0])
    return r.results[0]["out"]
```

```python
from contextlib import ExitStack

import concourse.bass as bass
from concourse import mybir

F32 = mybir.dt.float32
F32R = mybir.dt.float32r
BF16 = mybir.dt.bfloat16
ALU = mybir.AluOpType
ACT = mybir.ActivationFunctionType
AX = mybir.AxisListType.X

P = 128
T = 1024
NT = T // P
D = 256
KD = D // P
H = 16
DH = 128
LAG = 7
QLAG = 3
EPS = 1e-5

E0, K0, F0, C0 = 64, 8, 96, 32
SLOTS = E0 * C0
NSB = SLOTS // P
EPB = P // C0

QK1, EXP1 = D // 8, 2 * D
E1, K1, I1 = 8, 2, 176
SI1 = 2 * I1


def wait_pos(eng, sem, count):
    if not isinstance(count, int) or count > 0:
        eng.wait_ge(sem, count)


def modulation(nc, sb, src, cst, late, late_loaded, modv, x_res, load_sem):
    with ExitStack() as ctx:
        c_col = ctx.enter_context(nc.sbuf_tensor("c_col", [P, 2, KD], F32))
        s_col = ctx.enter_context(nc.sbuf_tensor("s_col", [P, 2, KD], F32))
        s_wide = ctx.enter_context(nc.sbuf_tensor("s_wide", [P, 2, KD, P], F32))
        wmod = ctx.enter_context(nc.sbuf_tensor("wmod", [P, 2, KD, 6 * D], F32))
        gneg = ctx.enter_context(nc.sbuf_tensor("gneg", [P, 2, 2, D], F32))
        gsign = ctx.enter_context(nc.sbuf_tensor("gsign", [P, 2, 2, D], F32))
        ps = [ctx.enter_context(nc.psum_tensor(f"mod_ps{i}", [P, 512], F32)) for i in range(6)]
        c_loaded, wmod_loaded, const_loaded = (nc.alloc_semaphore(n) for n in ("c_loaded", "wmod_loaded", "const_loaded"))
        silu_done, wide_done, mod_ready, mod_copied, gate_step = (
            nc.alloc_semaphore(n) for n in ("silu_done", "wide_done", "mod_ready", "mod_copied", "gate_step"))
        with nc.Block() as block:

            @block.sync
            def _(sp):
                for l in range(2):
                    sp.dma_start(c_col[:, l, :], src[f"L{l}_c"].rearrange("o (k p) -> p (o k)", p=P),
                                 allow_slow_non_contiguous=True).then_inc(c_loaded, 16)
                for l in range(2):
                    sp.dma_start(wmod[:, l], src[f"L{l}_wmod"].rearrange("(k p) n -> p k n", p=P)).then_inc(wmod_loaded, 16)
                sp.dma_start(x_res[:], src["L0_attn_x"].rearrange("o (n p) d -> p (o n) d", p=P)).then_inc(load_sem, 16)
                for dst, name in cst:
                    sp.dma_start(dst, src[name]).then_inc(const_loaded, 16)
                for dst, name in late:
                    sp.dma_start(dst, src[name]).then_inc(late_loaded, 16)
                sp.wait_ge(load_sem, 16)
                sp.wait_ge(const_loaded, 16 * len(cst))

            @block.scalar
            def _(act):
                act.wait_ge(c_loaded, 32)
                act.activation(s_col[:], c_col[:], ACT.Silu).then_inc(silu_done, 1)

            @block.tensor
            def _(pe):
                pe.wait_ge(wmod_loaded, 32)
                pe.wait_ge(wide_done, 4)
                for l in range(2):
                    for n in range(3):
                        for k in range(KD):
                            mm = pe.matmul(ps[3 * l + n][:], s_wide[:, l, k, :], wmod[:, l, k, n * 512:(n + 1) * 512],
                                           start=(k == 0), stop=(k == KD - 1))
                        mm.then_inc(mod_ready, 1)

            @block.vector
            def _(dve):
                dve.wait_ge(silu_done, 1)
                for l in range(2):
                    for k in range(KD):
                        dve.tensor_copy(s_wide[:, l, k, :], s_col[:, l, k:k + 1].to_broadcast([P, P])).then_inc(wide_done, 1)
                for l in range(2):
                    for n in range(3):
                        dve.wait_ge(mod_ready, 3 * l + n + 1)
                        dve.tensor_copy(modv[:, l, n * 512:(n + 1) * 512], ps[3 * l + n][:]).then_inc(mod_copied, 1)
                dve.wait_ge(mod_copied, 6)
                m = modv[:].rearrange("p l (a b d) -> p l a b d", a=2, b=3)
                dve.tensor_scalar(m[:, :, :, 1, :], m[:, :, :, 1, :], 1.0, None, ALU.add).then_inc(gate_step, 1)
                dve.tensor_scalar(gneg[:], m[:, :, :, 2, :], -1.0, 0.25, ALU.mult, ALU.max).then_inc(gate_step, 1)
                dve.tensor_scalar(gsign[:], m[:, :, :, 2, :], 0.0, 2.0, ALU.is_ge, ALU.mult).then_inc(gate_step, 1)
                dve.wait_ge(gate_step, 3)
                for l in range(2):
                    dve.tensor_tensor(gneg[:, l], gneg[:, l], m[:, l, :, 2, :], ALU.max).then_inc(gate_step, 1)
                dve.wait_ge(gate_step, 5)
                for l in range(2):
                    dve.scalar_tensor_tensor(m[:, l, :, 2, :], gsign[:, l], -1.0, gneg[:, l], ALU.add, ALU.mult).then_inc(gate_step, 1)
                dve.wait_ge(gate_step, 7)


class NormSems:

    def __init__(self, nc):
        self.stats, self.mv, self.std, self.rstd, self.z, self.h, self.turned, self.copied = (
            nc.alloc_semaphore("ln_" + n) for n in ("stats", "mv", "std", "rstd", "z", "h", "turned", "copied"))
        self.norms = self.turns = 0


def norm_tiles(nc, tag, sems, x, scale, shift, h, hT, ident, eps_col):
    with ExitStack() as ctx:
        stats = ctx.enter_context(nc.sbuf_tensor(f"{tag}_stats", [P, NT, 6], F32))
        mv = ctx.enter_context(nc.sbuf_tensor(f"{tag}_mv", [P, NT, 2], F32))
        std = ctx.enter_context(nc.sbuf_tensor(f"{tag}_std", [P, NT], F32))
        rstd = ctx.enter_context(nc.sbuf_tensor(f"{tag}_rstd", [P, NT], F32))
        z = ctx.enter_context(nc.sbuf_tensor(f"{tag}_z", [P, NT, D], F32))
        ps = [ctx.enter_context(nc.psum_tensor(f"{tag}_ps{i}", [P, 512], F32)) for i in range(4)]
        norms, turns = sems.norms, sems.turns
        with nc.Block() as block:

            @block.vector
            def _(dve):
                for t in range(NT):
                    dve.bn_stats(stats[:, t, :], x[:, t, :]).then_inc(sems.stats, 1)
                for t in range(NT):
                    dve.wait_ge(sems.stats, norms * NT + t + 1)
                    dve.bn_aggr(mv[:, t, :], stats[:, t, :]).then_inc(sems.mv, 1)
                dve.wait_ge(sems.mv, norms * NT + NT)
                for t in range(NT):
                    dve.scalar_tensor_tensor(z[:, t, :], x[:, t, :], mv[:, t, 0:1], scale, ALU.subtract, ALU.mult).then_inc(sems.z, 1)
                    if t == 1:
                        dve.wait_ge(sems.std, norms + 1)
                        dve.reciprocal(rstd[:], std[:]).then_inc(sems.rstd, 1)
                dve.wait_ge(sems.rstd, norms + 1)
                for t in range(NT):
                    dve.wait_ge(sems.z, norms * NT + t + 1)
                    dve.scalar_tensor_tensor(h[:, t, :], z[:, t, :], rstd[:, t:t + 1], shift, ALU.mult, ALU.add).then_inc(sems.h, 1)

            @block.scalar
            def _(act):
                act.wait_ge(sems.mv, norms * NT + NT)
                act.activation(std[:], mv[:, :, 1], ACT.Sqrt, bias=eps_col[:]).then_inc(sems.std, 1)
                if hT is not None:
                    for t in range(NT):
                        act.wait_ge(sems.turned, turns + t + 1)
                        act.activation(hT[:, :, t * P:(t + 1) * P], ps[t % 4][:, 0:KD * P].rearrange("p (k c) -> p k c", k=KD),
                                       ACT.Copy).then_inc(sems.copied, 1)

            @block.tensor
            def _(pe):
                if hT is not None:
                    for t in range(NT):
                        pe.wait_ge(sems.h, norms * NT + t + 1)
                        if t >= 4:
                            pe.wait_ge(sems.copied, turns + t - 3)
                        for k in range(KD):
                            mm = pe.transpose(ps[t % 4][:, k * P:(k + 1) * P], h[:, t, k * P:(k + 1) * P], ident[:])
                        mm.then_inc(sems.turned, 1)

    sems.norms += 1
    sems.turns += NT if hT is not None else 0


def latent(nc, src, hT, ckvT, ckv, w_down, wv_t, wo, late_loaded, ident):
    with ExitStack() as ctx:
        ps = [ctx.enter_context(nc.psum_tensor(f"lat_ps{i}", [P, 512], F32)) for i in range(8)]
        lat_ready, lat_copied, turned, ckv_copied, wov_ready, wov_copied = (
            nc.alloc_semaphore("lat_" + n) for n in ("ready", "copied", "turned", "ckv_copied", "wov_ready", "wov_copied"))
        with nc.Block() as block:

            @block.tensor
            def _(pe):
                for c in range(2):
                    for k in range(KD):
                        mm = pe.matmul(ps[c][:], w_down[:, k, :], hT[:, k, c * 512:(c + 1) * 512], start=(k == 0), stop=(k == KD - 1))
                    mm.then_inc(lat_ready, 1)
                pe.wait_ge(late_loaded, 32)
                for g in range(H // 2):
                    if g == 2:
                        for c in range(2):
                            pe.wait_ge(lat_copied, c + 1)
                            for n in range(4):
                                mm = pe.transpose(ps[2 + c][:, n * P:(n + 1) * P], ckvT[:, (4 * c + n) * P:(4 * c + n + 1) * P], ident[:])
                            mm.then_inc(turned, 1)
                    if g >= 4:
                        pe.wait_ge(wov_copied, g - 3)
                    for u in range(2):
                        mm = pe.matmul(ps[4 + g % 4][:, u * D:(u + 1) * D], wv_t[:, 2 * g + u, :], wo[:, 2 * g + u, :],
                                       start=(u == 0), stop=True, skip_group_check=True)
                    mm.then_inc(wov_ready, 1)

            @block.vector
            def _(dve):
                for c in range(2):
                    dve.wait_ge(lat_ready, c + 1)
                    dve.tensor_copy(ckvT[:, c * 512:(c + 1) * 512], ps[c][:]).then_inc(lat_copied, 1)
                for c in range(2):
                    dve.wait_ge(turned, c + 1)
                    dve.tensor_copy(ckv[:, 4 * c:4 * c + 4, :], ps[2 + c][:].rearrange("p (n l) -> p n l", n=4)).then_inc(ckv_copied, 1)

            @block.scalar
            def _(act):
                for g in range(H // 2):
                    act.wait_ge(wov_ready, g + 1)
                    act.activation(wo[:, 2 * g:2 * g + 2, :], ps[4 + g % 4][:].rearrange("p (u d) -> p u d", u=2),
                                   ACT.Copy).then_inc(wov_copied, 1)


def attention0(nc, src, hT, ckvT, ckv, outT, rope, ident, ident_b, mask_b):
    with ExitStack() as ctx:
        def sb(name, shape, dt=F32):
            return ctx.enter_context(nc.sbuf_tensor(name, shape, dt))

        def ps(name):
            return ctx.enter_context(nc.psum_tensor(name, [P, 512], F32))

        w_q = [sb(f"w_q{b}", [P, KD, DH]) for b in range(2)]
        w_k = [sb(f"w_k{b}", [P, DH]) for b in range(2)]
        qk_hi = [sb(f"qk_hi{b}", [P, 2, T], F32R) for b in range(2)]
        qk_lo = [sb(f"qk_lo{b}", [P, 2, T], F32R) for b in range(2)]
        rope_a = [sb(f"rope_a{b}", [P, 2, DH]) for b in range(2)]
        rope_b = [sb(f"rope_b{b}", [P, 2, DH]) for b in range(2)]
        rope_r = [sb(f"rope_r{b}", [P, 2, DH]) for b in range(4)]
        turned = [sb(f"turned{b}", [P, 2, P]) for b in range(2)]
        probs = [sb(f"probs{b}", [P, T]) for b in range(4)]
        probsT = [sb(f"probsT{b}", [P, NT, P]) for b in range(2)]
        nmax, rowsum, rinv = sb("nmax", [P, 4]), sb("rowsum", [P, 4]), sb("rinv", [P, 4])
        s_ps = [ctx.enter_context(nc.psum_tensor(f"s_ps{b}", [P, 2, 512], F32)) for b in range(2)]
        t_ps, o_ps, pj_ps = [ps("t_ps0"), ps("t_ps1")], ps("o_ps"), ps("pj_ps")

        def sem(n):
            return nc.alloc_semaphore("a0_" + n)

        w_ready = [sem("w_ready0"), sem("w_ready1")]
        proj_done, ab_done, rope_done, qk_turned, qk_copied, qk_split = (
            sem(n) for n in ("proj_done", "ab_done", "rope_done", "qk_turned", "qk_copied", "qk_split"))
        s_ready, max_done, exp_done, recip_done, norm_done = (
            sem(n) for n in ("s_ready", "max_done", "exp_done", "recip_done", "norm_done"))
        t_ready = [sem("t_ready0"), sem("t_ready1")]
        t_copied = [sem("t_copied0"), sem("t_copied1")]
        pv_done, o_copied, pool_steps = sem("pv_done"), sem("o_copied"), sem("pool_steps")

        wq_d = src["wq_split"].rearrange("(k p) n -> p k n", p=P)
        wk_d = src["w_k"]

        def scores_view(slot, i):
            w = (i + 1) * P
            if w <= 512:
                return s_ps[slot][:, 0:1, 0:w], [(0, 0, w)]
            return s_ps[slot][:, 0:2, 0:w // 2], [(0, 0, w // 2), (1, w // 2, w)]

        def steps(eng, step):
            for i in range(NT):
                step(0, i, 0)
            with eng.Fori(0, (H - 2) // 2) as pair:
                for u in (1, 2):
                    for i in range(NT):
                        step(2 * pair + u, i, u % 2)
            for i in range(NT):
                step(H - 1, i, (H - 1) % 2)
            for i in range(4):
                step(H, i, H % 2)

        def at(h, i, u):
            if i < 0:
                h, i, u = h - 1, i + NT, 1 - u
            if i >= NT:
                h, i, u = h + 1, i - NT, 1 - u
            return h, i, u, h * NT + i

        def real(h):
            return not isinstance(h, int) or 0 <= h < H

        with nc.Block() as block:

            @block.sync
            def _(sp):
                def load(h, b):
                    wait_pos(sp, proj_done, NT * (h - 1))
                    sp.dma_start(w_q[b][:], wq_d[:, :, bass.ds(h * DH, DH)]).then_inc(w_ready[b], 16)
                    sp.dma_start(w_k[b][:], wk_d[:, bass.ds(h * DH, DH)]).then_inc(w_ready[b], 16)

                load(0, 0)
                load(1, 1)
                with sp.Fori(1, H // 2) as pair:
                    for b in range(2):
                        load(2 * pair + b, b)

            @block.tensor
            def _(pe):
                def project(h, i, u, n):
                    wait_pos(pe, ab_done, n)
                    pe.wait_ge(w_ready[u], 16 * h + 32 - 16 * u)
                    for k in range(KD):
                        pe.matmul(pj_ps[:, 0:DH], hT[:, k, i * P:(i + 1) * P], w_q[u][:, k, :],
                                  start=(k == 0), stop=(k == KD - 1))
                    pe.matmul(pj_ps[:, DH:2 * DH], ckvT[:, i * P:(i + 1) * P], w_k[u][:],
                              start=False, stop=True, skip_group_check=True).then_inc(proj_done, 1)

                def turn_qk(n, b, g):
                    pe.wait_ge(rope_done, n + 1)
                    wait_pos(pe, o_copied, g - 3)
                    wait_pos(pe, qk_copied, n)
                    for j in range(2):
                        mm = pe.transpose(o_ps[:, (2 + j) * P:(3 + j) * P], rope_r[b][:, j, :], ident[:])
                    mm.then_inc(qk_turned, 1)

                def step(h, i, u):
                    g = h * NT + i
                    hn, tn, un, n = at(h, i + LAG, u)
                    hp, tp, up, _ = at(h, i - 2, u)
                    hv, tv, _, _ = at(h, i - 3, u)
                    hl = at(h, i + LAG - QLAG, u)[0]
                    if real(h):
                        pe.wait_ge(qk_split, g + (2 if i == 0 else 1))
                        wait_pos(pe, exp_done, g - 1)
                        _, parts = scores_view(i % 2, i)
                        d0 = i * P
                        for bank, lo, hi in parts:
                            last = hi == (i + 1) * P
                            if last:
                                pe.matmul(s_ps[i % 2][:, bank, d0 - lo:d0 - lo + P], ident_b[:], mask_b[:],
                                          start=True, stop=False, skip_group_check=True)
                            top = max(hi, 2 * P)
                            for m, (q, k) in enumerate(((qk_hi, qk_hi), (qk_hi, qk_lo), (qk_lo, qk_hi))):
                                mm = pe.matmul(s_ps[i % 2][:, bank, 0:top - lo], q[u][:, 0, i * P:(i + 1) * P], k[u][:, 1, lo:top],
                                               start=(m == 0 and not last), stop=(m == 2), skip_group_check=True)
                        mm.then_inc(s_ready, 1)
                    if real(hl):
                        turn_qk(n - QLAG, (i + LAG - QLAG) % 4, g)
                    if real(hp):
                        pe.wait_ge(norm_done, g - 1)
                        for j in range(tp // 4 + 1):
                            before = g - 2 if j == 0 else hp * 4 + tp - 4
                            wait_pos(pe, t_copied[j], before)
                            for kb in range(4 * j, min(4 * j + 4, tp + 1)):
                                mm = pe.transpose(t_ps[j][:, (kb % 4) * P:(kb % 4 + 1) * P],
                                                  probs[tp % 4][:, kb * P:(kb + 1) * P], ident[:])
                            mm.then_inc(t_ready[j], 1)
                    if real(hn):
                        project(hn, tn, un, n)
                    if real(hv):
                        pe.wait_ge(t_copied[0], g - 2)
                        wait_pos(pe, o_copied, g - 3)
                        if real(hl):
                            pe.wait_ge(qk_copied, n - QLAG + 1)
                        for kb in range(tv + 1):
                            if kb == 4:
                                pe.wait_ge(t_copied[1], hv * 4 + tv - 3)
                            mm = pe.matmul(o_ps[:, 0:P], ckv[:, kb, :], probsT[tv % 2][:, kb, :],
                                           start=(kb == 0), stop=(kb == tv))
                        mm.then_inc(pv_done, 1)

                for n in range(LAG):
                    if n >= QLAG:
                        turn_qk(n - QLAG, (n - QLAG) % 4, 0)
                    project(0, n, 0, n)
                steps(pe, step)

            @block.vector
            def _(dve):
                def rope_products(i, n, b):
                    dve.wait_ge(proj_done, n + 1)
                    wait_pos(dve, rope_done, n - 1)
                    x = pj_ps[:, 0:2 * DH].rearrange("p (a d) -> p a d", a=2)
                    half = DH // 2
                    dve.tensor_tensor(rope_a[b][:], x, rope[:, 0, i], ALU.mult)
                    dve.tensor_tensor(rope_b[b][:, :, 0:half], x[:, :, half:DH], rope[:, 1, i, :, 0:half], ALU.mult)
                    dve.tensor_tensor(rope_b[b][:, :, half:DH], x[:, :, 0:half], rope[:, 1, i, :, half:DH],
                                      ALU.mult).then_inc(ab_done, 1)

                def step(h, i, u):
                    g = h * NT + i
                    hn, tn, un, n = at(h, i + LAG, u)
                    hl, tl, ul, nl = at(h, i + LAG - QLAG, u)
                    h1, t1, _, _ = at(h, i - 1, u)
                    hp, tp, up, _ = at(h, i - 2, u)
                    ho, to, _, _ = at(h, i - 4, u)
                    if real(ho):
                        dve.wait_ge(pv_done, g - 3)
                        dve.tensor_copy(outT[:, ho, to * P:(to + 1) * P], o_ps[:, 0:P]).then_inc(o_copied, 1)
                    if real(h1):
                        dve.wait_ge(exp_done, g)
                        dve.reciprocal(rinv[:, t1 % 4:t1 % 4 + 1], rowsum[:, t1 % 4:t1 % 4 + 1]).then_inc(recip_done, 1)
                    if real(h):
                        dve.wait_ge(s_ready, g + 1)
                        dve.tensor_reduce(nmax[:, i % 4:i % 4 + 1], scores_view(i % 2, i)[0], mybir.AxisListType.XY, ALU.max,
                                          negate=True).then_inc(max_done, 1)
                    if real(hp) and tp >= 4:
                        dve.wait_ge(t_ready[1], hp * 4 + tp - 3)
                        wait_pos(dve, pv_done, g - 3)
                        w = tp - 3
                        dve.tensor_copy(probsT[tp % 2][:, 4:4 + w, :], t_ps[1][:, 0:w * P].rearrange("p (a c) -> p a c", a=w))\
                           .then_inc(t_copied[1], 1)
                    if real(hn):
                        rope_products(tn, n, (i + LAG) % 2)

                for n in range(LAG):
                    rope_products(n, n, n % 2)
                steps(dve, step)

            @block.scalar
            def _(act):
                def copy_qk(i, u, n):
                    act.wait_ge(qk_turned, n + 1)
                    wait_pos(act, qk_split, n - 1)
                    x = o_ps[:, 2 * P:4 * P].rearrange("p (a c) -> p a c", a=2)
                    act.activation(qk_hi[u][:, :, i * P:(i + 1) * P], x, ACT.Copy)
                    act.activation(turned[i % 2][:], x, ACT.Copy).then_inc(qk_copied, 1)

                def step(h, i, u):
                    g = h * NT + i
                    hl, tl, ul, nl = at(h, i + LAG - QLAG, u)
                    hp, tp, up, _ = at(h, i - 2, u)
                    if real(hl):
                        copy_qk(tl, ul, nl)
                    if real(hp):
                        act.wait_ge(t_ready[0], g - 1)
                        wait_pos(act, pv_done, g - 3)
                        w = min(tp + 1, 4)
                        act.activation(probsT[tp % 2][:, 0:w, :], t_ps[0][:, 0:w * P].rearrange("p (a c) -> p a c", a=w),
                                       ACT.Copy).then_inc(t_copied[0], 1)
                    if real(h):
                        act.wait_ge(max_done, g + 1)
                        view, parts = scores_view(i % 2, i)
                        out = probs[i % 4][:, 0:(i + 1) * P].rearrange("p (a c) -> p a c", a=len(parts))
                        act.activation(out, view, ACT.Exp, bias=nmax[:, i % 4:i % 4 + 1],
                                       accum_out=rowsum[:, i % 4:i % 4 + 1]).then_inc(exp_done, 1)

                for n in range(LAG - QLAG):
                    copy_qk(n, 0, n)
                steps(act, step)

            @block.gpsimd
            def _(pool):
                def rope_sum(n, b, r):
                    pool.wait_ge(ab_done, n + 1)
                    wait_pos(pool, qk_turned, n - 3)
                    pool.tensor_tensor(rope_r[r][:], rope_a[b][:], rope_b[b][:], ALU.add).then_inc(rope_done, 1)

                def split_qk(i, u, n):
                    pool.wait_ge(qk_copied, n + 1)
                    cols = slice(i * P, (i + 1) * P)
                    pool.tensor_tensor(qk_lo[u][:, :, cols], turned[i % 2][:], qk_hi[u][:, :, cols], ALU.subtract).then_inc(qk_split, 1)

                def step(h, i, u):
                    g = h * NT + i
                    hn, _, _, n = at(h, i + LAG, u)
                    hl, tl, ul, nl = at(h, i + LAG - QLAG, u)
                    h1, t1, _, _ = at(h, i - 1, u)
                    if real(h1):
                        pool.wait_ge(recip_done, g)
                        pool.sem_inc(pool_steps, 1)
                        p = probs[t1 % 4][:, 0:(t1 + 1) * P]
                        pool.tensor_scalar(p, p, rinv[:, t1 % 4:t1 % 4 + 1], 1.0, ALU.mult, ALU.mult).then_inc(norm_done, 1)
                    if real(hl):
                        split_qk(tl, ul, nl)
                    if real(hn):
                        rope_sum(n, (i + LAG) % 2, (i + LAG) % 4)

                for n in range(LAG):
                    if n >= QLAG:
                        split_qk(n - QLAG, 0, n - QLAG)
                    rope_sum(n, n % 2, n % 4)
                steps(pool, step)


def output0(nc, src, outT, wo, gate, x_res):
    with ExitStack() as ctx:
        part = [ctx.enter_context(nc.sbuf_tensor(f"wo_part{i}", [P, D], F32)) for i in range(2)]
        ps = [ctx.enter_context(nc.psum_tensor(f"wo_ps{i}", [P, 512], F32)) for i in range(2)]
        y_ready, gated, added = (nc.alloc_semaphore(n) for n in ("wo_ready", "wo_gated", "wo_added"))
        with nc.Block() as block:

            @block.tensor
            def _(pe):
                for t in range(NT):
                    if t >= 2:
                        pe.wait_ge(gated, t - 1)
                    for h in range(H):
                        mm = pe.matmul(ps[t % 2][:, 0:D], outT[:, h, t * P:(t + 1) * P], wo[:, h, :], start=(h == 0), stop=(h == H - 1))
                    mm.then_inc(y_ready, 1)

            @block.vector
            def _(dve):
                for t in range(NT):
                    dve.wait_ge(y_ready, t + 1)
                    dve.tensor_tensor(part[t % 2][:], ps[t % 2][:, 0:D], gate, ALU.mult).then_inc(gated, 1)
                    dve.wait_ge(gated, t + 1)
                    dve.tensor_tensor(x_res[:, t, :], x_res[:, t, :], part[t % 2][:], ALU.add).then_inc(added, 1)


def route0(nc, src, h, hT, hw_hi, hw_lo, onehot, posT, ident):
    with ExitStack() as ctx:
        def sb(name, shape, dt=F32):
            return ctx.enter_context(nc.sbuf_tensor(name, shape, dt))

        def sem(n):
            return nc.alloc_semaphore("r0_" + n)

        rw = sb("rw", [P, KD, E0])
        ones_b, before_b = sb("ones_b", [P, P], BF16), sb("before_b", [P, P], BF16)
        slot_c = sb("slot_c", [P, C0])
        nmax, total, inv = sb("r_nmax", [P, NT]), sb("r_total", [P, NT]), sb("r_inv", [P, NT])
        shifted, ex, marked = sb("r_shifted", [P, NT, E0]), sb("r_ex", [P, NT, E0]), sb("r_marked", [P, NT, E0])
        top = sb("r_top", [P, NT, K0])
        chosen, chosen_b = sb("r_chosen", [P, NT, E0]), sb("r_chosen_b", [P, NT, E0], BF16)
        off, place = sb("r_off", [P, NT, E0]), sb("r_place", [P, NT, E0])
        wts = sb("r_wts", [P, NT, E0])
        ps = [ctx.enter_context(nc.psum_tensor(f"r_ps{i}", [P, 512], F32)) for i in range(4)]
        loaded, logits_ready, shifted_done, exp_done, step_done, chosen_done, pos_ready, place_done, turned, split_hi = (
            sem(n) for n in ("loaded", "logits_ready", "shifted_done", "exp_done", "step_done", "chosen_done", "pos_ready",
                             "place_done", "turned", "split_hi"))
        logits = ps[0][:].rearrange("p (n e) -> p n e", n=NT)
        pos = ps[1][:].rearrange("p (n e) -> p n e", n=NT)
        with nc.Block() as block:

            @block.sync
            def _(sp):
                sp.dma_start(rw[:], src["router_t"]).then_inc(loaded, 16)
                sp.dma_start(ones_b[:], src["ones_b"]).then_inc(loaded, 16)
                sp.dma_start(before_b[:], src["before_b"]).then_inc(loaded, 16)
                sp.dma_start(slot_c[:], src["slot_c"]).then_inc(loaded, 16)

            @block.tensor
            def _(pe):
                pe.wait_ge(loaded, 64)
                for n in range(NT):
                    for k in range(KD):
                        mm = pe.matmul(logits[:, n, :], hT[:, k, n * P:(n + 1) * P], rw[:, k, :], start=(k == 0), stop=(k == KD - 1))
                mm.then_inc(logits_ready, 1)
                pe.wait_ge(chosen_done, 1)
                for n in range(NT):
                    for m in range(n + 1):
                        mm = pe.matmul(pos[:, n, :], (before_b if m == n else ones_b)[:], chosen_b[:, m, :],
                                       start=(m == 0), stop=(m == n))
                mm.then_inc(pos_ready, 1)
                pe.wait_ge(place_done, 1)
                for n in range(NT):
                    mm = pe.transpose(ps[2 + n // 4][0:E0, (n % 4) * P:(n % 4 + 1) * P], place[:, n, :], ident[:])
                    if n % 4 == 3:
                        mm.then_inc(turned, 1)

            @block.scalar
            def _(act):
                act.wait_ge(shifted_done, 1)
                act.activation(ex[:], shifted[:], ACT.Exp).then_inc(exp_done, 1)
                act.activation(hw_hi[:, :, 0:D], h[:], ACT.Copy).then_inc(split_hi, 1)

            @block.gpsimd
            def _(pool):
                pool.memset(hw_hi[:, :, D + E0:].bitcast(F32), 0.0).then_inc(split_hi, 1)
                pool.memset(hw_lo[:, :, D + E0:].bitcast(F32), 0.0).then_inc(split_hi, 1)
                pool.memset(posT[:], 0.0).then_inc(split_hi, 1)

            @block.vector
            def _(dve):
                done = [0]

                def after(ins):
                    done[0] += 1
                    ins.then_inc(step_done, 1)
                    dve.wait_ge(step_done, done[0])

                dve.wait_ge(logits_ready, 1)
                after(dve.tensor_reduce(nmax[:], logits, AX, ALU.max, negate=True))
                dve.tensor_tensor(shifted[:], logits, nmax[:].unsqueeze(2).to_broadcast([P, NT, E0]), ALU.add).then_inc(shifted_done, 1)
                dve.wait_ge(exp_done, 1)
                for n in range(NT):
                    ins = dve.max(top[:, n, :], ex[:, n, :])
                after(ins)
                for n in range(NT):
                    ins = dve.match_replace(marked[:, n, :], top[:, n, :], ex[:, n, :], -1.0)
                after(ins)
                after(dve.tensor_scalar(chosen[:], marked[:], 0.0, None, ALU.is_lt))
                dve.tensor_copy(chosen_b[:], chosen[:]).then_inc(chosen_done, 1)
                after(dve.tensor_tensor(wts[:], ex[:], chosen[:], ALU.mult))
                after(dve.tensor_reduce(total[:], wts[:], AX, ALU.add))
                after(dve.reciprocal(inv[:], total[:]))
                after(dve.tensor_tensor(wts[:], wts[:], inv[:].unsqueeze(2).to_broadcast([P, NT, E0]), ALU.mult))
                after(dve.tensor_scalar(off[:], chosen[:], -100.0, 100.0, ALU.mult, ALU.add))
                dve.wait_ge(pos_ready, 1)
                after(dve.tensor_tensor(off[:], off[:], pos, ALU.add))
                after(dve.tensor_scalar(place[:], off[:], 200.0, None, ALU.min))
                dve.sem_inc(place_done, 1)
                for n in range(NT):
                    dve.tensor_tensor(onehot[:, n].rearrange("p (e c) -> p e c", c=C0), place[:, n, :].unsqueeze(2).to_broadcast([P, E0, C0]),
                                      slot_c[:].unsqueeze(1).to_broadcast([P, E0, C0]), ALU.is_equal)
                after(dve.tensor_copy(hw_hi[:, :, D:D + E0], wts[:]))
                dve.tensor_tensor(hw_lo[:, :, D:D + E0], wts[:], hw_hi[:, :, D:D + E0], ALU.subtract)
                dve.wait_ge(split_hi, 4)
                dve.tensor_tensor(hw_lo[:, :, 0:D], h[:], hw_hi[:, :, 0:D], ALU.subtract)
                for j in range(2):
                    dve.wait_ge(turned, j + 1)
                    ins = dve.tensor_copy(posT[0:E0, j * 512:(j + 1) * 512], ps[2 + j][0:E0, :])
                after(ins)


def gather0(nc, src, hw_hi, hw_lo, onehot, xgT, wg):
    with ExitStack() as ctx:
        own = ctx.enter_context(nc.sbuf_tensor("own_b", [P, SLOTS], BF16))
        ps = [ctx.enter_context(nc.psum_tensor(f"g_ps{i}", [P, 512], F32)) for i in range(4)]
        own_loaded, g_ready, g_copied = (nc.alloc_semaphore(n) for n in ("own_loaded", "g_ready", "g_copied"))
        groups = [(s, k) for s in range(SLOTS // 512) for k in range(KD + 1)]
        with nc.Block() as block:

            @block.sync
            def _(sp):
                sp.dma_start(own[:], src["own_b"]).then_inc(own_loaded, 16)

            @block.tensor
            def _(pe):
                for q, (s, k) in enumerate(groups):
                    if q >= 4:
                        pe.wait_ge(g_copied, q - 3)
                    for n in range(NT):
                        for part in (hw_hi, hw_lo):
                            mm = pe.matmul(ps[q % 4][:], part[:, n, k * P:(k + 1) * P], onehot[:, n, s * 512:(s + 1) * 512],
                                           start=(n == 0 and part is hw_hi), stop=(n == NT - 1 and part is hw_lo))
                    mm.then_inc(g_ready, 1)

            @block.vector
            def _(dve):
                dve.wait_ge(own_loaded, 16)
                for q, (s, k) in enumerate(groups):
                    dve.wait_ge(g_ready, q + 1)
                    cols = slice(s * 512, (s + 1) * 512)
                    if k < KD:
                        dve.tensor_copy(xgT[:, k, cols], ps[q % 4][:]).then_inc(g_copied, 1)
                    else:
                        dve.tensor_tensor(wg[:, cols], ps[q % 4][:], own[:, cols], ALU.mult).then_inc(g_copied, 1)


def experts0(nc, src, xgT, wg, posT, gate, x_res):
    with ExitStack() as ctx:
        def sb(name, shape, dt=F32):
            return ctx.enter_context(nc.sbuf_tensor(name, shape, dt))

        def sem(n):
            return nc.alloc_semaphore("e0_" + n)

        RING = 4
        w_up = [sb(f"e_up{i}", [P, EPB, 2, KD, F0]) for i in range(RING)]
        w_dn = [sb(f"e_dn{i}", [F0, EPB, D]) for i in range(RING)]
        sel = sb("e_sel", [P, NSB, P], BF16)
        ones = sb("e_ones", [P, F0])
        c_col = sb("e_c", [P, 1])
        sil, act_v, act_w = ([sb(f"e_{n}{i}", [F0, P]) for i in range(2)] for n in ("sil", "av", "aw"))
        y_hi = [sb(f"e_yhi{i}", [P, D], F32R) for i in range(2)]
        y_lo = [sb(f"e_ylo{i}", [P, D], F32R) for i in range(2)]
        back = [sb(f"e_back{i}", [P, T], F32R) for i in range(4)]
        part = [sb(f"e_part{i}", [P, D]) for i in range(2)]
        up_ps = ctx.enter_context(nc.psum_tensor("e_up_ps", [P, 512], F32))
        y_ps = ctx.enter_context(nc.psum_tensor("e_y_ps", [P, 512], F32))
        sel_ps = [ctx.enter_context(nc.psum_tensor(f"e_sel_ps{i}", [P, 512], F32)) for i in range(2)]
        sum_ps = ctx.enter_context(nc.psum_tensor("e_sum_ps", [P, NT // 2, 2, D], F32))
        w_ready = [sem(f"w_ready{i}") for i in range(RING)]
        const_ready, up_ready, sil_done, act_v_done, act_done, y_ready, hi_done, lo_done, sel_ready, back_done, comb_done, gated, added = (
            sem(n) for n in ("const_ready", "up_ready", "sil_done", "act_v_done", "act_done", "y_ready", "hi_done", "lo_done",
                             "sel_ready", "back_done", "comb_done", "gated", "added"))

        def steps(eng, step):
            for u in range(4):
                step(u, u)
            with eng.Fori(1, NSB // 4) as four:
                for u in range(4):
                    step(4 * four + u, u)
            for u in range(2):
                step(NSB + u, u)

        def real(b):
            return not isinstance(b, int) or 0 <= b < NSB

        with nc.Block() as block:

            @block.sync
            def _(sp):
                def load(b, i):
                    wait_pos(sp, y_ready, b - RING + 1)
                    sp.dma_start(w_up[i][:], src["w_up0"][:, bass.ds(b * EPB, EPB)]).then_inc(w_ready[i], 16)
                    sp.dma_start(w_dn[i][:], src["w_dn0"][:, bass.ds(b * EPB, EPB)]).then_inc(w_ready[i], 16)

                sp.dma_start(sel[:], src["sel_b"]).then_inc(const_ready, 16)
                sp.dma_start(ones[:], src["ones_f"]).then_inc(const_ready, 16)
                sp.dma_start(c_col[:], src["c_col"]).then_inc(const_ready, 16)
                for i in range(RING):
                    load(i, i)
                with sp.Fori(1, NSB // 4) as four:
                    for i in range(RING):
                        load(4 * four + i, i)

            @block.tensor
            def _(pe):
                def select(b, half):
                    wait_pos(pe, back_done, 2 * b + half - 1)
                    pe.matmul(sel_ps[half][:], sel[:, b, :], posT[:, half * 512:(half + 1) * 512],
                              start=True, stop=True).then_inc(sel_ready, 1)

                def step(b, u):
                    if real(b):
                        pe.wait_ge(w_ready[u], 8 * b - 8 * u + 32)
                        wait_pos(pe, act_done, b)
                        for e in range(EPB):
                            for a in range(2):
                                for k in range(KD):
                                    pe.matmul(up_ps[0:F0, a * P + e * C0:a * P + (e + 1) * C0], w_up[u][:, e, a, k, :],
                                              xgT[:, k, bass.ds(b * P + e * C0, C0)],
                                              start=(e == 0 and a == 0 and k == 0), stop=(k == KD - 1), skip_group_check=True)
                        pe.matmul(up_ps[0:F0, 2 * P:3 * P], ones[:], wg[:, bass.ds(b * P, P)], start=False, stop=True,
                                  skip_group_check=True).then_inc(up_ready, 1)
                        select(b, 0)
                        select(b, 1)
                    if real(b - 1):
                        pe.wait_ge(act_done, b)
                        wait_pos(pe, lo_done, b - 1)
                        for e in range(EPB):
                            mm = pe.matmul(y_ps[e * C0:(e + 1) * C0, 0:D], act_w[(u - 1) % 2][:, e * C0:(e + 1) * C0],
                                           w_dn[(u - 1) % 4][:, e, :], start=True, stop=True)
                        mm.then_inc(y_ready, 1)
                    if real(b - 2):
                        pe.wait_ge(lo_done, b - 1)
                        pe.wait_ge(back_done, 2 * b - 2)
                        for t in range(NT):
                            for y in (y_hi, y_lo):
                                first = isinstance(b, int) and b == 2 and t % 2 == 0 and y is y_hi
                                mm = pe.matmul(sum_ps[:, t // 2, t % 2, :], back[(u - 2) % 4][:, t * P:(t + 1) * P], y[(u - 2) % 2][:],
                                               start=first, stop=(isinstance(b, int) and b == NSB + 1 and y is y_lo),
                                               skip_group_check=True)
                        mm.then_inc(comb_done, 1)

                pe.wait_ge(const_ready, 48)
                steps(pe, step)

            @block.scalar
            def _(act):
                def step(b, u):
                    if real(b):
                        act.wait_ge(up_ready, b + 1)
                        wait_pos(act, act_v_done, b - 1)
                        act.activation(sil[u % 2][:], up_ps[0:F0, 0:P], ACT.Silu).then_inc(sil_done, 1)
                    if real(b - 1):
                        act.wait_ge(y_ready, b)
                        wait_pos(act, comb_done, b - 2)
                        act.activation(y_hi[(u - 1) % 2][:], y_ps[:, 0:D], ACT.Copy).then_inc(hi_done, 1)

                steps(act, step)

            @block.vector
            def _(dve):
                def step(b, u):
                    if real(b):
                        dve.wait_ge(sil_done, b + 1)
                        dve.tensor_tensor(act_v[u % 2][:], sil[u % 2][:], up_ps[0:F0, P:2 * P], ALU.mult).then_inc(act_v_done, 1)
                        dve.wait_ge(act_v_done, b + 1)
                        wait_pos(dve, y_ready, b - 1)
                        dve.tensor_tensor(act_w[u % 2][:], act_v[u % 2][:], up_ps[0:F0, 2 * P:3 * P], ALU.mult).then_inc(act_done, 1)
                        for half in range(2):
                            dve.wait_ge(sel_ready, 2 * b + half + 1)
                            wait_pos(dve, comb_done, b - 3)
                            dve.tensor_scalar(back[u][:, half * 512:(half + 1) * 512], sel_ps[half][:], c_col[:], None,
                                              ALU.is_equal).then_inc(back_done, 1)
                    if real(b - 1):
                        dve.wait_ge(hi_done, b)
                        dve.tensor_tensor(y_lo[(u - 1) % 2][:], y_ps[:, 0:D], y_hi[(u - 1) % 2][:], ALU.subtract).then_inc(lo_done, 1)

                dve.wait_ge(const_ready, 48)
                steps(dve, step)
                dve.wait_ge(comb_done, NSB)
                for t in range(NT):
                    dve.tensor_tensor(part[t % 2][:], sum_ps[:, t // 2, t % 2, :], gate, ALU.mult).then_inc(gated, 1)
                    dve.wait_ge(gated, t + 1)
                    dve.tensor_tensor(x_res[:, t, :], x_res[:, t, :], part[t % 2][:], ALU.add).then_inc(added, 1)


def project1(nc, src, hT, qT, kT, value, catT, bias, mask_b):
    LOC, VAL, PRE = 2 * QK1, 2 * QK1 + EXP1 - D, EXP1
    with ExitStack() as ctx:
        def sb(name, shape, dt=F32):
            return ctx.enter_context(nc.sbuf_tensor(name, shape, dt))

        def sem(n):
            return nc.alloc_semaphore("p1_" + n)

        w = sb("expand", [P, KD, 2 * QK1 + 2 * EXP1])
        gate_v = [sb(f"gate_v{i}", [P, D]) for i in range(2)]
        gate_l = [sb(f"gate_l{i}", [P, 512]) for i in range(2)]
        pm, pos_e, pos_l, pos_s = sb("pm", [P, 1]), sb("pos_e", [P, 2]), sb("pos_l", [P, 1]), sb("pos_s", [P, 2])
        ps = [ctx.enter_context(nc.psum_tensor(f"p1_ps{i}", [P, 512], F32)) for i in range(8)]
        w_loaded, pos_loaded, pos_abs, pos_ln, pos_step = (sem(n) for n in ("w_loaded", "pos_loaded", "pos_abs", "pos_ln", "pos_step"))
        qk_ready, qk_copied, v_ready, v_gate, v_done, l_ready, l_gate, l_done = (
            sem(n) for n in ("qk_ready", "qk_copied", "v_ready", "v_gate", "v_done", "l_ready", "l_gate", "l_done"))
        with nc.Block() as block:

            @block.sync
            def _(sp):
                sp.dma_start(w[:], src["expand_t"]).then_inc(w_loaded, 16)
                sp.dma_start(pm[:], src["pos_mult"].to_broadcast([P, 1])).then_inc(pos_loaded, 16)
                sp.dma_start(bias[:], src["rel"]).then_inc(pos_loaded, 16)

            @block.tensor
            def _(pe):
                pe.wait_ge(w_loaded, 16)

                def product(out, lhs, rhs):
                    for k in range(KD):
                        mm = pe.matmul(out, lhs(k), rhs(k), start=(k == 0), stop=(k == KD - 1))
                    return mm

                for j in range(2):
                    for c in range(2):
                        product(ps[2 * j + c][0:QK1, :], lambda k: w[:, k, j * QK1:(j + 1) * QK1],
                                lambda k: hT[:, k, c * 512:(c + 1) * 512]).then_inc(qk_ready, 1)
                for t in range(NT):
                    if t >= 2:
                        pe.wait_ge(v_done, t - 1)
                    for g in range(2):
                        mm = product(ps[4 + t % 2][:, g * D:(g + 1) * D], lambda k: hT[:, k, t * P:(t + 1) * P],
                                     lambda k: w[:, k, VAL + g * PRE:VAL + g * PRE + D])
                    mm.then_inc(v_ready, 1)
                for q in range(4):
                    c, half = q // 2, q % 2
                    pe.wait_ge(qk_copied, 4)
                    if q >= 2:
                        pe.wait_ge(l_done, q - 1)
                    for g in range(2):
                        mm = product(ps[2 * (q % 2) + g][:], lambda k: w[:, k, LOC + g * PRE + c * P:LOC + g * PRE + (c + 1) * P],
                                     lambda k: hT[:, k, half * 512:(half + 1) * 512])
                    mm.then_inc(l_ready, 1)

            @block.scalar
            def _(act):
                act.wait_ge(pos_abs, 1)
                act.activation(pos_e[:, 1:2], pos_e[:, 0:1], ACT.Exp).then_inc(pos_ln, 1)
                act.wait_ge(pos_ln, 1)
                act.activation(pos_l[:], pos_e[:, 1:2], ACT.Ln, bias=1.0).then_inc(pos_ln, 1)
                for t in range(NT):
                    act.wait_ge(v_ready, t + 1)
                    if t >= 2:
                        act.wait_ge(v_done, t - 1)
                    act.activation(gate_v[t % 2][:], ps[4 + t % 2][:, D:2 * D], ACT.Gelu).then_inc(v_gate, 1)
                for q in range(4):
                    act.wait_ge(l_ready, q + 1)
                    if q >= 2:
                        act.wait_ge(l_done, q - 1)
                    act.activation(gate_l[q % 2][:], ps[2 * (q % 2) + 1][:], ACT.Gelu).then_inc(l_gate, 1)

            @block.vector
            def _(dve):
                dve.wait_ge(pos_loaded, 32)
                dve.scalar_tensor_tensor(pos_e[:, 0:1], pm[:], -1.0, pm[:], ALU.mult, ALU.min).then_inc(pos_abs, 1)
                dve.tensor_scalar(pos_s[:, 0:1], pm[:], 0.0, None, ALU.max).then_inc(pos_step, 1)
                dve.wait_ge(pos_step, 1)
                dve.wait_ge(pos_ln, 2)
                dve.tensor_tensor(pos_s[:, 1:2], pos_s[:, 0:1], pos_l[:], ALU.add).then_inc(pos_step, 1)
                for j in range(2):
                    for c in range(2):
                        dve.wait_ge(qk_ready, 2 * j + c + 1)
                        dve.tensor_scalar((kT if j else qT)[:, c * 512:(c + 1) * 512], ps[2 * j + c][0:QK1, :],
                                          1.0 if j else QK1 ** -0.5, None, ALU.mult).then_inc(qk_copied, 1)
                dve.wait_ge(pos_step, 2)
                dve.tensor_scalar(bias[:], bias[:], pos_s[:, 1:2], None, ALU.mult).then_inc(pos_step, 1)
                dve.wait_ge(pos_step, 3)
                dve.tensor_tensor(bias[:, T - P:T], bias[:, T - P:T], mask_b[:], ALU.add).then_inc(pos_step, 1)
                for t in range(NT):
                    dve.wait_ge(v_gate, t + 1)
                    dve.tensor_tensor(value[:, t, :], gate_v[t % 2][:], ps[4 + t % 2][:, 0:D], ALU.mult).then_inc(v_done, 1)
                for q in range(4):
                    c, half = q // 2, q % 2
                    dve.wait_ge(l_gate, q + 1)
                    dve.tensor_tensor(catT[:, c, half * 512:(half + 1) * 512], gate_l[q % 2][:], ps[2 * (q % 2)][:],
                                      ALU.mult).then_inc(l_done, 1)


def attend1(nc, src, qT, kT, value, catT, bias, hm, gate, x_res, ident):
    with ExitStack() as ctx:
        def sb(name, shape, dt=F32):
            return ctx.enter_context(nc.sbuf_tensor(name, shape, dt))

        def sem(n):
            return nc.alloc_semaphore("a1_" + n)

        proj = sb("proj1", [P, 4, D])
        s_sb = [sb(f"s1_{i}", [P, T]) for i in range(2)]
        probs = [sb(f"probs1_{i}", [P, T]) for i in range(3)]
        probsT = [sb(f"probs1T{i}", [P, NT, P]) for i in range(2)]
        nmax, rowsum, rinv = sb("nmax1", [P, NT]), sb("rowsum1", [P, NT]), sb("rinv1", [P, NT])
        part = [sb(f"part1_{i}", [P, 2, D]) for i in range(2)]
        s_ps = [ctx.enter_context(nc.psum_tensor(f"s1_ps{b}", [P, 2, 512], F32)) for b in range(2)]
        t_ps = [ctx.enter_context(nc.psum_tensor(f"t1_ps{b}", [P, 512], F32)) for b in range(2)]
        o_ps = ctx.enter_context(nc.psum_tensor("o1_ps", [P, 512], F32))
        y_ps = ctx.enter_context(nc.psum_tensor("y1_ps", [P, 512], F32))
        w_loaded, s_ready, biased, max_done, exp_done, recip_done, norm_done, pv_done, o_copied, y_ready, y_step, added = (
            sem(n) for n in ("w_loaded", "s_ready", "biased", "max_done", "exp_done", "recip_done", "norm_done", "pv_done",
                             "o_copied", "y_ready", "y_step", "added"))
        t_ready = [sem("t_ready0"), sem("t_ready1")]
        t_copied = [sem("t_copied0"), sem("t_copied1")]
        parts = [[(0, 0, (i + 1) * P)] if i < 4 else [(0, 0, (i + 1) * P // 2), (1, (i + 1) * P // 2, (i + 1) * P)] for i in range(NT)]

        def view(slot, i):
            return s_ps[slot][:, 0:len(parts[i]), 0:parts[i][0][2]]

        def halves(ap, i):
            return ap.rearrange("p (a c) -> p a c", a=len(parts[i]))

        with nc.Block() as block:

            @block.sync
            def _(sp):
                sp.dma_start(proj[:], src["project_t"]).then_inc(w_loaded, 16)

            @block.tensor
            def _(pe):
                for i in range(NT + 3):
                    if i < NT:
                        if i >= 2:
                            pe.wait_ge(biased, i - 1)
                        for bank, lo, hi in parts[i]:
                            mm = pe.matmul(s_ps[i % 2][:, bank, 0:hi - lo], qT[:, i * P:(i + 1) * P], kT[:, lo:hi], start=True, stop=True)
                        mm.then_inc(s_ready, 1)
                    p = i - 2
                    if 0 <= p < NT:
                        pe.wait_ge(norm_done, p + 1)
                        for j in range(p // 4 + 1):
                            wait_pos(pe, t_copied[j], p if j == 0 else p - 4)
                            for kb in range(4 * j, min(4 * j + 4, p + 1)):
                                mm = pe.transpose(t_ps[j][:, (kb % 4) * P:(kb % 4 + 1) * P], probs[p % 3][:, kb * P:(kb + 1) * P], ident[:])
                            mm.then_inc(t_ready[j], 1)
                    y = i - 3
                    if 0 <= y < NT:
                        pe.wait_ge(w_loaded, 16)
                        pe.wait_ge(o_copied, y + 1)
                        wait_pos(pe, y_step, 2 * y - 1)
                        for c in range(4):
                            mm = pe.matmul(y_ps[:, 0:D], catT[:, c, y * P:(y + 1) * P], proj[:, c, :], start=(c == 0), stop=(c == 3))
                        mm.then_inc(y_ready, 1)
                    if 0 <= p < NT:
                        pe.wait_ge(t_copied[0], p + 1)
                        if p >= 4:
                            pe.wait_ge(t_copied[1], p - 3)
                        wait_pos(pe, o_copied, p)
                        for v in range(2):
                            for kb in range(p + 1):
                                mm = pe.matmul(o_ps[:, v * P:(v + 1) * P], value[:, kb, v * P:(v + 1) * P], probsT[p % 2][:, kb, :],
                                               start=(kb == 0), stop=(kb == p))
                        mm.then_inc(pv_done, 1)

            @block.vector
            def _(dve):
                for i in range(NT + 3):
                    if i < NT:
                        dve.wait_ge(s_ready, i + 1)
                        wait_pos(dve, exp_done, i - 1)
                        off = (NT - 1 - i) * P
                        dve.tensor_tensor(halves(s_sb[i % 2][:, 0:(i + 1) * P], i), view(i % 2, i),
                                          halves(bias[:, off:off + (i + 1) * P], i), ALU.add).then_inc(biased, 1)
                        dve.wait_ge(biased, i + 1)
                        dve.tensor_reduce(nmax[:, i:i + 1], s_sb[i % 2][:, 0:(i + 1) * P], AX, ALU.max, negate=True).then_inc(max_done, 1)
                    p = i - 2
                    if 0 <= p < NT:
                        dve.wait_ge(t_ready[0], p + 1)
                        wait_pos(dve, pv_done, p - 1)
                        n = min(p + 1, 4)
                        dve.tensor_copy(probsT[p % 2][:, 0:n, :], t_ps[0][:, 0:n * P].rearrange("p (a c) -> p a c", a=n))\
                           .then_inc(t_copied[0], 1)
                    if i < NT:
                        dve.wait_ge(exp_done, i + 1)
                        dve.reciprocal(rinv[:, i:i + 1], rowsum[:, i:i + 1]).then_inc(recip_done, 1)
                    y = i - 3
                    if 0 <= y < NT:
                        dve.wait_ge(y_ready, y + 1)
                        dve.tensor_tensor(part[y % 2][:, 0, :], y_ps[:, 0:D], hm[:, y, :], ALU.add).then_inc(y_step, 1)
                        dve.wait_ge(y_step, 2 * y + 1)
                        dve.tensor_tensor(part[y % 2][:, 1, :], part[y % 2][:, 0, :], gate, ALU.mult).then_inc(y_step, 1)
                        dve.wait_ge(y_step, 2 * y + 2)
                        dve.tensor_tensor(x_res[:, y, :], x_res[:, y, :], part[y % 2][:, 1, :], ALU.add).then_inc(added, 1)
                    if 0 <= p < NT:
                        dve.wait_ge(pv_done, p + 1)
                        dve.tensor_copy(catT[:, 2:4, p * P:(p + 1) * P], o_ps[:, 0:2 * P].rearrange("p (a c) -> p a c", a=2))\
                           .then_inc(o_copied, 1)

            @block.scalar
            def _(act):
                for i in range(NT + 2):
                    if i < NT:
                        act.wait_ge(max_done, i + 1)
                        act.activation(probs[i % 3][:, 0:(i + 1) * P], s_sb[i % 2][:, 0:(i + 1) * P], ACT.Exp, bias=nmax[:, i:i + 1],
                                       accum_out=rowsum[:, i:i + 1]).then_inc(exp_done, 1)
                    p = i - 2
                    if p >= 4:
                        act.wait_ge(t_ready[1], p - 3)
                        wait_pos(act, pv_done, p - 1)
                        n = p - 3
                        act.activation(probsT[p % 2][:, 4:4 + n, :], t_ps[1][:, 0:n * P].rearrange("p (a c) -> p a c", a=n),
                                       ACT.Copy).then_inc(t_copied[1], 1)

            @block.gpsimd
            def _(pool):
                for i in range(NT):
                    pool.wait_ge(recip_done, i + 1)
                    p = probs[i % 3][:, 0:(i + 1) * P]
                    pool.tensor_scalar(p, p, rinv[:, i:i + 1], 1.0, ALU.mult, ALU.mult).then_inc(norm_done, 1)


NE1 = E1 + 2
HI1 = I1 // 2


def route1(nc, src, hT, comb, h_hi, h_lo):
    with ExitStack() as ctx:
        def sb(name, shape, dt=F32):
            return ctx.enter_context(nc.sbuf_tensor(name, shape, dt))

        rw = sb("rw1", [P, KD, E1])
        one_t = sb("one_t", [P, E1])
        nmax, total, inv, best2, above_n, wsum = (sb(f"r1_{n}", [P, NT]) for n in ("nmax", "total", "inv", "second", "above_n", "wsum"))
        shifted, prob, above, equal, rank, ok, wts = (sb(f"r1_{n}", [P, NT, E1]) for n in
                                                      ("shifted", "prob", "above", "equal", "rank", "ok", "wts"))
        top = sb("r1_top", [P, NT, 8])
        ps = ctx.enter_context(nc.psum_tensor("r1_ps", [P, 512], F32))
        loaded, logits_ready, shifted_done, exp_done, step_done, split_done = (
            nc.alloc_semaphore("r1_" + n) for n in ("loaded", "logits_ready", "shifted_done", "exp_done", "step_done", "split_done"))
        logits = ps[:, 0:NT * E1].rearrange("p (n e) -> p n e", n=NT)

        def wide(col):
            return col.unsqueeze(2).to_broadcast([P, NT, E1])

        with nc.Block() as block:

            @block.sync
            def _(sp):
                sp.dma_start(rw[:], src["gate_t"]).then_inc(loaded, 16)

            @block.tensor
            def _(pe):
                pe.wait_ge(loaded, 16)
                for n in range(NT):
                    for k in range(KD):
                        mm = pe.matmul(logits[:, n, :], hT[:, k, n * P:(n + 1) * P], rw[:, k, :], start=(k == 0), stop=(k == KD - 1))
                mm.then_inc(logits_ready, 1)

            @block.scalar
            def _(act):
                act.activation(h_hi[:], hT[:], ACT.Copy).then_inc(split_done, 1)
                act.wait_ge(shifted_done, 1)
                act.activation(prob[:], shifted[:], ACT.Exp).then_inc(exp_done, 1)

            @block.vector
            def _(dve):
                done = [0]

                def after(ins):
                    done[0] += 1
                    ins.then_inc(step_done, 1)
                    dve.wait_ge(step_done, done[0])

                after(dve.memset(one_t[:], 1.0))
                after(dve.memset(comb[:], 1.0))
                dve.wait_ge(logits_ready, 1)
                after(dve.tensor_reduce(nmax[:], logits, AX, ALU.max, negate=True))
                dve.tensor_tensor(shifted[:], logits, wide(nmax[:]), ALU.add).then_inc(shifted_done, 1)
                dve.wait_ge(exp_done, 1)
                after(dve.tensor_reduce(total[:], prob[:], AX, ALU.add))
                after(dve.reciprocal(inv[:], total[:]))
                after(dve.tensor_tensor(prob[:], prob[:], wide(inv[:]), ALU.mult))
                for n in range(NT):
                    ins = dve.max(top[:, n, :], prob[:, n, :])
                after(ins)
                after(dve.tensor_copy(best2[:], top[:, :, K1 - 1]))
                dve.tensor_tensor(above[:], prob[:], wide(best2[:]), ALU.is_gt)
                after(dve.tensor_tensor(equal[:], prob[:], wide(best2[:]), ALU.is_equal))
                dve.tensor_reduce(above_n[:], above[:], AX, ALU.add)
                for n in range(NT):
                    ins = dve.tensor_tensor_scan(rank[:, n, :], one_t[:], equal[:, n, :], 0.0, ALU.mult, ALU.add)
                after(ins)
                after(dve.tensor_tensor(rank[:], rank[:], wide(above_n[:]), ALU.add))
                after(dve.scalar_tensor_tensor(ok[:], rank[:], float(K1), equal[:], ALU.is_le, ALU.mult))
                after(dve.tensor_tensor(ok[:], ok[:], above[:], ALU.add))
                after(dve.tensor_tensor(wts[:], prob[:], ok[:], ALU.mult))
                after(dve.tensor_reduce(wsum[:], wts[:], AX, ALU.add))
                after(dve.tensor_scalar(wsum[:], wsum[:], 1e-20, None, ALU.add))
                after(dve.reciprocal(inv[:], wsum[:]))
                after(dve.tensor_tensor(comb[:, :, 0:E1], wts[:], wide(inv[:]), ALU.mult))
                dve.wait_ge(split_done, 1)
                after(dve.tensor_tensor(h_lo[:], hT[:], h_hi[:], ALU.subtract))


def experts1(nc, src, h_hi, h_lo, comb, gate, x_res):
    with ExitStack() as ctx:
        def sb(name, shape, dt=F32):
            return ctx.enter_context(nc.sbuf_tensor(name, shape, dt))

        def sem(n):
            return nc.alloc_semaphore("e1_" + n)

        wu = [sb(f"wu{i}", [P, KD, 2 * I1]) for i in range(2)]
        wd = [sb(f"wd{i}", [HI1, 2, D]) for i in range(2)]
        wu_hi, wu_lo = ([sb(f"wu_{n}{i}", [P, KD, 2 * I1], F32R) for i in range(2)] for n in ("hi", "lo"))
        wd_hi, wd_lo = ([sb(f"wd_{n}{i}", [HI1, 2, D], F32R) for i in range(2)] for n in ("hi", "lo"))
        sil = [sb(f"sil{i}", [HI1, 512]) for i in range(2)]
        prod = [sb(f"prod{i}", [HI1, 512]) for i in range(2)]
        a_hi, a_lo = ([sb(f"a_{n}{i}", [HI1, 2, T], F32R) for i in range(2)] for n in ("hi", "lo"))
        acc = sb("acc", [P, NT, D])
        up_ps = [ctx.enter_context(nc.psum_tensor(f"up1_ps{i}", [P, 2, 512], F32)) for i in range(2)]
        dn_ps = [ctx.enter_context(nc.psum_tensor(f"dn1_ps{i}", [P, 512], F32)) for i in range(4)]
        w_ready = [sem("w_ready0"), sem("w_ready1")]
        up_hi, dn_hi, up_split, dn_split, up_ready, sil_done, prod_done, hi_done, lo_done, dn_ready, summed, last_step = (
            sem(n) for n in ("up_hi", "dn_hi", "up_split", "dn_split", "up_ready", "sil_done", "prod_done", "hi_done", "lo_done", "dn_ready", "summed", "last_step"))
        acc_zero, pool_steps = sem("acc_zero"), sem("pool_steps")
        UNITS = [(c, half) for c in range(2) for half in range(2)]

        def steps(eng, step):
            step(0, 0)
            step(1, 1)
            with eng.Fori(1, NE1 // 2) as pair:
                for b in range(2):
                    step(2 * pair + b, b)
            step(NE1, 0)

        def real(e):
            return not isinstance(e, int) or 0 <= e < NE1

        with nc.Block() as block:

            @block.sync
            def _(sp):
                def load(e, b):
                    wait_pos(sp, up_split, e - 1)
                    sp.dma_start(wu[b][:], src["w_up1"][:, bass.ds(e, 1)].rearrange("p a k i -> p (a k) i")).then_inc(w_ready[b], 16)
                    wait_pos(sp, dn_split, e - 1)
                    sp.dma_start(wd[b][:], src["w_dn1"][:, bass.ds(e, 1)].rearrange("p a c d -> p (a c) d")).then_inc(w_ready[b], 16)

                load(0, 0)
                load(1, 1)
                with sp.Fori(1, NE1 // 2) as pair:
                    for b in range(2):
                        load(2 * pair + b, b)

            @block.gpsimd
            def _(pool):
                def step(e, b):
                    if real(e):
                        pool.wait_ge(w_ready[b], 16 * e - 16 * b + 32)
                        wait_pos(pool, up_ready, 4 * (e - 1))
                        pool.sem_inc(pool_steps, 1)
                        pool.tensor_copy(wu_hi[b][:], wu[b][:]).then_inc(up_hi, 1)
                        pool.wait_ge(up_hi, e + 1)
                        pool.tensor_tensor(wu_lo[b][:], wu[b][:], wu_hi[b][:], ALU.subtract).then_inc(up_split, 1)
                    if real(e - 1):
                        if not isinstance(e, int) or e > 2:
                            pool.wait_ge(dn_ready, NT * (e - 2))
                            pool.sem_inc(pool_steps, 1)
                        pool.tensor_copy(wd_hi[1 - b][:], wd[1 - b][:]).then_inc(dn_hi, 1)
                        pool.wait_ge(dn_hi, e)
                        pool.tensor_tensor(wd_lo[1 - b][:], wd[1 - b][:], wd_hi[1 - b][:], ALU.subtract).then_inc(dn_split, 1)

                steps(pool, step)

            @block.tensor
            def _(pe):
                def step(e, b):
                    if real(e):
                        pe.wait_ge(up_split, e + 1)
                        for q, (c, half) in enumerate(UNITS):
                            wait_pos(pe, prod_done, 4 * e + q - 1)
                            for g in range(2):
                                cols = slice(g * I1 + c * HI1, g * I1 + (c + 1) * HI1)
                                for k in range(KD):
                                    for n, (w, h) in enumerate(((wu_hi, h_hi), (wu_lo, h_hi), (wu_hi, h_lo))):
                                        mm = pe.matmul(up_ps[q % 2][0:HI1, g, :], w[b][:, k, cols], h[:, k, half * 512:(half + 1) * 512],
                                                       start=(k == 0 and n == 0), stop=(k == KD - 1 and n == 2))
                            mm.then_inc(up_ready, 1)
                    if real(e - 1):
                        pe.wait_ge(dn_split, e)
                        for t in range(NT):
                            if t % 4 == 0:
                                pe.wait_ge(lo_done, 4 * e - 1 + t // 4)
                            wait_pos(pe, summed, NT * (e - 1) + t - 3)
                            for c in range(2):
                                for n, (a, w) in enumerate(((a_hi, wd_hi), (a_hi, wd_lo), (a_lo, wd_hi))):
                                    mm = pe.matmul(dn_ps[t % 4][:, 0:D], a[1 - b][:, c, t * P:(t + 1) * P], w[1 - b][:, c, :],
                                                   start=(c == 0 and n == 0), stop=(c == 1 and n == 2))
                            mm.then_inc(dn_ready, 1)

                steps(pe, step)

            @block.scalar
            def _(act):
                def step(e, b):
                    if not real(e):
                        return
                    for q in range(5):
                        if q < 4:
                            act.wait_ge(up_ready, 4 * e + q + 1)
                            wait_pos(act, prod_done, 4 * e + q - 1)
                            act.activation(sil[q % 2][:], up_ps[q % 2][0:HI1, 0, :], ACT.Silu).then_inc(sil_done, 1)
                        if q >= 1:
                            c, half = UNITS[q - 1]
                            act.wait_ge(prod_done, 4 * e + q)
                            wait_pos(act, dn_ready, NT * (e - 1))
                            act.activation(a_hi[b][:, c, half * 512:(half + 1) * 512], prod[(q - 1) % 2][:], ACT.Copy).then_inc(hi_done, 1)

                steps(act, step)

            @block.vector
            def _(dve):
                def step(e, b):
                    if real(e):
                        for q in range(5):
                            if q < 4:
                                dve.wait_ge(sil_done, 4 * e + q + 1)
                                wait_pos(dve, lo_done, 4 * e + q - 1)
                                dve.tensor_tensor(prod[q % 2][:], sil[q % 2][:], up_ps[q % 2][0:HI1, 1, :], ALU.mult).then_inc(prod_done, 1)
                            if q >= 1:
                                c, half = UNITS[q - 1]
                                dve.wait_ge(hi_done, 4 * e + q)
                                cols = slice(half * 512, (half + 1) * 512)
                                dve.tensor_tensor(a_lo[b][:, c, cols], prod[(q - 1) % 2][:], a_hi[b][:, c, cols], ALU.subtract)\
                                   .then_inc(lo_done, 1)
                    if real(e - 1):
                        for t in range(NT):
                            dve.wait_ge(dn_ready, NT * (e - 1) + t + 1)
                            wait_pos(dve, summed, NT * (e - 2) + t + 1)
                            w = comb[:, t, e - 1:e] if isinstance(e, int) else comb[:, t, bass.ds(e - 1, 1)]
                            dve.scalar_tensor_tensor(acc[:, t, :], dn_ps[t % 4][:, 0:D], w, acc[:, t, :], ALU.mult, ALU.add).then_inc(summed, 1)

                dve.memset(acc[:], 0.0).then_inc(acc_zero, 1)
                dve.wait_ge(acc_zero, 1)
                steps(dve, step)
                for t in range(NT):
                    dve.wait_ge(summed, NT * (NE1 - 1) + t + 1)
                    dve.tensor_tensor(acc[:, t, :], acc[:, t, :], gate, ALU.mult).then_inc(last_step, 1)
                dve.wait_ge(last_step, NT)
                dve.tensor_tensor(x_res[:], x_res[:], acc[:], ALU.add).then_inc(last_step, 1)


def rest(nc, src, norm_sems, x_res, row, ident, ident_b, mask_b, eps_col, stop):
    with ExitStack() as ctx:
        def sb(name, shape, dt=F32):
            return ctx.enter_context(nc.sbuf_tensor(name, shape, dt))

        posT, xgT, wg = sb("posT", [P, T], BF16), sb("xgT", [P, KD, SLOTS]), sb("wg", [P, SLOTS])
        with ExitStack() as inner:
            onehot = inner.enter_context(nc.sbuf_tensor("onehot", [P, NT, SLOTS], F32R))
            hw_hi = inner.enter_context(nc.sbuf_tensor("hw_hi", [P, NT, D + P], F32R))
            hw_lo = inner.enter_context(nc.sbuf_tensor("hw_lo", [P, NT, D + P], F32R))
            with ExitStack() as routing:
                h = routing.enter_context(nc.sbuf_tensor("h1", [P, NT, D], F32))
                hT = routing.enter_context(nc.sbuf_tensor("h1T", [P, KD, T], F32))
                norm_tiles(nc, "ln1", norm_sems, x_res, row(0, 4), row(0, 3), h, hT, ident, eps_col)
                route0(nc, src, h, hT, hw_hi, hw_lo, onehot, posT, ident)
            gather0(nc, src, hw_hi, hw_lo, onehot, xgT, wg)
        experts0(nc, src, xgT, wg, posT, row(0, 5), x_res)
    if stop < 3:
        return
    with ExitStack() as ctx:
        def sb(name, shape, dt=F32):
            return ctx.enter_context(nc.sbuf_tensor(name, shape, dt))

        rows = sb("ln_rows", [P, 2, D])
        hm, h, hT = sb("hm", [P, NT, D]), sb("h2", [P, NT, D]), sb("h2T", [P, KD, T])
        qT, kT, value, catT = sb("q1T", [QK1, T]), sb("k1T", [QK1, T]), sb("value", [P, NT, D]), sb("catT", [P, 4, T])
        bias = sb("bias", [P, T])
        rows_loaded = nc.alloc_semaphore("rows_loaded")
        with nc.Block() as block:

            @block.sync
            def _(sp):
                sp.dma_start(rows[:, 0, :], src["ln_gamma"].to_broadcast([P, D])).then_inc(rows_loaded, 16)
                sp.dma_start(rows[:, 1, :], src["ln_beta"].to_broadcast([P, D])).then_inc(rows_loaded, 16)
                sp.wait_ge(rows_loaded, 32)

        norm_tiles(nc, "ln2", norm_sems, x_res, row(1, 1), row(1, 0), hm, None, ident, eps_col)
        norm_tiles(nc, "ln3", norm_sems, hm, rows[:, 0, :], rows[:, 1, :], h, hT, ident, eps_col)
        project1(nc, src, hT, qT, kT, value, catT, bias, mask_b)
        attend1(nc, src, qT, kT, value, catT, bias, hm, row(1, 2), x_res, ident)
    if stop < 4:
        return
    with ExitStack() as ctx:
        def sb(name, shape, dt=F32):
            return ctx.enter_context(nc.sbuf_tensor(name, shape, dt))

        h_hi, h_lo, comb = sb("h3_hi", [P, KD, T], F32R), sb("h3_lo", [P, KD, T], F32R), sb("comb", [P, NT, NE1])
        with nc.sbuf_tensor("h3", [P, NT, D], F32) as h, nc.sbuf_tensor("h3T", [P, KD, T], F32) as hT:
            norm_tiles(nc, "ln4", norm_sems, x_res, row(1, 4), row(1, 3), h, hT, ident, eps_col)
            route1(nc, src, hT, comb, h_hi, h_lo)
        experts1(nc, src, h_hi, h_lo, comb, row(1, 5), x_res)


def store(nc, x, out):
    with nc.semaphore("stored") as stored, nc.Block() as block:

        @block.sync
        def _(sp):
            sp.dma_start(out.rearrange("o (n p) d -> p (o n) d", p=P), x[:]).then_inc(stored, 16)
            sp.wait_ge(stored, 16)


def build(nc, src, out, stop=99):
    with ExitStack() as ctx:
        def sb(name, shape, dt=F32):
            return ctx.enter_context(nc.sbuf_tensor(name, shape, dt))

        x_res = sb("x_res", [P, NT, D])
        modv = sb("modv", [P, 2, 6 * D])
        ident, ident_b = sb("ident", [P, P]), sb("ident_b", [P, P], BF16)
        mask_b = sb("mask_b", [P, P], BF16)
        eps_col = sb("eps_col", [P, 1])
        x_loaded = nc.alloc_semaphore("x_loaded")
        norm_sems = NormSems(nc)

        def row(l, j):
            return modv[:, l, j * D:(j + 1) * D]

        consts = [(ident[:], "ident"), (ident_b[:], "ident_b"), (mask_b[:], "mask_b"), (eps_col[:], "eps")]
        with ExitStack() as inner:
            outT = inner.enter_context(nc.sbuf_tensor("outT", [P, H, T], F32))
            wo = inner.enter_context(nc.sbuf_tensor("wo", [P, H, D], F32))
            late_loaded = nc.alloc_semaphore("late_loaded")
            with ExitStack() as first:
                rope = first.enter_context(nc.sbuf_tensor("rope", [P, 2, NT, 2, DH], F32))
                w_down = first.enter_context(nc.sbuf_tensor("w_down", [P, KD, P], F32))
                hT = first.enter_context(nc.sbuf_tensor("hT", [P, KD, T], F32))
                ckvT = first.enter_context(nc.sbuf_tensor("ckvT", [P, T], F32))
                ckv = first.enter_context(nc.sbuf_tensor("ckv", [P, NT, P], F32))
                with nc.sbuf_tensor("wv_t", [P, H, P], F32) as wv_t:
                    modulation(nc, sb, src, consts + [(rope[:], "rope"), (w_down[:], "w_down_p")],
                               [(wo[:], "wo_p"), (wv_t[:], "wv_t")], late_loaded, modv, x_res, x_loaded)
                    with nc.sbuf_tensor("h0", [P, NT, D], F32) as h:
                        norm_tiles(nc, "ln0", norm_sems, x_res, row(0, 1), row(0, 0), h, hT, ident, eps_col)
                    latent(nc, src, hT, ckvT, ckv, w_down, wv_t, wo, late_loaded, ident)
                attention0(nc, src, hT, ckvT, ckv, outT, rope, ident, ident_b, mask_b)
            output0(nc, src, outT, wo, row(0, 2), x_res)
        if stop > 1:
            rest(nc, src, norm_sems, x_res, row, ident, ident_b, mask_b, eps_col, stop)
        store(nc, x_res, out)


def laid_out(inputs):
    import numpy as np

    a = {k: np.ascontiguousarray(v) for k, v in inputs.items()}
    f32 = np.float32
    wq = a["L0_attn_wq"].reshape(D, H, DH // 2, 2).transpose(0, 1, 3, 2).reshape(D, H * DH)
    wup = a["L0_attn_w_up"].reshape(P, H, 2, DH)
    wk = wup[:, :, 0].reshape(P, H, DH // 2, 2).transpose(0, 1, 3, 2).reshape(P, H * DH)
    inv_freq = (1.0 / 10000.0 ** (np.arange(0, DH, 2, dtype=f32) / f32(DH))).astype(f32)
    ang = np.arange(T, dtype=f32)[:, None] * inv_freq[None, :]
    cos, sin = np.cos(ang).astype(f32), np.sin(ang).astype(f32)
    table = np.stack([np.concatenate([cos, cos], 1), np.concatenate([-sin, sin], 1)])
    table = np.stack([table * f32(DH ** -0.5), table], axis=2)
    table = table.reshape(2, NT, P, 2, DH).transpose(2, 0, 1, 3, 4)
    upper = np.arange(P)[None, :] > np.arange(P)[:, None]
    bf = np.dtype("bfloat16")
    out = {
        "L0_attn_x": a["L0_attn_x"], "wq_split": wq, "w_k": wk, "wv_t": wup[:, :, 1].transpose(2, 1, 0),
        "wo_p": a["L0_attn_wo"].reshape(H, DH, D).transpose(1, 0, 2),
        "w_down_p": a["L0_attn_w_down"].reshape(KD, P, P).transpose(1, 0, 2),
        "L0_c": a["L0_c"], "L1_c": a["L1_c"], "L0_wmod": a["L0_wmod"], "L1_wmod": a["L1_wmod"],
        "rope": table, "ident": np.eye(P, dtype=f32), "ident_b": np.eye(P).astype(bf),
        "mask_b": np.where(upper, -3e38, 0.0).astype(bf), "eps": np.full((P, 1), EPS, f32),
    }
    experts, slots = np.arange(P), np.arange(SLOTS)
    w1 = np.stack([a["L0_ffn_w1"], a["L0_ffn_v1"]]).reshape(2, E0, F0, KD, P)
    out |= {
        "router_t": a["L0_ffn_router_w"].reshape(E0, KD, P).transpose(2, 1, 0),
        "ones_b": np.ones((P, P)).astype(bf), "before_b": upper.astype(bf),
        "slot_c": np.tile(np.arange(C0, dtype=f32), (P, 1)),
        "own_b": (slots[None, :] // C0 == experts[:, None]).astype(bf),
        "sel_b": (slots[None, :] // C0 == experts[:, None]).astype(bf).reshape(P, NSB, P),
        "ones_f": np.ones((P, F0), f32), "c_col": (np.arange(P) % C0).astype(f32)[:, None],
        "w_up0": w1.transpose(4, 1, 0, 3, 2), "w_dn0": a["L0_ffn_w2"].transpose(1, 0, 2),
    }
    rel = np.arange(T, dtype=f32)[None, :] - np.arange(P, dtype=f32)[:, None] - f32(T - P)
    gate_s, up_s = a["L1_ffn_shared_wg"].reshape(2, 2, I1, D)
    wg = np.concatenate([a["L1_ffn_expert_wg"], np.stack([gate_s, up_s], 1).reshape(2, 2 * I1, D)])
    wd = np.concatenate([a["L1_ffn_expert_wd"], a["L1_ffn_shared_wd"].reshape(D, 2, I1).transpose(1, 0, 2)])
    out |= {
        "expand_t": a["L1_attn_expand"].reshape(-1, KD, P).transpose(2, 1, 0), "rel": rel,
        "project_t": a["L1_attn_project"].reshape(D, 4, P).transpose(2, 1, 0),
        "pos_mult": a["L1_attn_pos_mult"].reshape(1, 1),
        "ln_gamma": a["L1_attn_ln_gamma"].reshape(1, D), "ln_beta": a["L1_attn_ln_beta"].reshape(1, D),
        "gate_t": a["L1_ffn_gate_w"].reshape(E1, KD, P).transpose(2, 1, 0),
        "w_up1": wg.reshape(NE1, 2 * I1, KD, P).transpose(3, 0, 2, 1),
        "w_dn1": wd.reshape(NE1, D, 2, HI1).transpose(3, 0, 2, 1),
    }
    return {k: np.ascontiguousarray(v) for k, v in out.items()}


def kernel(**inputs):
    import concourse.bacc as _bacc
    from concourse import mybir as _mybir
    from concourse.bass_utils import run_bass_kernel_spmd as _run

    nc = _bacc.Bacc("TRN2", target_bir_lowering=False, num_devices=1)
    arrays = laid_out(inputs)
    src = {n: nc.dram_tensor(f"in_{n}", a.shape, _mybir.dt.from_np(a.dtype), kind="ExternalInput").ap() for n, a in arrays.items()}
    out = nc.dram_tensor("out", (1, T, D), F32, kind="ExternalOutput").ap()
    build(nc, src, out)
    r = _run(nc, [{f"in_{n}": a for n, a in arrays.items()}], core_ids=[0])
    return r.results[0]["out"]
```

```python
from contextlib import ExitStack

import concourse.bass as bass
from concourse import mybir

F32 = mybir.dt.float32
F32R = mybir.dt.float32r
BF16 = mybir.dt.bfloat16
ALU = mybir.AluOpType
ACT = mybir.ActivationFunctionType
AX = mybir.AxisListType.X

P = 128
T = 1024
NT = T // P
D = 256
KD = D // P
H = 16
DH = 128
LAG = 7
QLAG = 3
EPS = 1e-5

E0, K0, F0, C0 = 64, 8, 96, 32
SLOTS = E0 * C0
NSB = SLOTS // P
EPB = P // C0

QK1, EXP1 = D // 8, 2 * D
E1, K1, I1 = 8, 2, 176
SI1 = 2 * I1

NE1 = E1 + 1
NC1 = -(-(E1 * I1 + SI1) // P)
WU1 = 2 * KD * P + P


def wait_pos(eng, sem, count):
    if not isinstance(count, int) or count > 0:
        eng.wait_ge(sem, count)


def finish_modulation(dve, m, gneg, gsign, step):
    dve.tensor_scalar(m[:, :, 1, :], m[:, :, 1, :], 1.0, None, ALU.add).then_inc(step, 1)
    dve.tensor_scalar(gneg[:], m[:, :, 2, :], -1.0, 0.25, ALU.mult, ALU.max).then_inc(step, 1)
    dve.tensor_scalar(gsign[:], m[:, :, 2, :], 0.0, 2.0, ALU.is_ge, ALU.mult).then_inc(step, 1)
    dve.wait_ge(step, 3)
    dve.tensor_tensor(gneg[:], gneg[:], m[:, :, 2, :], ALU.max).then_inc(step, 1)
    dve.wait_ge(step, 4)
    dve.scalar_tensor_tensor(m[:, :, 2, :], gsign[:], -1.0, gneg[:], ALU.add, ALU.mult).then_inc(step, 1)


def modulation(nc, src, cst, late, modv, s_col, x_res, load_sem, norm_sems, stats, mv):
    with ExitStack() as ctx:
        c_col = ctx.enter_context(nc.sbuf_tensor("c_col", [P, 2, KD], F32))
        s_wide = ctx.enter_context(nc.sbuf_tensor("s_wide", [P, KD, P], F32))
        wmod = ctx.enter_context(nc.sbuf_tensor("wmod", [P, KD, 6 * D], F32))
        gneg = ctx.enter_context(nc.sbuf_tensor("gneg", [P, 2, D], F32))
        gsign = ctx.enter_context(nc.sbuf_tensor("gsign", [P, 2, D], F32))
        ps = [ctx.enter_context(nc.psum_tensor(f"mod_ps{i}", [P, 512], F32)) for i in range(3)]
        c_loaded, wmod_loaded, const_loaded = (nc.alloc_semaphore(n) for n in ("c_loaded", "wmod_loaded", "const_loaded"))
        silu_done, wide_done, mod_ready, mod_copied, gate_step = (
            nc.alloc_semaphore(n) for n in ("silu_done", "wide_done", "mod_ready", "mod_copied", "gate_step"))
        with nc.Block() as block:

            @block.sync
            def _(sp):
                for l in range(2):
                    sp.dma_start(c_col[:, l, :], src[f"L{l}_c"].rearrange("o (k p) -> p (o k)", p=P),
                                 allow_slow_non_contiguous=True).then_inc(c_loaded, 16)
                sp.dma_start(wmod[:], src["L0_wmod"].rearrange("(k p) n -> p k n", p=P)).then_inc(wmod_loaded, 16)
                sp.dma_start(x_res[:], src["L0_attn_x"].rearrange("o (n p) d -> p (o n) d", p=P)).then_inc(load_sem, 16)
                for dst, name in cst:
                    sp.dma_start(dst, src[name]).then_inc(const_loaded, 16)
                for dst, name, loaded in late:
                    sp.dma_start(dst, src[name]).then_inc(loaded, 16)
                sp.wait_ge(load_sem, 16)
                sp.wait_ge(const_loaded, 16 * len(cst))

            @block.scalar
            def _(act):
                act.wait_ge(c_loaded, 32)
                act.activation(s_col[:], c_col[:], ACT.Silu).then_inc(silu_done, 1)

            @block.tensor
            def _(pe):
                pe.wait_ge(wmod_loaded, 16)
                pe.wait_ge(wide_done, KD)
                for n in range(3):
                    for k in range(KD):
                        mm = pe.matmul(ps[n][:], s_wide[:, k, :], wmod[:, k, n * 512:(n + 1) * 512], start=(k == 0), stop=(k == KD - 1))
                    mm.then_inc(mod_ready, 1)

            @block.vector
            def _(dve):
                dve.wait_ge(silu_done, 1)
                for k in range(KD):
                    dve.tensor_copy(s_wide[:, k, :], s_col[:, 0, k:k + 1].to_broadcast([P, P])).then_inc(wide_done, 1)
                dve.wait_ge(load_sem, 16)
                for t in range(NT):
                    tile_stats(dve, norm_sems, norm_sems.norms, x_res[:, t, :], stats, mv, t)
                for n in range(3):
                    dve.wait_ge(mod_ready, n + 1)
                    dve.tensor_copy(modv[:, 0, n * 512:(n + 1) * 512], ps[n][:]).then_inc(mod_copied, 1)
                dve.wait_ge(mod_copied, 3)
                finish_modulation(dve, modv[:, 0].rearrange("p (a b d) -> p a b d", a=2, b=3), gneg, gsign, gate_step)


class NormSems:

    def __init__(self, nc):
        self.stats, self.mv, self.std, self.rstd, self.z, self.h, self.turned, self.copied, self.copied_k1, self.cols = (
            nc.alloc_semaphore("ln_" + n) for n in ("stats", "mv", "std", "rstd", "z", "h", "turned", "copied", "copied_k1", "cols"))
        self.norms = self.turns = self.folded = 0


def tile_stats(dve, sems, norm, x_t, stats, mv, t):
    dve.bn_stats(stats[:, t, :], x_t).then_inc(sems.stats, 1)
    dve.wait_ge(sems.stats, norm * NT + t + 1)
    dve.bn_aggr(mv[:, t, :], stats[:, t, :]).then_inc(sems.mv, 1)


def norm_tiles(nc, tag, sems, x, scale, shift, h, mv, eps_col, hT=None, ident=None, loads=None, next_stats=None):
    with ExitStack() as ctx:
        std = ctx.enter_context(nc.sbuf_tensor(f"{tag}_std", [P, NT], F32))
        rstd = ctx.enter_context(nc.sbuf_tensor(f"{tag}_rstd", [P, NT], F32))
        z = ctx.enter_context(nc.sbuf_tensor(f"{tag}_z", [P, NT, D], F32))
        ps = [ctx.enter_context(nc.psum_tensor(f"{tag}_ps{i}", [P, 512], F32)) for i in range(4)]
        norms, turns = sems.norms, sems.turns
        with nc.Block() as block:

            @block.sync
            def _(sp):
                if loads is not None:
                    loads(sp)

            @block.vector
            def _(dve):
                for t in range(NT):
                    dve.scalar_tensor_tensor(z[:, t, :], x[:, t, :], mv[:, t, 0:1], scale, ALU.subtract, ALU.mult).then_inc(sems.z, 1)
                    if t == 1:
                        dve.wait_ge(sems.std, norms + 1)
                        dve.reciprocal(rstd[:], std[:]).then_inc(sems.rstd, 1)
                dve.wait_ge(sems.rstd, norms + 1)
                for t in range(NT):
                    dve.wait_ge(sems.z, (norms - sems.folded) * NT + t + 1)
                    dve.scalar_tensor_tensor(h[:, t, :], z[:, t, :], rstd[:, t:t + 1], shift, ALU.mult, ALU.add).then_inc(sems.h, 1)
                    if next_stats is not None:
                        dve.wait_ge(sems.h, norms * NT + t + 1)
                        tile_stats(dve, sems, norms + 1, h[:, t, :], *next_stats, t)

            @block.scalar
            def _(act):
                act.activation(std[:], mv[:, :, 1], ACT.Sqrt, bias=eps_col[:]).then_inc(sems.std, 1)
                if hT is not None:
                    for t in range(NT):
                        act.wait_ge(sems.turned, turns + t + 1)
                        act.activation(hT[:, :, t * P:(t + 1) * P], ps[t % 4][:, 0:KD * P].rearrange("p (k c) -> p k c", k=KD),
                                       ACT.Copy).then_inc(sems.copied, 1)

            @block.tensor
            def _(pe):
                if hT is not None:
                    for t in range(NT):
                        pe.wait_ge(sems.h, norms * NT + t + 1)
                        if t >= 4:
                            pe.wait_ge(sems.copied, turns + t - 3)
                        for k in range(KD):
                            mm = pe.transpose(ps[t % 4][:, k * P:(k + 1) * P], h[:, t, k * P:(k + 1) * P], ident[:])
                        mm.then_inc(sems.turned, 1)

    sems.norms += 1
    sems.turns += NT if hT is not None else 0


def norm_turned(nc, tag, sems, x, scale, shift, hT, mv, ident, eps_col, loads=None):
    with ExitStack() as ctx:
        std = ctx.enter_context(nc.sbuf_tensor(f"{tag}_std", [P, NT], F32))
        rstd = ctx.enter_context(nc.sbuf_tensor(f"{tag}_rstd", [P, NT], F32))
        h = ctx.enter_context(nc.sbuf_tensor(f"{tag}_h", [P, NT, D], F32))
        cols = ctx.enter_context(nc.sbuf_tensor(f"{tag}_cols", [P, 2, KD], F32))
        ps = [[ctx.enter_context(nc.psum_tensor(f"{tag}_ps{k}{i}", [P, 512], F32)) for i in range(2)] for k in range(KD)]
        col_ps = ctx.enter_context(nc.psum_tensor(f"{tag}_col_ps", [P, 2, KD, P], F32))
        norms, turns, folded = sems.norms, sems.turns, sems.folded
        with nc.Block() as block:

            @block.sync
            def _(sp):
                if loads is not None:
                    loads(sp)

            @block.scalar
            def _(act):
                act.activation(std[:], mv[:, :, 1], ACT.Sqrt, bias=eps_col[:]).then_inc(sems.std, 1)
                act.wait_ge(sems.cols, 2 * folded + 2)
                for t in range(NT):
                    act.wait_ge(sems.turned, turns + t + 1)
                    act.activation(hT[:, 0, t * P:(t + 1) * P], ps[0][t % 2][:, 0:P], ACT.Identity, scale=cols[:, 0, 0:1],
                                   bias=cols[:, 1, 0:1]).then_inc(sems.copied, 1)

            @block.tensor
            def _(pe):
                for j, row in enumerate((scale, shift)):
                    for k in range(KD):
                        mm = pe.transpose(col_ps[:, j, k, :], row[:, k * P:(k + 1) * P], ident[:])
                mm.then_inc(sems.cols, 1)
                for t in range(NT):
                    pe.wait_ge(sems.h, norms * NT + t + 1)
                    if t >= 2:
                        pe.wait_ge(sems.copied, turns + t - 1)
                        pe.wait_ge(sems.copied_k1, folded * NT + t - 1)
                    for k in range(KD):
                        mm = pe.transpose(ps[k][t % 2][:, 0:P], h[:, t, k * P:(k + 1) * P], ident[:])
                    mm.then_inc(sems.turned, 1)

            @block.vector
            def _(dve):
                def fold(t):
                    dve.wait_ge(sems.turned, turns + t + 1)
                    dve.tensor_scalar(hT[:, 1, t * P:(t + 1) * P], ps[1][t % 2][:, 0:P], cols[:, 0, 1:2], cols[:, 1, 1:2],
                                      ALU.mult, ALU.add).then_inc(sems.copied_k1, 1)

                dve.wait_ge(sems.cols, 2 * folded + 1)
                dve.tensor_copy(cols[:], col_ps[:, :, :, 0]).then_inc(sems.cols, 1)
                dve.wait_ge(sems.std, norms + 1)
                dve.reciprocal(rstd[:], std[:]).then_inc(sems.rstd, 1)
                dve.wait_ge(sems.rstd, norms + 1)
                dve.wait_ge(sems.cols, 2 * folded + 2)
                for t in range(NT):
                    dve.tensor_scalar(h[:, t, :], x[:, t, :], mv[:, t, 0:1], rstd[:, t:t + 1], ALU.subtract, ALU.mult).then_inc(sems.h, 1)
                    if t >= 2:
                        fold(t - 2)
                fold(NT - 2)
                fold(NT - 1)

    sems.norms += 1
    sems.turns += NT
    sems.folded += 1


def latent(nc, hT, ckvT, ckv, w_down, ident):
    with ExitStack() as ctx:
        ps = [ctx.enter_context(nc.psum_tensor(f"lat_ps{i}", [P, 512], F32)) for i in range(4)]
        lat_ready, lat_copied, turned, ckv_copied = (nc.alloc_semaphore("lat_" + n) for n in ("ready", "copied", "turned", "ckv_copied"))
        with nc.Block() as block:

            @block.tensor
            def _(pe):
                for c in range(2):
                    for k in range(KD):
                        mm = pe.matmul(ps[c][:], w_down[:, k, :], hT[:, k, c * 512:(c + 1) * 512], start=(k == 0), stop=(k == KD - 1))
                    mm.then_inc(lat_ready, 1)
                for c in range(2):
                    pe.wait_ge(lat_copied, c + 1)
                    for n in range(4):
                        mm = pe.transpose(ps[2 + c][:, n * P:(n + 1) * P], ckvT[:, (4 * c + n) * P:(4 * c + n + 1) * P], ident[:])
                    mm.then_inc(turned, 1)

            @block.vector
            def _(dve):
                for c in range(2):
                    dve.wait_ge(lat_ready, c + 1)
                    dve.tensor_copy(ckvT[:, c * 512:(c + 1) * 512], ps[c][:]).then_inc(lat_copied, 1)

            @block.scalar
            def _(act):
                for c in range(2):
                    act.wait_ge(turned, c + 1)
                    act.activation(ckv[:, 4 * c:4 * c + 4, :], ps[2 + c][:].rearrange("p (n l) -> p n l", n=4), ACT.Copy).then_inc(ckv_copied, 1)


def attention0(nc, src, hT, ckvT, ckv, outT, wv_t, wo, late_loaded, rope, rope_loaded, ident, ident_b, mask_b):
    with ExitStack() as ctx:
        def sb(name, shape, dt=F32):
            return ctx.enter_context(nc.sbuf_tensor(name, shape, dt))

        def ps(name):
            return ctx.enter_context(nc.psum_tensor(name, [P, 512], F32))

        w_q = [sb(f"w_q{b}", [P, KD, DH]) for b in range(2)]
        w_k = [sb(f"w_k{b}", [P, DH]) for b in range(2)]
        qk_hi = [sb(f"qk_hi{b}", [P, 2, T], F32R) for b in range(2)]
        qk_lo = [sb(f"qk_lo{b}", [P, 2, T], F32R) for b in range(2)]
        rope_a = [sb(f"rope_a{b}", [P, 2, DH]) for b in range(2)]
        rope_b = [sb(f"rope_b{b}", [P, 2, DH]) for b in range(2)]
        rope_r = [sb(f"rope_r{b}", [P, 2, DH]) for b in range(4)]
        turned = [sb(f"turned{b}", [P, 2, P]) for b in range(2)]
        probs = [sb(f"probs{b}", [P, T]) for b in range(4)]
        probsT = [sb(f"probsT{b}", [P, NT, P]) for b in range(2)]
        nmax, rowsum, rinv = sb("nmax", [P, 4]), sb("rowsum", [P, 4]), sb("rinv", [P, 4])
        s_ps = [ctx.enter_context(nc.psum_tensor(f"s_ps{b}", [P, 2, 512], F32)) for b in range(2)]
        t_ps, o_ps, pj_ps = [ps("t_ps0"), ps("t_ps1")], ps("o_ps"), ps("pj_ps")

        def sem(n):
            return nc.alloc_semaphore("a0_" + n)

        w_ready = [sem("w_ready0"), sem("w_ready1")]
        proj_done, ab_done, rope_done, qk_turned, qk_copied, qk_split = (
            sem(n) for n in ("proj_done", "ab_done", "rope_done", "qk_turned", "qk_copied", "qk_split"))
        s_ready, max_done, exp_done, recip_done, norm_done = (
            sem(n) for n in ("s_ready", "max_done", "exp_done", "recip_done", "norm_done"))
        t_ready = [sem("t_ready0"), sem("t_ready1")]
        t_copied = [sem("t_copied0"), sem("t_copied1")]
        pv_done, o_copied, pool_steps = sem("pv_done"), sem("o_copied"), sem("pool_steps")
        wov_ready, wov_copied = sem("wov_ready"), sem("wov_copied")

        wq_d = src["wq_split"].rearrange("(k p) n -> p k n", p=P)
        wk_d = src["w_k"]

        def scores_view(slot, i):
            w = (i + 1) * P
            if w <= 512:
                return s_ps[slot][:, 0:1, 0:w], [(0, 0, w)]
            return s_ps[slot][:, 0:2, 0:w // 2], [(0, 0, w // 2), (1, w // 2, w)]

        def steps(eng, step):
            for i in range(NT):
                step(0, i, 0)
            with eng.Fori(0, (H - 2) // 2) as pair:
                for u in (1, 2):
                    for i in range(NT):
                        step(2 * pair + u, i, u % 2)
            for i in range(NT):
                step(H - 1, i, (H - 1) % 2)
            for i in range(3):
                step(H, i, H % 2)

        def at(h, i, u):
            if i < 0:
                h, i, u = h - 1, i + NT, 1 - u
            if i >= NT:
                h, i, u = h + 1, i - NT, 1 - u
            return h, i, u, h * NT + i

        def real(h):
            return not isinstance(h, int) or 0 <= h < H

        with nc.Block() as block:

            @block.sync
            def _(sp):
                def load(h, b):
                    wait_pos(sp, proj_done, NT * (h - 1))
                    sp.dma_start(w_q[b][:], wq_d[:, :, bass.ds(h * DH, DH)]).then_inc(w_ready[b], 16)
                    sp.dma_start(w_k[b][:], wk_d[:, bass.ds(h * DH, DH)]).then_inc(w_ready[b], 16)

                load(0, 0)
                load(1, 1)
                with sp.Fori(1, H // 2) as pair:
                    for b in range(2):
                        load(2 * pair + b, b)

            @block.tensor
            def _(pe):
                def project(h, i, u, n):
                    wait_pos(pe, ab_done, n)
                    pe.wait_ge(w_ready[u], 16 * h + 32 - 16 * u)
                    for k in range(KD):
                        pe.matmul(pj_ps[:, 0:DH], hT[:, k, i * P:(i + 1) * P], w_q[u][:, k, :],
                                  start=(k == 0), stop=(k == KD - 1))
                    pe.matmul(pj_ps[:, DH:2 * DH], ckvT[:, i * P:(i + 1) * P], w_k[u][:],
                              start=False, stop=True, skip_group_check=True).then_inc(proj_done, 1)

                def turn_qk(n, b, g):
                    pe.wait_ge(rope_done, n + 1)
                    wait_pos(pe, o_copied, g - 3)
                    wait_pos(pe, qk_copied, n)
                    for j in range(2):
                        mm = pe.transpose(o_ps[:, (2 + j) * P:(3 + j) * P], rope_r[b][:, j, :], ident[:])
                    mm.then_inc(qk_turned, 1)

                def step(h, i, u):
                    g = h * NT + i
                    hn, tn, un, n = at(h, i + LAG, u)
                    hp, tp, up, _ = at(h, i - 2, u)
                    hv, tv, _, _ = at(h, i - 3, u)
                    hl = at(h, i + LAG - QLAG, u)[0]
                    if real(hl):
                        turn_qk(n - QLAG, (i + LAG - QLAG) % 4, g)
                    if real(h):
                        pe.wait_ge(qk_split, g + (2 if i == 0 else 1))
                        wait_pos(pe, exp_done, g - 1)
                        _, parts = scores_view(i % 2, i)
                        d0 = i * P
                        for bank, lo, hi in parts:
                            last = hi == (i + 1) * P
                            if last:
                                pe.matmul(s_ps[i % 2][:, bank, d0 - lo:d0 - lo + P], ident_b[:], mask_b[:],
                                          start=True, stop=False, skip_group_check=True)
                            top = max(hi, 2 * P)
                            for m, (q, k) in enumerate(((qk_hi, qk_hi), (qk_hi, qk_lo), (qk_lo, qk_hi))):
                                mm = pe.matmul(s_ps[i % 2][:, bank, 0:top - lo], q[u][:, 0, i * P:(i + 1) * P], k[u][:, 1, lo:top],
                                               start=(m == 0 and not last), stop=(m == 2), skip_group_check=True)
                        mm.then_inc(s_ready, 1)
                    if real(hp):
                        pe.wait_ge(norm_done, g - 1)
                        for j in range(tp // 4 + 1):
                            before = g - 2 if j == 0 else hp * 4 + tp - 4
                            wait_pos(pe, t_copied[j], before)
                            for kb in range(4 * j, min(4 * j + 4, tp + 1)):
                                mm = pe.transpose(t_ps[j][:, (kb % 4) * P:(kb % 4 + 1) * P],
                                                  probs[tp % 4][:, kb * P:(kb + 1) * P], ident[:])
                            mm.then_inc(t_ready[j], 1)
                    if real(hv):
                        pe.wait_ge(t_copied[0], g - 2)
                        wait_pos(pe, o_copied, g - 3)
                        if real(hl):
                            pe.wait_ge(qk_copied, n - QLAG + 1)
                        for kb in range(tv + 1):
                            if kb == 4:
                                pe.wait_ge(t_copied[1], hv * 4 + tv - 3)
                            mm = pe.matmul(o_ps[:, 0:P], ckv[:, kb, :], probsT[tv % 2][:, kb, :],
                                           start=(kb == 0), stop=(kb == tv))
                        mm.then_inc(pv_done, 1)
                    if real(hn):
                        project(hn, tn, un, n)

                for n in range(H // 2):
                    if QLAG <= n < LAG:
                        turn_qk(n - QLAG, (n - QLAG) % 4, 0)
                    if n < LAG:
                        project(0, n, 0, n)
                    if n == 0:
                        pe.wait_ge(late_loaded, 32)
                    if n >= 4:
                        pe.wait_ge(wov_copied, n - 3)
                    for v in range(2):
                        mm = pe.matmul(s_ps[n // 2 % 2][:, n % 2, v * D:(v + 1) * D], wv_t[:, 2 * n + v, :], wo[:, 2 * n + v, :],
                                       start=(v == 0), stop=True, skip_group_check=True)
                    mm.then_inc(wov_ready, 1)
                pe.wait_ge(wov_copied, H // 2)
                steps(pe, step)

            @block.vector
            def _(dve):
                def rope_products(i, n, b):
                    dve.wait_ge(proj_done, n + 1)
                    wait_pos(dve, rope_done, n - 1)
                    x = pj_ps[:, 0:2 * DH].rearrange("p (a d) -> p a d", a=2)
                    half, cos, sin = DH // 2, rope[:, 0, i], rope[:, 1, i]
                    dve.tensor_tensor(rope_a[b][:].rearrange("p a (s d) -> p a s d", s=2), x.rearrange("p a (s d) -> p a s d", s=2),
                                      cos.unsqueeze(2).to_broadcast([P, 2, 2, half]), ALU.mult)
                    dve.scalar_tensor_tensor(rope_b[b][:, :, 0:half], x[:, :, half:DH], -1.0, sin, ALU.mult, ALU.mult)
                    dve.tensor_tensor(rope_b[b][:, :, half:DH], x[:, :, 0:half], sin, ALU.mult).then_inc(ab_done, 1)

                def step(h, i, u):
                    g = h * NT + i
                    hn, tn, un, n = at(h, i + LAG, u)
                    hl, tl, ul, nl = at(h, i + LAG - QLAG, u)
                    h1, t1, _, _ = at(h, i - 1, u)
                    hp, tp, up, _ = at(h, i - 2, u)
                    ho, to, _, _ = at(h, i - 3, u)
                    if real(h1):
                        dve.wait_ge(exp_done, g)
                        dve.reciprocal(rinv[:, t1 % 4:t1 % 4 + 1], rowsum[:, t1 % 4:t1 % 4 + 1]).then_inc(recip_done, 1)
                    if real(h):
                        dve.wait_ge(s_ready, g + 1)
                        dve.tensor_reduce(nmax[:, i % 4:i % 4 + 1], scores_view(i % 2, i)[0], mybir.AxisListType.XY, ALU.max,
                                          negate=True).then_inc(max_done, 1)
                    if real(hp) and tp >= 4:
                        dve.wait_ge(t_ready[1], hp * 4 + tp - 3)
                        wait_pos(dve, pv_done, g - 3)
                        w = tp - 3
                        dve.tensor_copy(probsT[tp % 2][:, 4:4 + w, :], t_ps[1][:, 0:w * P].rearrange("p (a c) -> p a c", a=w))\
                           .then_inc(t_copied[1], 1)
                    if real(ho):
                        dve.wait_ge(pv_done, g - 2)
                        dve.tensor_copy(outT[:, ho, to * P:(to + 1) * P], o_ps[:, 0:P]).then_inc(o_copied, 1)
                    if real(hn):
                        rope_products(tn, n, (i + LAG) % 2)

                dve.wait_ge(rope_loaded, 16)
                for n in range(LAG):
                    rope_products(n, n, n % 2)
                steps(dve, step)

            @block.scalar
            def _(act):
                def copy_qk(i, u, n):
                    act.wait_ge(qk_turned, n + 1)
                    wait_pos(act, qk_split, n - 1)
                    x = o_ps[:, 2 * P:4 * P].rearrange("p (a c) -> p a c", a=2)
                    act.activation(qk_hi[u][:, :, i * P:(i + 1) * P], x, ACT.Copy)
                    act.activation(turned[i % 2][:], x, ACT.Copy).then_inc(qk_copied, 1)

                def step(h, i, u):
                    g = h * NT + i
                    hl, tl, ul, nl = at(h, i + LAG - QLAG, u)
                    hp, tp, up, _ = at(h, i - 2, u)
                    if real(hl):
                        copy_qk(tl, ul, nl)
                    if real(hp):
                        act.wait_ge(t_ready[0], g - 1)
                        wait_pos(act, pv_done, g - 3)
                        w = min(tp + 1, 4)
                        act.activation(probsT[tp % 2][:, 0:w, :], t_ps[0][:, 0:w * P].rearrange("p (a c) -> p a c", a=w),
                                       ACT.Copy).then_inc(t_copied[0], 1)
                    if real(h):
                        act.wait_ge(max_done, g + 1)
                        view, parts = scores_view(i % 2, i)
                        out = probs[i % 4][:, 0:(i + 1) * P].rearrange("p (a c) -> p a c", a=len(parts))
                        act.activation(out, view, ACT.Exp, bias=nmax[:, i % 4:i % 4 + 1],
                                       accum_out=rowsum[:, i % 4:i % 4 + 1]).then_inc(exp_done, 1)

                for n in range(H // 2):
                    if QLAG <= n < LAG:
                        copy_qk(n - QLAG, 0, n - QLAG)
                    act.wait_ge(wov_ready, n + 1)
                    act.activation(wo[:, 2 * n:2 * n + 2, :], s_ps[n // 2 % 2][:, n % 2, :].rearrange("p (v d) -> p v d", v=2),
                                   ACT.Copy).then_inc(wov_copied, 1)
                steps(act, step)

            @block.gpsimd
            def _(pool):
                def rope_sum(n, b, r):
                    pool.wait_ge(ab_done, n + 1)
                    wait_pos(pool, qk_turned, n - 3)
                    pool.tensor_tensor(rope_r[r][:], rope_a[b][:], rope_b[b][:], ALU.add).then_inc(rope_done, 1)

                def split_qk(i, u, n):
                    pool.wait_ge(qk_copied, n + 1)
                    cols = slice(i * P, (i + 1) * P)
                    pool.tensor_tensor(qk_lo[u][:, :, cols], turned[i % 2][:], qk_hi[u][:, :, cols], ALU.subtract).then_inc(qk_split, 1)

                def step(h, i, u):
                    g = h * NT + i
                    hn, _, _, n = at(h, i + LAG, u)
                    hl, tl, ul, nl = at(h, i + LAG - QLAG, u)
                    h1, t1, _, _ = at(h, i - 1, u)
                    if real(h1):
                        pool.wait_ge(recip_done, g)
                        pool.sem_inc(pool_steps, 1)
                        p = probs[t1 % 4][:, 0:(t1 + 1) * P]
                        pool.tensor_scalar(p, p, rinv[:, t1 % 4:t1 % 4 + 1], 1.0, ALU.mult, ALU.mult).then_inc(norm_done, 1)
                    if real(hl):
                        split_qk(tl, ul, nl)
                    if real(hn):
                        rope_sum(n, (i + LAG) % 2, (i + LAG) % 4)

                for n in range(LAG):
                    if n >= QLAG:
                        split_qk(n - QLAG, 0, n - QLAG)
                    rope_sum(n, n % 2, n % 4)
                steps(pool, step)


def output0(nc, norm_sems, stats, mv, outT, wo, gate, x_res):
    with ExitStack() as ctx:
        wo_hi, wo_lo = (ctx.enter_context(nc.sbuf_tensor(f"wo_{n}", [P, H, D], F32R)) for n in ("hi", "lo"))
        o_hi, o_lo = ([ctx.enter_context(nc.sbuf_tensor(f"o_{n}{i}", [P, H, P], F32R)) for i in range(2)] for n in ("hi", "lo"))
        part = [ctx.enter_context(nc.sbuf_tensor(f"wo_part{i}", [P, D], F32)) for i in range(2)]
        ps = [ctx.enter_context(nc.psum_tensor(f"wo_ps{i}", [P, 512], F32)) for i in range(2)]
        y_ready, gated, added, hi_done, lo_done = (nc.alloc_semaphore("wo_" + n) for n in ("ready", "gated", "added", "hi_done", "lo_done"))

        def tile(t):
            return outT[:, :, t * P:(t + 1) * P]

        with nc.Block() as block:

            @block.scalar
            def _(act):
                act.activation(wo_hi[:], wo[:], ACT.Copy).then_inc(hi_done, 1)
                for t in range(1, NT):
                    if t >= 3:
                        act.wait_ge(y_ready, t - 1)
                    act.activation(o_hi[t % 2][:], tile(t), ACT.Copy).then_inc(hi_done, 1)

            @block.tensor
            def _(pe):
                for t in range(NT):
                    if t >= 1:
                        pe.wait_ge(lo_done, t + 1)
                    if t >= 2:
                        pe.wait_ge(gated, t - 1)
                    for h in range(H):
                        if t == 0:
                            mm = pe.matmul(ps[0][:, 0:D], outT[:, h, 0:P], wo[:, h, :], start=(h == 0), stop=(h == H - 1))
                            continue
                        for n, (o, w) in enumerate(((o_hi, wo_hi), (o_hi, wo_lo), (o_lo, wo_hi))):
                            mm = pe.matmul(ps[t % 2][:, 0:D], o[t % 2][:, h, :], w[:, h, :],
                                           start=(h == 0 and n == 0), stop=(h == H - 1 and n == 2))
                    mm.then_inc(y_ready, 1)

            @block.vector
            def _(dve):
                def split(t):
                    dve.wait_ge(hi_done, t + 1)
                    if t >= 3:
                        dve.wait_ge(y_ready, t - 1)
                    dve.tensor_tensor(o_lo[t % 2][:], tile(t), o_hi[t % 2][:], ALU.subtract).then_inc(lo_done, 1)

                dve.wait_ge(hi_done, 1)
                dve.tensor_tensor(wo_lo[:], wo[:], wo_hi[:], ALU.subtract).then_inc(lo_done, 1)
                split(1)
                split(2)
                for t in range(NT):
                    dve.wait_ge(y_ready, t + 1)
                    dve.tensor_tensor(part[t % 2][:], ps[t % 2][:, 0:D], gate, ALU.mult).then_inc(gated, 1)
                    if 3 <= t + 2 < NT:
                        split(t + 2)
                    dve.wait_ge(gated, t + 1)
                    dve.tensor_tensor(x_res[:, t, :], x_res[:, t, :], part[t % 2][:], ALU.add).then_inc(added, 1)
                    dve.wait_ge(added, t + 1)
                    tile_stats(dve, norm_sems, norm_sems.norms, x_res[:, t, :], stats, mv, t)


def route0(nc, loaded, rw, ones_b, before_b, wmod, s_col, mod1, h, hT, hw_hi, hw_lo, place, posT, ident):
    with ExitStack() as ctx:
        def sb(name, shape, dt=F32):
            return ctx.enter_context(nc.sbuf_tensor(name, shape, dt))

        def sem(n):
            return nc.alloc_semaphore("r0_" + n)

        s_wide = sb("s_wide1", [P, KD, P])
        mod_ps = [ctx.enter_context(nc.psum_tensor(f"mod1_ps{i}", [P, 512], F32)) for i in range(3)]
        nmax, total, inv = sb("r_nmax", [P, NT]), sb("r_total", [P, NT]), sb("r_inv", [P, NT])
        shifted, ex, marked = sb("r_shifted", [P, NT, E0]), sb("r_ex", [P, NT, E0]), sb("r_marked", [P, NT, E0])
        top = sb("r_top", [P, NT, K0])
        chosen, chosen_b = sb("r_chosen", [P, NT, E0]), sb("r_chosen_b", [P, NT, E0], BF16)
        off = sb("r_off", [P, NT, E0])
        wts = sb("r_wts", [P, NT, E0])
        ps = [ctx.enter_context(nc.psum_tensor(f"r_ps{i}", [P, 512], F32)) for i in range(4)]
        (logits_ready, shifted_done, exp_done, step_done, chosen_done, pos_ready, place_done, turned, wts_hi, h_hi, zeroed,
         pos_copied, wide_done, mod_ready, mod_copied) = (
            sem(n) for n in ("logits_ready", "shifted_done", "exp_done", "step_done", "chosen_done", "pos_ready",
                             "place_done", "turned", "wts_hi", "h_hi", "zeroed", "pos_copied", "wide_done", "mod_ready", "mod_copied"))
        logits = ps[0][:].rearrange("p (n e) -> p n e", n=NT)
        pos = ps[1][:].rearrange("p (n e) -> p n e", n=NT)
        with nc.Block() as block:

            @block.tensor
            def _(pe):
                pe.wait_ge(loaded, 16 * 5)
                for n in range(NT):
                    for k in range(KD):
                        mm = pe.matmul(logits[:, n, :], hT[:, k, n * P:(n + 1) * P], rw[:, k, :], start=(k == 0), stop=(k == KD - 1))
                mm.then_inc(logits_ready, 1)
                pe.wait_ge(wide_done, KD)
                for n in range(3):
                    for k in range(KD):
                        mm = pe.matmul(mod_ps[n][:], s_wide[:, k, :], wmod[:, k, n * 512:(n + 1) * 512], start=(k == 0), stop=(k == KD - 1))
                    mm.then_inc(mod_ready, 1)
                pe.wait_ge(chosen_done, 1)
                for n in range(NT):
                    for m in range(n + 1):
                        mm = pe.matmul(pos[:, n, :], (before_b if m == n else ones_b)[:], chosen_b[:, m, :],
                                       start=(m == 0), stop=(m == n))
                mm.then_inc(pos_ready, 1)
                pe.wait_ge(place_done, 1)
                for n in range(NT):
                    mm = pe.transpose(ps[2 + n // 4][0:E0, (n % 4) * P:(n % 4 + 1) * P], place[:, n, :], ident[:])
                    if n % 4 == 3:
                        mm.then_inc(turned, 1)

            @block.scalar
            def _(act):
                for k in range(KD):
                    act.activation(s_wide[:, k, :], s_col[:, 1, k:k + 1].to_broadcast([P, P]), ACT.Copy).then_inc(wide_done, 1)
                act.activation(hw_hi[:, :, 0:D], h[:], ACT.Copy).then_inc(h_hi, 1)
                act.wait_ge(shifted_done, 1)
                act.activation(ex[:], shifted[:], ACT.Exp).then_inc(exp_done, 1)
                for n in range(3):
                    act.wait_ge(mod_ready, n + 1)
                    act.activation(mod1[:, n * 512:(n + 1) * 512], mod_ps[n][:], ACT.Copy).then_inc(mod_copied, 1)
                for j in range(2):
                    act.wait_ge(turned, j + 1)
                    act.wait_ge(zeroed, 3)
                    act.activation(posT[0:E0, j * 512:(j + 1) * 512], ps[2 + j][0:E0, :], ACT.Copy).then_inc(pos_copied, 1)

            @block.gpsimd
            def _(pool):
                pool.memset(posT[:], 0.0).then_inc(zeroed, 1)
                pool.memset(hw_hi[:, :, D + E0:].bitcast(F32), 0.0).then_inc(zeroed, 1)
                pool.memset(hw_lo[:, :, D + E0:].bitcast(F32), 0.0).then_inc(zeroed, 1)
                pool.wait_ge(h_hi, 1)
                pool.tensor_tensor(hw_lo[:, :, 0:D], h[:], hw_hi[:, :, 0:D], ALU.subtract).then_inc(h_hi, 1)

            @block.vector
            def _(dve):
                done = [0]

                def after(ins):
                    done[0] += 1
                    ins.then_inc(step_done, 1)
                    dve.wait_ge(step_done, done[0])

                dve.wait_ge(logits_ready, 1)
                after(dve.tensor_reduce(nmax[:], logits, AX, ALU.max, negate=True))
                dve.tensor_tensor(shifted[:], logits, nmax[:].unsqueeze(2).to_broadcast([P, NT, E0]), ALU.add).then_inc(shifted_done, 1)
                dve.wait_ge(exp_done, 1)
                for n in range(NT):
                    ins = dve.max(top[:, n, :], ex[:, n, :])
                after(ins)
                for n in range(NT):
                    ins = dve.match_replace(marked[:, n, :], top[:, n, :], ex[:, n, :], -1.0)
                after(ins)
                after(dve.tensor_scalar(chosen[:], marked[:], 0.0, None, ALU.is_lt))
                dve.tensor_copy(chosen_b[:], chosen[:]).then_inc(chosen_done, 1)
                after(dve.tensor_tensor(wts[:], ex[:], chosen[:], ALU.mult))
                after(dve.tensor_reduce(total[:], wts[:], AX, ALU.add))
                after(dve.reciprocal(inv[:], total[:]))
                after(dve.tensor_tensor(wts[:], wts[:], inv[:].unsqueeze(2).to_broadcast([P, NT, E0]), ALU.mult))
                after(dve.tensor_scalar(off[:], chosen[:], -100.0, 100.0, ALU.mult, ALU.add))
                dve.wait_ge(pos_ready, 1)
                after(dve.tensor_tensor(off[:], off[:], pos, ALU.add))
                after(dve.tensor_scalar(place[:], off[:], 200.0, None, ALU.min))
                dve.sem_inc(place_done, 1)
                dve.tensor_copy(hw_hi[:, :, D:D + E0], wts[:]).then_inc(wts_hi, 1)
                dve.wait_ge(wts_hi, 1)
                dve.tensor_tensor(hw_lo[:, :, D:D + E0], wts[:], hw_hi[:, :, D:D + E0], ALU.subtract).then_inc(wts_hi, 1)


def gather0(nc, src, load, hw_hi, hw_lo, place, slot_c, onehot, xgT, wcol, mod1):
    with ExitStack() as ctx:
        own = ctx.enter_context(nc.sbuf_tensor("own_b", [P, SLOTS], BF16))
        wg = ctx.enter_context(nc.sbuf_tensor("wg", [P, SLOTS], F32))
        gneg = ctx.enter_context(nc.sbuf_tensor("gneg1", [P, 2, D], F32))
        gsign = ctx.enter_context(nc.sbuf_tensor("gsign1", [P, 2, D], F32))
        ps = [ctx.enter_context(nc.psum_tensor(f"g_ps{i}", [P, 512], F32)) for i in range(4)]
        col_ps = ctx.enter_context(nc.psum_tensor("g_col_ps", [P, 512], F32))
        own_loaded, onehot_ready, g_ready, g_copied, col_ready, mod_step = (
            nc.alloc_semaphore(n) for n in ("own_loaded", "onehot_ready", "g_ready", "g_copied", "g_col_ready", "mod1_step"))
        groups = [(s, k) for s in range(SLOTS // 512) for k in range(KD + 1)]
        with nc.Block() as block:

            @block.sync
            def _(sp):
                sp.dma_start(own[:], src["own_b"]).then_inc(own_loaded, 16)

            @block.tensor
            def _(pe):
                def sum_weights(s):
                    pe.wait_ge(g_copied, (s + 1) * (KD + 1))
                    for b in range(4 * s, 4 * s + 4):
                        mm = pe.matmul(col_ps[:, b:b + 1], wg[:, b * P:(b + 1) * P], load.ones[:], start=True, stop=True)
                    mm.then_inc(col_ready, 1)

                pe.wait_ge(load.const_ready, 48)
                for q, (s, k) in enumerate(groups):
                    if q >= 4:
                        pe.wait_ge(g_copied, q - 3)
                    if s >= 1 and k == KD:
                        sum_weights(s - 1)
                    for n in range(NT):
                        if k == 0:
                            pe.wait_ge(onehot_ready, s * NT + n + 1)
                        for part in (hw_hi, hw_lo):
                            mm = pe.matmul(ps[q % 4][:], part[:, n, k * P:(k + 1) * P], onehot[:, n, s * 512:(s + 1) * 512],
                                           start=(n == 0 and part is hw_hi), stop=(n == NT - 1 and part is hw_lo))
                    mm.then_inc(g_ready, 1)
                sum_weights(SLOTS // 512 - 1)

            @block.vector
            def _(dve):
                def build_onehot(s):
                    es = slice(s * 512 // C0, (s + 1) * 512 // C0)
                    for n in range(NT):
                        dve.tensor_tensor(onehot[:, n, s * 512:(s + 1) * 512].rearrange("p (e c) -> p e c", c=C0),
                                          place[:, n, es].unsqueeze(2).to_broadcast([P, 512 // C0, C0]),
                                          slot_c[:].unsqueeze(1).to_broadcast([P, 512 // C0, C0]), ALU.is_equal).then_inc(onehot_ready, 1)

                build_onehot(0)
                dve.wait_ge(own_loaded, 16)
                for q, (s, k) in enumerate(groups):
                    if k == 0 and s + 1 < SLOTS // 512:
                        build_onehot(s + 1)
                    if q == 2:
                        finish_modulation(dve, mod1.rearrange("p (a b d) -> p a b d", a=2, b=3), gneg, gsign, mod_step)
                    dve.wait_ge(g_ready, q + 1)
                    cols = slice(s * 512, (s + 1) * 512)
                    if k < KD:
                        dve.tensor_copy(xgT[:, k, cols], ps[q % 4][:]).then_inc(g_copied, 1)
                    else:
                        dve.tensor_tensor(wg[:, cols], ps[q % 4][:], own[:, cols], ALU.mult).then_inc(g_copied, 1)
                dve.wait_ge(col_ready, SLOTS // 512)
                dve.tensor_copy(wcol[:], col_ps[:, 0:NSB]).then_inc(g_copied, 1)


class ExpertLoads0:
    RING = 4

    def __init__(self, nc, ctx, src, ident):
        def sb(name, shape, dt=F32):
            return ctx.enter_context(nc.sbuf_tensor(name, shape, dt))

        self.src, self.ident = src, ident
        self.w_up = [sb(f"e_up{i}", [P, EPB, KD, 2 * F0]) for i in range(self.RING)]
        self.w_dn = [sb(f"e_dn{i}", [F0, EPB, D]) for i in range(self.RING)]
        self.sel, self.ones, self.c_col = sb("e_sel", [P, NSB, P], BF16), sb("e_ones", [P, 1]), sb("e_c", [P, 1])
        self.w_ready = [nc.alloc_semaphore(f"e0_w_ready{i}") for i in range(self.RING)]
        self.const_ready, self.y_ready = nc.alloc_semaphore("e0_const_ready"), nc.alloc_semaphore("e0_y_ready")

    def constants(self, sp):
        for dst, name in ((self.sel, "sel_b"), (self.ones, "ones_f"), (self.c_col, "c_col")):
            sp.dma_start(dst[:], self.src[name]).then_inc(self.const_ready, 16)

    def __call__(self, sp, b, i):
        wait_pos(sp, self.y_ready, b - self.RING + 1)
        sp.dma_start(self.w_up[i][:], self.src["w_up0"][:, bass.ds(b * EPB, EPB)]).then_inc(self.w_ready[i], 16)
        sp.dma_start(self.w_dn[i][:], self.src["w_dn0"][:, bass.ds(b * EPB, EPB)]).then_inc(self.w_ready[i], 16)


def experts0(nc, load, norm_sems, stats, mv, xgT, wcol, posT, gate, x_res):
    with ExitStack() as ctx:
        def sb(name, shape, dt=F32):
            return ctx.enter_context(nc.sbuf_tensor(name, shape, dt))

        def sem(n):
            return nc.alloc_semaphore("e0_" + n)

        w_up, w_dn, sel, c_col = load.w_up, load.w_dn, load.sel, load.c_col
        w_ready, const_ready, y_ready = load.w_ready, load.const_ready, load.y_ready
        rows_x = [sb(f"e_x{i}", [P, KD, P]) for i in range(2)]
        sil, glu = ([sb(f"e_{n}{i}", [P, F0]) for i in range(2)] for n in ("sil", "glu"))
        gluT = [sb(f"e_gluT{i}", [F0, P]) for i in range(2)]
        y_hi = [sb(f"e_yhi{i}", [P, D], F32R) for i in range(2)]
        y_lo = [sb(f"e_ylo{i}", [P, D], F32R) for i in range(2)]
        back = [sb(f"e_back{i}", [P, T], F32R) for i in range(4)]
        part = sb("e_part", [P, NT // 2, 2, D])
        up_ps = ctx.enter_context(nc.psum_tensor("e_up_ps", [P, 512], F32))
        turn_ps = ctx.enter_context(nc.psum_tensor("e_turn_ps", [P, 512], F32))
        y_ps = ctx.enter_context(nc.psum_tensor("e_y_ps", [P, 512], F32))
        sel_ps = ctx.enter_context(nc.psum_tensor("e_sel_ps", [P, 512], F32))
        sum_ps = ctx.enter_context(nc.psum_tensor("e_sum_ps", [P, NT // 2, 2, D], F32))
        x_done, up_ready, sil_done, glu_done, turned, turn_copied, hi_done, lo_done, sel_ready, back_done, comb_done, gated, added = (
            sem(n) for n in ("x_done", "up_ready", "sil_done", "glu_done", "turned", "turn_copied", "hi_done", "lo_done",
                             "sel_ready", "back_done", "comb_done", "gated", "added"))

        def steps(eng, step):
            for u in range(4):
                step(u, u)
            with eng.Fori(1, NSB // 4) as four:
                for u in range(4):
                    step(4 * four + u, u)
            for u in range(3):
                step(NSB + u, u)

        def real(b):
            return not isinstance(b, int) or 0 <= b < NSB

        def weight(b):
            return wcol[:, b:b + 1] if isinstance(b, int) else wcol[:, bass.ds(b, 1)]

        with nc.Block() as block:

            @block.sync
            def _(sp):
                with sp.Fori(1, NSB // 4) as four:
                    for i in range(load.RING):
                        load(sp, 4 * four + i, i)

            @block.tensor
            def _(pe):
                def select(b, half):
                    wait_pos(pe, back_done, 2 * b + half)
                    pe.matmul(sel_ps[:], sel[:, b, :], posT[:, half * 512:(half + 1) * 512],
                              start=True, stop=True).then_inc(sel_ready, 1)

                def step(b, u):
                    if real(b):
                        pe.wait_ge(w_ready[u], 8 * b - 8 * u + 32)
                        pe.wait_ge(x_done, b + 1)
                        wait_pos(pe, glu_done, b)
                        select(b, 0)
                        for k in range(KD):
                            for e in range(EPB):
                                mm = pe.matmul(up_ps[e * C0:(e + 1) * C0, 0:2 * F0], rows_x[u % 2][:, k, e * C0:(e + 1) * C0],
                                               w_up[u][:, e, k, :], start=(k == 0), stop=(k == KD - 1), skip_group_check=True)
                        mm.then_inc(up_ready, 1)
                    if real(b - 1):
                        pe.wait_ge(glu_done, b)
                        wait_pos(pe, turn_copied, b - 1)
                        pe.transpose(turn_ps[0:F0, 0:P], glu[(u - 1) % 2][:], load.ident[:]).then_inc(turned, 1)
                    if real(b - 2):
                        pe.wait_ge(turn_copied, b - 1)
                        wait_pos(pe, lo_done, b - 2)
                        for e in range(EPB):
                            mm = pe.matmul(y_ps[e * C0:(e + 1) * C0, 0:D], gluT[u % 2][:, e * C0:(e + 1) * C0],
                                           w_dn[(u - 2) % 4][:, e, :], start=True, stop=True)
                        mm.then_inc(y_ready, 1)
                    if real(b):
                        select(b, 1)
                    if real(b - 3):
                        pe.wait_ge(lo_done, b - 2)
                        pe.wait_ge(back_done, 2 * b - 4)
                        for t in range(NT):
                            for y in (y_hi, y_lo):
                                first = isinstance(b, int) and b == 3 and t % 2 == 0 and y is y_hi
                                mm = pe.matmul(sum_ps[:, t // 2, t % 2, :], back[(u - 3) % 4][:, t * P:(t + 1) * P], y[(u - 3) % 2][:],
                                               start=first, stop=(isinstance(b, int) and b == NSB + 2 and y is y_lo),
                                               skip_group_check=True)
                        mm.then_inc(comb_done, 1)

                pe.wait_ge(const_ready, 48)
                steps(pe, step)

            @block.scalar
            def _(act):
                def step(b, u):
                    if real(b):
                        wait_pos(act, up_ready, b - 1)
                        act.activation(rows_x[u % 2][:], xgT[:, :, bass.ds(b * P, P)], ACT.Copy).then_inc(x_done, 1)
                    if real(b - 1):
                        act.wait_ge(turned, b)
                        wait_pos(act, y_ready, b - 2)
                        act.activation(gluT[(u - 1) % 2][:], turn_ps[0:F0, 0:P], ACT.Copy).then_inc(turn_copied, 1)
                    if real(b):
                        act.wait_ge(up_ready, b + 1)
                        wait_pos(act, glu_done, b - 1)
                        act.activation(sil[u % 2][:], up_ps[:, 0:F0], ACT.Silu).then_inc(sil_done, 1)
                    if real(b - 2):
                        act.wait_ge(y_ready, b - 1)
                        wait_pos(act, comb_done, b - 3)
                        act.activation(y_hi[u % 2][:], y_ps[:, 0:D], ACT.Copy, scale=weight(b - 2)).then_inc(hi_done, 1)

                steps(act, step)

            @block.vector
            def _(dve):
                def map_back(b, u, half):
                    dve.wait_ge(sel_ready, 2 * b + half + 1)
                    wait_pos(dve, comb_done, b - 3)
                    dve.tensor_scalar(back[u][:, half * 512:(half + 1) * 512], sel_ps[:], c_col[:], None, ALU.is_equal).then_inc(back_done, 1)

                def step(b, u):
                    if real(b):
                        map_back(b, u, 0)
                        dve.wait_ge(sil_done, b + 1)
                        wait_pos(dve, turned, b - 1)
                        dve.tensor_tensor(glu[u % 2][:], sil[u % 2][:], up_ps[:, F0:2 * F0], ALU.mult).then_inc(glu_done, 1)
                    if real(b - 2):
                        dve.wait_ge(hi_done, b - 1)
                        dve.scalar_tensor_tensor(y_lo[u % 2][:], y_ps[:, 0:D], weight(b - 2), y_hi[u % 2][:],
                                                 ALU.mult, ALU.subtract).then_inc(lo_done, 1)
                    if real(b):
                        map_back(b, u, 1)

                dve.wait_ge(const_ready, 48)
                steps(dve, step)
                dve.wait_ge(comb_done, NSB)
                for q in range(NT // 2):
                    dve.tensor_tensor(part[:, q], sum_ps[:, q], gate.unsqueeze(1).to_broadcast([P, 2, D]), ALU.mult).then_inc(gated, 1)
                for q in range(NT // 2):
                    dve.wait_ge(added, q + 1)
                    for t in (2 * q, 2 * q + 1):
                        tile_stats(dve, norm_sems, norm_sems.norms, x_res[:, t, :], stats, mv, t)

            @block.gpsimd
            def _(pool):
                for q in range(NT // 2):
                    pool.wait_ge(gated, q + 1)
                    x = x_res[:, 2 * q:2 * q + 2, :]
                    pool.tensor_tensor(x, x, part[:, q], ALU.add).then_inc(added, 1)


def project1(nc, w_loaded, pos_loaded, w, pm, hT, qT, kT, value, catT, bias, mask_b):
    VAL, PRE = EXP1 - D, EXP1
    with ExitStack() as ctx:
        def sb(name, shape, dt=F32):
            return ctx.enter_context(nc.sbuf_tensor(name, shape, dt))

        def sem(n):
            return nc.alloc_semaphore("p1_" + n)

        gate_v = [sb(f"gate_v{i}", [P, D]) for i in range(2)]
        gate_l = [sb(f"gate_l{i}", [P, 512]) for i in range(2)]
        pos_e, pos_l, pos_s = sb("pos_e", [P, 2]), sb("pos_l", [P, 1]), sb("pos_s", [P, 2])
        ps = [ctx.enter_context(nc.psum_tensor(f"p1_ps{i}", [P, 512], F32)) for i in range(8)]
        h_hi, h_lo = sb("h2_hi", [P, KD, T], F32R), sb("h2_lo", [P, KD, T], F32R)
        w_hi, w_lo = sb("expand_hi", [P, KD, 2 * EXP1], F32R), sb("expand_lo", [P, KD, 2 * EXP1], F32R)
        w_v = w[:, :, 6 * QK1:]
        pos_abs, pos_ln, pos_step = (sem(n) for n in ("pos_abs", "pos_ln", "pos_step"))
        hi_done, lo_done, qk_hi = (sem(n) for n in ("hi_done", "lo_done", "qk_hi"))
        qk_ready, qk_copied, v_ready, v_gate, v_done, l_ready, l_gate, l_done = (
            sem(n) for n in ("qk_ready", "qk_copied", "v_ready", "v_gate", "v_done", "l_ready", "l_gate", "l_done"))
        with nc.Block() as block:

            @block.tensor
            def _(pe):
                pe.wait_ge(w_loaded, 16)

                def product(out, lhs, lhs_cols, rhs, rhs_cols):
                    for k in range(KD):
                        for n, (a, b) in enumerate(((0, 0), (0, 1), (1, 0))):
                            mm = pe.matmul(out, lhs[a][:, k, lhs_cols], rhs[b][:, k, rhs_cols],
                                           start=(k == 0 and n == 0), stop=(k == KD - 1 and n == 2))
                    return mm

                for j in range(2):
                    for c in range(2):
                        for k in range(KD):
                            mm = pe.matmul(ps[2 * j + c][0:3 * QK1, :], w[:, k, 3 * j * QK1:3 * (j + 1) * QK1],
                                           hT[:, k, c * 512:(c + 1) * 512], start=(k == 0), stop=(k == KD - 1))
                        mm.then_inc(qk_ready, 1)
                pe.wait_ge(lo_done, 2)
                for t in range(NT):
                    if t >= 2:
                        pe.wait_ge(v_done, t - 1)
                    for g in range(2):
                        mm = product(ps[4 + t % 2][:, g * D:(g + 1) * D], (h_hi, h_lo), slice(t * P, (t + 1) * P),
                                     (w_hi, w_lo), slice(VAL + g * PRE, VAL + g * PRE + D))
                    mm.then_inc(v_ready, 1)
                for q in range(4):
                    c, half = q // 2, q % 2
                    pe.wait_ge(qk_copied, 4)
                    if q >= 2:
                        pe.wait_ge(l_done, q - 1)
                    for g in range(2):
                        mm = product(ps[2 * (q % 2) + g][:], (w_hi, w_lo), slice(g * PRE + c * P, g * PRE + (c + 1) * P),
                                     (h_hi, h_lo), slice(half * 512, (half + 1) * 512))
                    mm.then_inc(l_ready, 1)

            @block.scalar
            def _(act):
                act.wait_ge(w_loaded, 16)
                act.activation(w_hi[:], w_v, ACT.Copy).then_inc(hi_done, 1)
                act.activation(h_hi[:], hT[:], ACT.Copy).then_inc(hi_done, 1)
                act.wait_ge(pos_abs, 1)
                act.activation(pos_e[:, 1:2], pos_e[:, 0:1], ACT.Exp).then_inc(pos_ln, 1)
                act.wait_ge(pos_ln, 1)
                act.activation(pos_l[:], pos_e[:, 1:2], ACT.Ln, bias=1.0).then_inc(pos_ln, 1)
                for j in range(2):
                    for c in range(2):
                        act.wait_ge(qk_ready, 2 * j + c + 1)
                        act.activation((kT if j else qT)[:, c * 512:(c + 1) * 512], ps[2 * j + c][0:3 * QK1, :], ACT.Copy,
                                       scale=1.0 if j else QK1 ** -0.5).then_inc(qk_hi, 1)
                for t in range(NT):
                    act.wait_ge(v_ready, t + 1)
                    if t >= 2:
                        act.wait_ge(v_done, t - 1)
                    act.activation(gate_v[t % 2][:], ps[4 + t % 2][:, D:2 * D], ACT.Gelu).then_inc(v_gate, 1)
                for q in range(4):
                    act.wait_ge(l_ready, q + 1)
                    if q >= 2:
                        act.wait_ge(l_done, q - 1)
                    act.activation(gate_l[q % 2][:], ps[2 * (q % 2) + 1][:], ACT.Gelu).then_inc(l_gate, 1)

            @block.gpsimd
            def _(pool):
                pool.wait_ge(hi_done, 1)
                pool.tensor_tensor(w_lo[:], w_v, w_hi[:], ALU.subtract).then_inc(lo_done, 1)

            @block.vector
            def _(dve):
                dve.wait_ge(pos_loaded, 32)
                dve.scalar_tensor_tensor(pos_e[:, 0:1], pm[:], -1.0, pm[:], ALU.mult, ALU.min).then_inc(pos_abs, 1)
                dve.tensor_scalar(pos_s[:, 0:1], pm[:], 0.0, None, ALU.max).then_inc(pos_step, 1)
                dve.wait_ge(pos_step, 1)
                dve.wait_ge(pos_ln, 2)
                dve.tensor_tensor(pos_s[:, 1:2], pos_s[:, 0:1], pos_l[:], ALU.add).then_inc(pos_step, 1)
                dve.wait_ge(hi_done, 2)
                dve.tensor_tensor(h_lo[:], hT[:], h_hi[:], ALU.subtract).then_inc(lo_done, 1)
                for j in range(2):
                    rows = slice(QK1, 2 * QK1) if j else slice(2 * QK1, 3 * QK1)
                    for c in range(2):
                        dve.wait_ge(qk_hi, 2 * j + c + 1)
                        part = (kT if j else qT)[rows, c * 512:(c + 1) * 512]
                        dve.scalar_tensor_tensor(part, ps[2 * j + c][rows, :], 1.0 if j else QK1 ** -0.5, part,
                                                 ALU.mult, ALU.subtract).then_inc(qk_copied, 1)
                dve.wait_ge(pos_step, 2)
                dve.tensor_scalar(bias[:], bias[:], pos_s[:, 1:2], None, ALU.mult).then_inc(pos_step, 1)
                dve.wait_ge(pos_step, 3)
                dve.tensor_tensor(bias[:, T - P:T], bias[:, T - P:T], mask_b[:], ALU.add).then_inc(pos_step, 1)
                for t in range(NT):
                    dve.wait_ge(v_gate, t + 1)
                    dve.tensor_tensor(value[:, t, :], gate_v[t % 2][:], ps[4 + t % 2][:, 0:D], ALU.mult).then_inc(v_done, 1)
                for q in range(4):
                    c, half = q // 2, q % 2
                    dve.wait_ge(l_gate, q + 1)
                    dve.tensor_tensor(catT[:, c, half * 512:(half + 1) * 512], gate_l[q % 2][:], ps[2 * (q % 2)][:],
                                      ALU.mult).then_inc(l_done, 1)


def attend1(nc, src, weights, norm_sems, stats, mv, qT, kT, value, catT, bias, hm, gate, x_res, ident):
    with ExitStack() as ctx:
        def sb(name, shape, dt=F32):
            return ctx.enter_context(nc.sbuf_tensor(name, shape, dt))

        def sem(n):
            return nc.alloc_semaphore("a1_" + n)

        proj = sb("proj1", [P, 4, D])
        s_sb = [sb(f"s1_{i}", [P, T]) for i in range(2)]
        probs = [sb(f"probs1_{i}", [P, T]) for i in range(3)]
        probsT = [sb(f"probs1T{i}", [P, NT, P]) for i in range(2)]
        nmax, rowsum, rinv = sb("nmax1", [P, NT]), sb("rowsum1", [P, NT]), sb("rinv1", [P, NT])
        part = [sb(f"part1_{i}", [P, 2, D]) for i in range(2)]
        s_ps = [ctx.enter_context(nc.psum_tensor(f"s1_ps{b}", [P, 2, 512], F32)) for b in range(2)]
        t_ps = [ctx.enter_context(nc.psum_tensor(f"t1_ps{b}", [P, 512], F32)) for b in range(2)]
        o_ps = ctx.enter_context(nc.psum_tensor("o1_ps", [P, 512], F32))
        y_ps = ctx.enter_context(nc.psum_tensor("y1_ps", [P, 512], F32))
        w_loaded, s_ready, biased, max_done, exp_done, recip_done, norm_done, pv_done, o_copied, y_ready, y_step, added = (
            sem(n) for n in ("w_loaded", "s_ready", "biased", "max_done", "exp_done", "recip_done", "norm_done", "pv_done",
                             "o_copied", "y_ready", "y_step", "added"))
        t_ready = [sem("t_ready0"), sem("t_ready1")]
        t_copied = [sem("t_copied0"), sem("t_copied1")]
        parts = [[(0, 0, (i + 1) * P)] if i < 4 else [(0, 0, (i + 1) * P // 2), (1, (i + 1) * P // 2, (i + 1) * P)] for i in range(NT)]

        def view(slot, i):
            return s_ps[slot][:, 0:len(parts[i]), 0:parts[i][0][2]]

        def halves(ap, i):
            return ap.rearrange("p (a c) -> p a c", a=len(parts[i]))

        with nc.Block() as block:

            @block.sync
            def _(sp):
                sp.dma_start(proj[:], src["project_t"]).then_inc(w_loaded, 16)
                for b in range(2):
                    weights.load(sp, b, b)

            @block.tensor
            def _(pe):
                for i in range(NT + 4):
                    if i < NT:
                        if i >= 2:
                            pe.wait_ge(biased, i - 1)
                        for bank, lo, hi in parts[i]:
                            mm = pe.matmul(s_ps[i % 2][:, bank, 0:hi - lo], qT[:, i * P:(i + 1) * P], kT[:, lo:hi], start=True, stop=True)
                        mm.then_inc(s_ready, 1)
                    p = i - 2
                    if 0 <= p < NT:
                        pe.wait_ge(norm_done, p + 1)
                        for j in range(p // 4 + 1):
                            wait_pos(pe, t_copied[j], p if j == 0 else p - 4)
                            for kb in range(4 * j, min(4 * j + 4, p + 1)):
                                mm = pe.transpose(t_ps[j][:, (kb % 4) * P:(kb % 4 + 1) * P], probs[p % 3][:, kb * P:(kb + 1) * P], ident[:])
                            mm.then_inc(t_ready[j], 1)
                    y = i - 4
                    if 0 <= y < NT:
                        pe.wait_ge(w_loaded, 16)
                        pe.wait_ge(o_copied, y + 1)
                        wait_pos(pe, y_step, 2 * y - 1)
                        for c in range(4):
                            mm = pe.matmul(y_ps[:, 0:D], catT[:, c, y * P:(y + 1) * P], proj[:, c, :], start=(c == 0), stop=(c == 3))
                        mm.then_inc(y_ready, 1)
                    v = i - 3
                    if 0 <= v < NT:
                        pe.wait_ge(t_copied[0], v + 1)
                        if v >= 4:
                            pe.wait_ge(t_copied[1], v - 3)
                        wait_pos(pe, o_copied, v)
                        for half in range(2):
                            for kb in range(v + 1):
                                mm = pe.matmul(o_ps[:, half * P:(half + 1) * P], value[:, kb, half * P:(half + 1) * P], probsT[v % 2][:, kb, :],
                                               start=(kb == 0), stop=(kb == v))
                        mm.then_inc(pv_done, 1)

            @block.vector
            def _(dve):
                for i in range(NT + 4):
                    if i < NT:
                        dve.wait_ge(s_ready, i + 1)
                        wait_pos(dve, exp_done, i - 1)
                        off = (NT - 1 - i) * P
                        dve.tensor_tensor(halves(s_sb[i % 2][:, 0:(i + 1) * P], i), view(i % 2, i),
                                          halves(bias[:, off:off + (i + 1) * P], i), ALU.add).then_inc(biased, 1)
                        dve.wait_ge(biased, i + 1)
                        dve.tensor_reduce(nmax[:, i:i + 1], s_sb[i % 2][:, 0:(i + 1) * P], AX, ALU.max, negate=True).then_inc(max_done, 1)
                    p = i - 2
                    if 0 <= p < NT:
                        dve.wait_ge(t_ready[0], p + 1)
                        wait_pos(dve, pv_done, p - 1)
                        n = min(p + 1, 4)
                        dve.tensor_copy(probsT[p % 2][:, 0:n, :], t_ps[0][:, 0:n * P].rearrange("p (a c) -> p a c", a=n))\
                           .then_inc(t_copied[0], 1)
                    if i < NT:
                        dve.wait_ge(exp_done, i + 1)
                        dve.reciprocal(rinv[:, i:i + 1], rowsum[:, i:i + 1]).then_inc(recip_done, 1)
                    y = i - 4
                    if 0 <= y < NT:
                        dve.wait_ge(y_ready, y + 1)
                        dve.tensor_tensor(part[y % 2][:, 0, :], y_ps[:, 0:D], hm[:, y, :], ALU.add).then_inc(y_step, 1)
                        dve.wait_ge(y_step, 2 * y + 1)
                        dve.tensor_tensor(part[y % 2][:, 1, :], part[y % 2][:, 0, :], gate, ALU.mult).then_inc(y_step, 1)
                        dve.wait_ge(y_step, 2 * y + 2)
                        dve.tensor_tensor(x_res[:, y, :], x_res[:, y, :], part[y % 2][:, 1, :], ALU.add).then_inc(added, 1)
                        dve.wait_ge(added, y + 1)
                        tile_stats(dve, norm_sems, norm_sems.norms, x_res[:, y, :], stats, mv, y)

            @block.scalar
            def _(act):
                for i in range(NT + 3):
                    if i < NT:
                        act.wait_ge(max_done, i + 1)
                        act.activation(probs[i % 3][:, 0:(i + 1) * P], s_sb[i % 2][:, 0:(i + 1) * P], ACT.Exp, bias=nmax[:, i:i + 1],
                                       accum_out=rowsum[:, i:i + 1]).then_inc(exp_done, 1)
                    p = i - 2
                    if 4 <= p < NT:
                        act.wait_ge(t_ready[1], p - 3)
                        wait_pos(act, pv_done, p - 1)
                        n = p - 3
                        act.activation(probsT[p % 2][:, 4:4 + n, :], t_ps[1][:, 0:n * P].rearrange("p (a c) -> p a c", a=n),
                                       ACT.Copy).then_inc(t_copied[1], 1)
                    v = i - 3
                    if 0 <= v < NT:
                        act.wait_ge(pv_done, v + 1)
                        act.activation(catT[:, 2:4, v * P:(v + 1) * P], o_ps[:, 0:2 * P].rearrange("p (a c) -> p a c", a=2),
                                       ACT.Copy).then_inc(o_copied, 1)

            @block.gpsimd
            def _(pool):
                for i in range(NT):
                    pool.wait_ge(recip_done, i + 1)
                    p = probs[i % 3][:, 0:(i + 1) * P]
                    pool.tensor_scalar(p, p, rinv[:, i:i + 1], 1.0, ALU.mult, ALU.mult).then_inc(norm_done, 1)
                for b in range(2):
                    pool.wait_ge(weights.ready[b], 32)
                    weights.split_up(pool, b, b)


def route1(nc, loaded, rw, hT, combT_hi, combT_lo, h_hi, h_lo, ident):
    with ExitStack() as ctx:
        def sb(name, shape, dt=F32):
            return ctx.enter_context(nc.sbuf_tensor(name, shape, dt))

        comb = sb("comb", [P, NT, NE1])
        one_t = sb("one_t", [P, E1])
        nmax, total, inv, best2, above_n, wsum = (sb(f"r1_{n}", [P, NT]) for n in ("nmax", "total", "inv", "second", "above_n", "wsum"))
        shifted, prob, above, equal, rank, ok, wts = (sb(f"r1_{n}", [P, NT, E1]) for n in
                                                      ("shifted", "prob", "above", "equal", "rank", "ok", "wts"))
        top = sb("r1_top", [P, NT, 8])
        ps = ctx.enter_context(nc.psum_tensor("r1_ps", [P, 512], F32))
        turn_ps = [ctx.enter_context(nc.psum_tensor(f"r1_turn_ps{i}", [P, 512], F32)) for i in range(2)]
        logits_ready, shifted_done, exp_done, step_done, split_done, comb_done, comb_turned, comb_hi, comb_lo = (
            nc.alloc_semaphore("r1_" + n) for n in ("logits_ready", "shifted_done", "exp_done", "step_done", "split_done", "comb_done", "comb_turned", "comb_hi", "comb_lo"))
        logits = ps[:, 0:NT * E1].rearrange("p (n e) -> p n e", n=NT)

        def wide(col):
            return col.unsqueeze(2).to_broadcast([P, NT, E1])

        with nc.Block() as block:

            @block.tensor
            def _(pe):
                pe.wait_ge(loaded, 16)
                for n in range(NT):
                    for k in range(KD):
                        mm = pe.matmul(logits[:, n, :], hT[:, k, n * P:(n + 1) * P], rw[:, k, :], start=(k == 0), stop=(k == KD - 1))
                mm.then_inc(logits_ready, 1)
                pe.wait_ge(comb_done, 1)
                for n in range(NT):
                    mm = pe.transpose(turn_ps[n // 4][0:NE1, (n % 4) * P:(n % 4 + 1) * P], comb[:, n, :], ident[:])
                    if n % 4 == 3:
                        mm.then_inc(comb_turned, 1)

            @block.scalar
            def _(act):
                act.activation(h_hi[:], hT[:], ACT.Copy).then_inc(split_done, 1)
                act.wait_ge(shifted_done, 1)
                act.activation(prob[:], shifted[:], ACT.Exp).then_inc(exp_done, 1)
                for j in range(2):
                    act.wait_ge(comb_turned, j + 1)
                    act.activation(combT_hi[:, j * 512:(j + 1) * 512], turn_ps[j][0:NE1, :], ACT.Copy).then_inc(comb_hi, 1)

            @block.gpsimd
            def _(pool):
                pool.wait_ge(split_done, 1)
                pool.tensor_tensor(h_lo[:], hT[:], h_hi[:], ALU.subtract).then_inc(split_done, 1)

            @block.vector
            def _(dve):
                done = [0]

                def after(ins):
                    done[0] += 1
                    ins.then_inc(step_done, 1)
                    dve.wait_ge(step_done, done[0])

                after(dve.memset(one_t[:], 1.0))
                after(dve.memset(comb[:], 1.0))
                dve.wait_ge(logits_ready, 1)
                after(dve.tensor_reduce(nmax[:], logits, AX, ALU.max, negate=True))
                dve.tensor_tensor(shifted[:], logits, wide(nmax[:]), ALU.add).then_inc(shifted_done, 1)
                dve.wait_ge(exp_done, 1)
                after(dve.tensor_reduce(total[:], prob[:], AX, ALU.add))
                after(dve.reciprocal(inv[:], total[:]))
                after(dve.tensor_tensor(prob[:], prob[:], wide(inv[:]), ALU.mult))
                for n in range(NT):
                    ins = dve.max(top[:, n, :], prob[:, n, :])
                after(ins)
                after(dve.tensor_copy(best2[:], top[:, :, K1 - 1]))
                dve.tensor_tensor(above[:], prob[:], wide(best2[:]), ALU.is_gt)
                after(dve.tensor_tensor(equal[:], prob[:], wide(best2[:]), ALU.is_equal))
                dve.tensor_reduce(above_n[:], above[:], AX, ALU.add)
                for n in range(NT):
                    ins = dve.tensor_tensor_scan(rank[:, n, :], one_t[:], equal[:, n, :], 0.0, ALU.mult, ALU.add)
                after(ins)
                after(dve.tensor_tensor(rank[:], rank[:], wide(above_n[:]), ALU.add))
                after(dve.scalar_tensor_tensor(ok[:], rank[:], float(K1), equal[:], ALU.is_le, ALU.mult))
                after(dve.tensor_tensor(ok[:], ok[:], above[:], ALU.add))
                after(dve.tensor_tensor(wts[:], prob[:], ok[:], ALU.mult))
                after(dve.tensor_reduce(wsum[:], wts[:], AX, ALU.add))
                after(dve.tensor_scalar(wsum[:], wsum[:], 1e-20, None, ALU.add))
                after(dve.reciprocal(inv[:], wsum[:]))
                dve.tensor_tensor(comb[:, :, 0:E1], wts[:], wide(inv[:]), ALU.mult).then_inc(comb_done, 1)
                for j in range(2):
                    dve.wait_ge(comb_hi, j + 1)
                    cols = slice(j * 512, (j + 1) * 512)
                    dve.tensor_tensor(combT_lo[:, cols], turn_ps[j][0:NE1, :], combT_hi[:, cols], ALU.subtract).then_inc(comb_lo, 1)


class ExpertWeights1:

    def __init__(self, nc, ctx, src):
        def sb(name, shape, dt=F32):
            return [ctx.enter_context(nc.sbuf_tensor(f"{name}{i}", shape, dt)) for i in range(2)]

        self.src = src
        self.wu, self.wd = sb("wu", [P, WU1]), sb("wd", [P, D])
        self.wu_hi, self.wu_lo, self.wd_hi, self.wd_lo = (
            sb(n, shape, F32R) for n, shape in (("wu_hi", [P, WU1]), ("wu_lo", [P, WU1]), ("wd_hi", [P, D]), ("wd_lo", [P, D])))
        self.ready = [nc.alloc_semaphore(f"w1_ready{i}") for i in range(2)]
        self.up_hi, self.up_split, self.dn_split = (nc.alloc_semaphore("w1_" + n) for n in ("up_hi", "up_split", "dn_split"))

    def load(self, sp, c, b):
        wait_pos(sp, self.up_split, c - 1)
        sp.dma_start(self.wu[b][:], self.src["w_up1"][:, bass.ds(c, 1)].rearrange("p a i -> p (a i)")).then_inc(self.ready[b], 16)
        wait_pos(sp, self.dn_split, c - 1)
        sp.dma_start(self.wd[b][:], self.src["w_dn1"][:, bass.ds(c, 1)].rearrange("p a d -> p (a d)")).then_inc(self.ready[b], 16)

    def split_up(self, pool, c, b):
        pool.tensor_copy(self.wu_hi[b][:], self.wu[b][:]).then_inc(self.up_hi, 1)
        pool.wait_ge(self.up_hi, c + 1)
        pool.tensor_tensor(self.wu_lo[b][:], self.wu[b][:], self.wu_hi[b][:], ALU.subtract).then_inc(self.up_split, 1)


def experts1(nc, weights, h_hi, h_lo, combT_hi, combT_lo, gate, x_res, out):
    with ExitStack() as ctx:
        def sb(name, shape, dt=F32):
            return ctx.enter_context(nc.sbuf_tensor(name, shape, dt))

        def sem(n):
            return nc.alloc_semaphore("e1_" + n)

        UNITS, W = 4, T // 4
        wd, wu_hi, wu_lo, wd_hi, wd_lo = weights.wd, weights.wu_hi, weights.wu_lo, weights.wd_hi, weights.wd_lo
        w_ready, up_split, dn_split = weights.ready, weights.up_split, weights.dn_split
        sil, glu, act_w = ([sb(f"e1_{n}{i}", [P, W]) for i in range(2)] for n in ("sil", "glu", "act"))
        a_hi, a_lo = ([sb(f"a_{n}{i}", [P, T], F32R) for i in range(2)] for n in ("hi", "lo"))
        part = sb("e1_part", [P, NT // 2, 2, D])
        up_ps = [ctx.enter_context(nc.psum_tensor(f"up1_ps{i}", [P, 2, W], F32)) for i in range(2)]
        wt_ps = [ctx.enter_context(nc.psum_tensor(f"wt1_ps{i}", [P, 512], F32)) for i in range(2)]
        sum_ps = ctx.enter_context(nc.psum_tensor("e1_sum_ps", [P, NT // 2, 2, D], F32))
        dn_hi, up_ready, sil_done, glu_done, act_done, hi_done, lo_done, dn_done, gated, added = (
            sem(n) for n in ("dn_hi", "up_ready", "sil_done", "glu_done", "act_done", "hi_done", "lo_done", "dn_done",
                             "gated", "added"))
        pool_steps, stored, added_late = sem("pool_steps"), sem("stored"), sem("added_late")

        def steps(eng, step):
            step(0, 0)
            step(1, 1)
            with eng.Fori(1, NC1 // 2) as pair:
                for b in range(2):
                    step(2 * pair + b, b)
            step(NC1, 0)

        def real(c):
            return not isinstance(c, int) or 0 <= c < NC1

        with nc.Block() as block:

            @block.sync
            def _(sp):
                with sp.Fori(1, NC1 // 2) as pair:
                    for b in range(2):
                        weights.load(sp, 2 * pair + b, b)
                rows = out.rearrange("o (n p) d -> p (o n) d", p=P)
                for q in (0, 2, 1, 3):
                    sp.wait_ge(added if q < 2 else added_late, q % 2 + 1)
                    sp.dma_start(rows[:, 2 * q:2 * q + 2, :], x_res[:, 2 * q:2 * q + 2, :]).then_inc(stored, 16)
                sp.wait_ge(stored, 16 * NT // 2)

            @block.gpsimd
            def _(pool):
                def step(c, b):
                    if real(c) and not (isinstance(c, int) and c < 2):
                        pool.wait_ge(w_ready[b], 16 * c - 16 * b + 32)
                        wait_pos(pool, up_ready, UNITS * (c - 1))
                        pool.sem_inc(pool_steps, 1)
                        weights.split_up(pool, c, b)
                    if real(c - 1):
                        if not isinstance(c, int) or c > 2:
                            pool.wait_ge(dn_done, c - 2)
                            pool.sem_inc(pool_steps, 1)
                        pool.tensor_copy(wd_hi[1 - b][:], wd[1 - b][:]).then_inc(dn_hi, 1)
                        pool.wait_ge(dn_hi, c)
                        pool.tensor_tensor(wd_lo[1 - b][:], wd[1 - b][:], wd_hi[1 - b][:], ALU.subtract).then_inc(dn_split, 1)

                steps(pool, step)
                for q in range(2):
                    pool.wait_ge(gated, q + 1)
                    x = x_res[:, 2 * q:2 * q + 2, :]
                    pool.tensor_tensor(x, x, part[:, q], ALU.add).then_inc(added, 1)

            @block.tensor
            def _(pe):
                def step(c, b):
                    if real(c):
                        pe.wait_ge(up_split, c + 1)
                        for q in range(UNITS):
                            toks = slice(q * W, (q + 1) * W)
                            wait_pos(pe, act_done, UNITS * c + q - 1)
                            for g in range(2):
                                for k in range(KD):
                                    cols = slice((2 * k + g) * P, (2 * k + g + 1) * P)
                                    for n, (w, h) in enumerate(((wu_hi, h_hi), (wu_lo, h_hi), (wu_hi, h_lo))):
                                        pe.matmul(up_ps[q % 2][:, g, :], w[b][:, cols], h[:, k, toks],
                                                  start=(k == 0 and n == 0), stop=(k == KD - 1 and n == 2))
                            for n, w in enumerate((combT_hi, combT_lo)):
                                mm = pe.matmul(wt_ps[q % 2][:, 0:W], wu_hi[b][0:NE1, 4 * P:5 * P], w[:, toks], start=(n == 0), stop=(n == 1))
                            mm.then_inc(up_ready, 1)
                    if real(c - 1):
                        first, last = isinstance(c, int) and c == 1, isinstance(c, int) and c == NC1
                        pe.wait_ge(dn_split, c)
                        for t in range(NT):
                            if t % 2 == 0:
                                pe.wait_ge(lo_done, UNITS * (c - 1) + t // 2 + 1)
                            for n, (a, w) in enumerate(((a_hi, wd_hi), (a_hi, wd_lo), (a_lo, wd_hi))):
                                mm = pe.matmul(sum_ps[:, t // 2, t % 2, :], a[1 - b][:, t * P:(t + 1) * P], w[1 - b][:],
                                               start=(first and t % 2 == 0 and n == 0), stop=(last and n == 2), skip_group_check=True)
                        mm.then_inc(dn_done, 1)

                steps(pe, step)

            @block.scalar
            def _(act):
                def step(c, b):
                    if not real(c):
                        return
                    for q in range(UNITS + 1):
                        n = UNITS * c + q
                        if q < UNITS:
                            act.wait_ge(up_ready, n + 1)
                            wait_pos(act, glu_done, n - 1)
                            act.activation(sil[q % 2][:], up_ps[q % 2][:, 0, :], ACT.Silu).then_inc(sil_done, 1)
                        if q >= 1:
                            act.wait_ge(act_done, n)
                            wait_pos(act, dn_done, c - 1)
                            act.activation(a_hi[b][:, (q - 1) * W:q * W], act_w[(q - 1) % 2][:], ACT.Copy).then_inc(hi_done, 1)

                steps(act, step)

            @block.vector
            def _(dve):
                def step(c, b):
                    if not real(c):
                        return
                    for q in range(UNITS + 1):
                        n = UNITS * c + q
                        if q < UNITS:
                            dve.wait_ge(sil_done, n + 1)
                            wait_pos(dve, act_done, n - 1)
                            dve.tensor_tensor(glu[q % 2][:], sil[q % 2][:], up_ps[q % 2][:, 1, :], ALU.mult).then_inc(glu_done, 1)
                        if q >= 1:
                            cols = slice((q - 1) * W, q * W)
                            dve.wait_ge(hi_done, n)
                            dve.tensor_tensor(a_lo[b][:, cols], act_w[(q - 1) % 2][:], a_hi[b][:, cols], ALU.subtract).then_inc(lo_done, 1)
                        if q < UNITS:
                            dve.wait_ge(glu_done, n + 1)
                            wait_pos(dve, lo_done, n - 1)
                            dve.tensor_tensor(act_w[q % 2][:], glu[q % 2][:], wt_ps[q % 2][:, 0:W], ALU.mult).then_inc(act_done, 1)

                steps(dve, step)
                dve.wait_ge(dn_done, NC1)
                for q in range(NT // 2):
                    dve.tensor_tensor(part[:, q], sum_ps[:, q], gate.unsqueeze(1).to_broadcast([P, 2, D]), ALU.mult).then_inc(gated, 1)
                dve.wait_ge(gated, NT // 2)
                for q in range(2, NT // 2):
                    x = x_res[:, 2 * q:2 * q + 2, :]
                    dve.tensor_tensor(x, x, part[:, q], ALU.add).then_inc(added_late, 1)


def rest(nc, src, norm_sems, stats, mv, x_res, row, modv, s_col, ident, mask_b, eps_col, out, stop):
    with ExitStack() as ctx:
        def sb(name, shape, dt=F32):
            return ctx.enter_context(nc.sbuf_tensor(name, shape, dt))

        posT, xgT, wcol = sb("posT", [P, T], BF16), sb("xgT", [P, KD, SLOTS]), sb("wcol", [P, NSB])
        load = ExpertLoads0(nc, ctx, src, ident)
        with ExitStack() as inner:
            place, slot_c = (inner.enter_context(nc.sbuf_tensor(n, shape, F32)) for n, shape in
                             (("place", [P, NT, E0]), ("slot_c", [P, C0])))
            hw_hi = inner.enter_context(nc.sbuf_tensor("hw_hi", [P, NT, D + P], F32R))
            hw_lo = inner.enter_context(nc.sbuf_tensor("hw_lo", [P, NT, D + P], F32R))
            with ExitStack() as routing:
                h = routing.enter_context(nc.sbuf_tensor("h1", [P, NT, D], F32))
                hT = routing.enter_context(nc.sbuf_tensor("h1T", [P, KD, T], F32))
                rw = routing.enter_context(nc.sbuf_tensor("rw", [P, KD, E0], F32))
                ones_b, before_b = (routing.enter_context(nc.sbuf_tensor(n, [P, P], BF16)) for n in ("ones_b", "before_b"))
                wmod = routing.enter_context(nc.sbuf_tensor("wmod1", [P, KD, 6 * D], F32))
                loaded = nc.alloc_semaphore("r0_loaded")

                def loads(sp):
                    for dst, name in ((rw, "router_t"), (ones_b, "ones_b"), (before_b, "before_b"), (slot_c, "slot_c"), (wmod, "wmod1_p")):
                        sp.dma_start(dst[:], src[name]).then_inc(loaded, 16)
                    load.constants(sp)
                    for b in range(load.RING):
                        load(sp, b, b)

                norm_tiles(nc, "ln1", norm_sems, x_res, row(0, 4), row(0, 3), h, mv, eps_col, hT, ident, loads)
                route0(nc, loaded, rw, ones_b, before_b, wmod, s_col, modv[:, 1], h, hT, hw_hi, hw_lo, place, posT, ident)
            onehot = inner.enter_context(nc.sbuf_tensor("onehot", [P, NT, SLOTS], F32R))
            gather0(nc, src, load, hw_hi, hw_lo, place, slot_c, onehot, xgT, wcol, modv[:, 1])
        experts0(nc, load, norm_sems, stats, mv, xgT, wcol, posT, row(0, 5), x_res)
    if stop < 3:
        return
    with ExitStack() as ctx:
        def sb(name, shape, dt=F32):
            return ctx.enter_context(nc.sbuf_tensor(name, shape, dt))

        weights = ExpertWeights1(nc, ctx, src)
        layer1(nc, src, norm_sems, stats, mv, x_res, row, ident, mask_b, eps_col, weights)
        if stop < 4:
            return
        h_hi, h_lo = sb("h3_hi", [P, KD, T], F32R), sb("h3_lo", [P, KD, T], F32R)
        combT_hi, combT_lo = sb("combT_hi", [NE1, T], F32R), sb("combT_lo", [NE1, T], F32R)
        rw = sb("rw1", [P, KD, E1])
        with nc.sbuf_tensor("h3T", [P, KD, T], F32) as hT:
            rw_loaded = nc.alloc_semaphore("r1_loaded")
            norm_turned(nc, "ln4", norm_sems, x_res, row(1, 4), row(1, 3), hT, mv, ident, eps_col,
                        lambda sp: sp.dma_start(rw[:], src["gate_t"]).then_inc(rw_loaded, 16))
            route1(nc, rw_loaded, rw, hT, combT_hi, combT_lo, h_hi, h_lo, ident)
        experts1(nc, weights, h_hi, h_lo, combT_hi, combT_lo, row(1, 5), x_res, out)


def layer1(nc, src, norm_sems, stats, mv, x_res, row, ident, mask_b, eps_col, weights):
    with ExitStack() as ctx:
        def sb(name, shape, dt=F32):
            return ctx.enter_context(nc.sbuf_tensor(name, shape, dt))

        rows = sb("ln_rows", [P, 2, D])
        hm, hT, mv2 = sb("hm", [P, NT, D]), sb("h2T", [P, KD, T]), sb("mv2", [P, NT, 2])
        qT, kT, value, catT = sb("q1T", [3 * QK1, T], F32R), sb("k1T", [3 * QK1, T], F32R), sb("value", [P, NT, D]), sb("catT", [P, 4, T])
        bias = sb("bias", [P, T])
        w, pm = sb("expand", [P, KD, 6 * QK1 + 2 * EXP1]), sb("pm", [P, 1])
        rows_loaded, w_loaded, pos_loaded = (nc.alloc_semaphore("p1_" + n) for n in ("rows_loaded", "w_loaded", "pos_loaded"))

        def load_rows(sp):
            sp.dma_start(rows[:, 0, :], src["ln_gamma"].to_broadcast([P, D])).then_inc(rows_loaded, 16)
            sp.dma_start(rows[:, 1, :], src["ln_beta"].to_broadcast([P, D])).then_inc(rows_loaded, 16)
            sp.dma_start(w[:], src["expand_t"]).then_inc(w_loaded, 16)
            sp.dma_start(pm[:], src["pos_mult"].to_broadcast([P, 1])).then_inc(pos_loaded, 16)
            sp.dma_start(bias[:], src["rel"]).then_inc(pos_loaded, 16)
            sp.wait_ge(rows_loaded, 32)

        norm_tiles(nc, "ln2", norm_sems, x_res, row(1, 1), row(1, 0), hm, mv, eps_col, loads=load_rows, next_stats=(stats, mv2))
        norm_turned(nc, "ln3", norm_sems, hm, rows[:, 0, :], rows[:, 1, :], hT, mv2, ident, eps_col)
        project1(nc, w_loaded, pos_loaded, w, pm, hT, qT, kT, value, catT, bias, mask_b)
        attend1(nc, src, weights, norm_sems, stats, mv, qT, kT, value, catT, bias, hm, row(1, 2), x_res, ident)


def store(nc, x, out):
    with nc.semaphore("stored") as stored, nc.Block() as block:

        @block.sync
        def _(sp):
            sp.dma_start(out.rearrange("o (n p) d -> p (o n) d", p=P), x[:]).then_inc(stored, 16)
            sp.wait_ge(stored, 16)


def build(nc, src, out, stop=99):
    with ExitStack() as ctx:
        def sb(name, shape, dt=F32):
            return ctx.enter_context(nc.sbuf_tensor(name, shape, dt))

        x_res = sb("x_res", [P, NT, D])
        modv = sb("modv", [P, 2, 6 * D])
        ident, ident_b = sb("ident", [P, P]), sb("ident_b", [P, P], BF16)
        mask_b = sb("mask_b", [P, P], BF16)
        eps_col = sb("eps_col", [P, 1])
        s_col = sb("s_col", [P, 2, KD])
        stats, mv = sb("stats", [P, NT, 6]), sb("mv", [P, NT, 2])
        x_loaded = nc.alloc_semaphore("x_loaded")
        norm_sems = NormSems(nc)

        def row(l, j):
            return modv[:, l, j * D:(j + 1) * D]

        consts = [(ident[:], "ident"), (ident_b[:], "ident_b"), (mask_b[:], "mask_b"), (eps_col[:], "eps")]
        with ExitStack() as inner:
            outT = inner.enter_context(nc.sbuf_tensor("outT", [P, H, T], F32))
            wo = inner.enter_context(nc.sbuf_tensor("wo", [P, H, D], F32))
            late_loaded, rope_loaded = nc.alloc_semaphore("late_loaded"), nc.alloc_semaphore("rope_loaded")
            with ExitStack() as first:
                rope = first.enter_context(nc.sbuf_tensor("rope", [P, 2, NT, 2, DH // 2], F32))
                w_down = first.enter_context(nc.sbuf_tensor("w_down", [P, KD, P], F32))
                hT = first.enter_context(nc.sbuf_tensor("hT", [P, KD, T], F32))
                ckvT = first.enter_context(nc.sbuf_tensor("ckvT", [P, T], F32))
                ckv = first.enter_context(nc.sbuf_tensor("ckv", [P, NT, P], F32))
                wv_t = first.enter_context(nc.sbuf_tensor("wv_t", [P, H, P], F32))
                modulation(nc, src, consts + [(w_down[:], "w_down_p")],
                           [(wo[:], "wo_p", late_loaded), (wv_t[:], "wv_t", late_loaded), (rope[:], "rope", rope_loaded)],
                           modv, s_col, x_res, x_loaded, norm_sems, stats, mv)
                norm_turned(nc, "ln0", norm_sems, x_res, row(0, 1), row(0, 0), hT, mv, ident, eps_col)
                latent(nc, hT, ckvT, ckv, w_down, ident)
                attention0(nc, src, hT, ckvT, ckv, outT, wv_t, wo, late_loaded, rope, rope_loaded, ident, ident_b, mask_b)
            output0(nc, norm_sems, stats, mv, outT, wo, row(0, 2), x_res)
        if stop > 1:
            rest(nc, src, norm_sems, stats, mv, x_res, row, modv, s_col, ident, mask_b, eps_col, out, stop)
        if stop < 4:
            store(nc, x_res, out)


def laid_out(inputs):
    import numpy as np

    a = {k: np.ascontiguousarray(v) for k, v in inputs.items()}
    f32 = np.float32
    wq = a["L0_attn_wq"].reshape(D, H, DH // 2, 2).transpose(0, 1, 3, 2).reshape(D, H * DH)
    wup = a["L0_attn_w_up"].reshape(P, H, 2, DH)
    wk = wup[:, :, 0].reshape(P, H, DH // 2, 2).transpose(0, 1, 3, 2).reshape(P, H * DH)
    inv_freq = (1.0 / 10000.0 ** (np.arange(0, DH, 2, dtype=f32) / f32(DH))).astype(f32)
    ang = np.arange(T, dtype=f32)[:, None] * inv_freq[None, :]
    cos, sin = np.cos(ang).astype(f32), np.sin(ang).astype(f32)
    table = np.stack([cos, sin])
    table = np.stack([table * f32(DH ** -0.5), table], axis=2)
    table = table.reshape(2, NT, P, 2, DH // 2).transpose(2, 0, 1, 3, 4)
    upper = np.arange(P)[None, :] > np.arange(P)[:, None]
    bf = np.dtype("bfloat16")
    out = {
        "L0_attn_x": a["L0_attn_x"], "wq_split": wq, "w_k": wk, "wv_t": wup[:, :, 1].transpose(2, 1, 0),
        "wo_p": a["L0_attn_wo"].reshape(H, DH, D).transpose(1, 0, 2),
        "w_down_p": a["L0_attn_w_down"].reshape(KD, P, P).transpose(1, 0, 2),
        "L0_c": a["L0_c"], "L1_c": a["L1_c"], "L0_wmod": a["L0_wmod"], "wmod1_p": a["L1_wmod"].reshape(KD, P, 6 * D).transpose(1, 0, 2),
        "rope": table, "ident": np.eye(P, dtype=f32), "ident_b": np.eye(P).astype(bf),
        "mask_b": np.where(upper, -3e38, 0.0).astype(bf), "eps": np.full((P, 1), EPS, f32),
    }
    experts, slots = np.arange(P), np.arange(SLOTS)
    w1 = np.stack([a["L0_ffn_w1"], a["L0_ffn_v1"]]).reshape(2, E0, F0, KD, P)
    out |= {
        "router_t": a["L0_ffn_router_w"].reshape(E0, KD, P).transpose(2, 1, 0),
        "ones_b": np.ones((P, P)).astype(bf), "before_b": upper.astype(bf),
        "slot_c": np.tile(np.arange(C0, dtype=f32), (P, 1)),
        "own_b": (slots[None, :] // C0 == experts[:, None]).astype(bf),
        "sel_b": (slots[None, :] // C0 == experts[:, None]).astype(bf).reshape(P, NSB, P),
        "ones_f": np.ones((P, 1), f32), "c_col": (np.arange(P) % C0).astype(f32)[:, None],
        "w_up0": w1.transpose(4, 1, 3, 0, 2), "w_dn0": a["L0_ffn_w2"].transpose(1, 0, 2),
    }
    rel = np.arange(T, dtype=f32)[None, :] - np.arange(P, dtype=f32)[:, None] - f32(T - P)
    pad = NC1 * P - (E1 * I1 + SI1)
    ew = a["L1_ffn_expert_wg"].reshape(E1, 2, I1, D).transpose(1, 0, 2, 3).reshape(2, E1 * I1, D)
    wg = np.concatenate([ew, a["L1_ffn_shared_wg"].reshape(2, SI1, D), np.zeros((2, pad, D), f32)], axis=1)
    wd = np.concatenate([a["L1_ffn_expert_wd"].transpose(0, 2, 1).reshape(E1 * I1, D), a["L1_ffn_shared_wd"].T, np.zeros((pad, D), f32)])
    unit_expert = np.minimum(np.arange(NC1 * P) // I1, E1)
    pick = (unit_expert[None, :] == np.arange(P)[:, None]).astype(f32).reshape(P, NC1, P)
    up = wg.reshape(2, NC1, P, KD, P).transpose(4, 1, 3, 0, 2).reshape(P, NC1, 2 * KD * P)
    expand = a["L1_attn_expand"]
    expand = np.concatenate([expand[:QK1]] * 3 + [expand[QK1:2 * QK1]] * 3 + [expand[2 * QK1:]])
    out |= {
        "expand_t": expand.reshape(-1, KD, P).transpose(2, 1, 0), "rel": rel,
        "project_t": a["L1_attn_project"].reshape(D, 4, P).transpose(2, 1, 0),
        "pos_mult": a["L1_attn_pos_mult"].reshape(1, 1),
        "ln_gamma": a["L1_attn_ln_gamma"].reshape(1, D), "ln_beta": a["L1_attn_ln_beta"].reshape(1, D),
        "gate_t": a["L1_ffn_gate_w"].reshape(E1, KD, P).transpose(2, 1, 0),
        "w_up1": np.concatenate([up, pick], axis=2), "w_dn1": wd.reshape(NC1, P, D).transpose(1, 0, 2),
    }
    return {k: np.ascontiguousarray(v) for k, v in out.items()}


def kernel(**inputs):
    import concourse.bacc as _bacc
    from concourse import mybir as _mybir
    from concourse.bass_utils import run_bass_kernel_spmd as _run

    nc = _bacc.Bacc("TRN2", target_bir_lowering=False, num_devices=1)
    arrays = laid_out(inputs)
    src = {n: nc.dram_tensor(f"in_{n}", a.shape, _mybir.dt.from_np(a.dtype), kind="ExternalInput").ap() for n, a in arrays.items()}
    out = nc.dram_tensor("out", (1, T, D), F32, kind="ExternalOutput").ap()
    build(nc, src, out)
    r = _run(nc, [{f"in_{n}": a for n, a in arrays.items()}], core_ids=[0])
    return r.results[0]["out"]
```
